# Optimizing a Trainium2 kernel written in Bass

```python
import numpy as np
import jax
import jax.numpy as jnp

def _softmax(x, axis=-1):
    return jax.nn.softmax(x, axis=axis)

def _gelu(x):
    return jax.nn.gelu(x, approximate=True)

def _silu(x):
    return jax.nn.silu(x)

def _sigmoid(x):
    return jax.nn.sigmoid(x)

def _layernorm(x, axis=-1, eps=1e-05):
    m = jnp.mean(x, axis=axis, keepdims=True)
    v = jnp.var(x, axis=axis, keepdims=True)
    return (x - m) / jnp.sqrt(v + eps)

def _scatter_add(tgt, idx, src, axis=0):
    return tgt.at[idx].add(src)

def _segment_sum(src, seg, n):
    return jax.ops.segment_sum(src, seg, n)
kernel_name = 'mk_early_fusion_embed_d2_tok_img768_r4_dc90ab'

def setup_inputs(seed: int=0):
    np.random.seed(seed)
    _w = jnp.asarray

    def _rec_inputs():
        import jax
        import jax.numpy as jnp
        _rk = jax.random.key(seed)
        x = -0.000348323 + 0.999952 * jax.random.normal(jax.random.fold_in(_rk, 1), (8, 3, 128, 128), jnp.float32)
        x_txt = jax.random.randint(jax.random.fold_in(_rk, 51), (8, 77), 0, 31999, jnp.int32)
        mask_BS_i2_0 = jnp.where(jnp.ones((8, 77), dtype=bool), 2, 0).astype(jnp.int32)
        return (x, x_txt, mask_BS_i2_0)
    x, x_txt, mask_BS_i2_0 = _rec_inputs()

    def _L0_tok_setup():
        import jax, jax.numpy as jnp
        import numpy as np
        PATCH = 16

        def _shifted_concat(x):
            B, C, H, W = x.shape
            xp = jnp.pad(x, ((0, 0), (0, 0), (1, 1), (1, 1)))
            right = xp[:, :, 1:1 + H, 0:W]
            left = xp[:, :, 1:1 + H, 2:2 + W]
            down = xp[:, :, 0:H, 1:1 + W]
            up = xp[:, :, 2:2 + H, 1:1 + W]
            return jnp.concatenate([x, right, left, down, up], axis=1)

        def _patchify(x, p):
            B, C, H, W = x.shape
            h, w = (H // p, W // p)
            x = x.reshape(B, C, h, p, w, p)
            x = x.transpose(0, 2, 4, 3, 5, 1)
            return x.reshape(B, h * w, p * p * C)

        def _layernorm(x, gamma, beta, eps=1e-05):
            mu = jnp.mean(x, axis=-1, keepdims=True)
            var = jnp.var(x, axis=-1, keepdims=True)
            return (x - mu) * jax.lax.rsqrt(var + eps) * gamma + beta
        key = jax.random.key(seed)
        k1, k2 = jax.random.split(key)
        B, H, W = (32, 96, 96)
        patch_dim = PATCH * PATCH * 15
        d_hidn = 192
        x = jax.random.normal(k1, (B, 3, H, W), dtype=jnp.float32)
        gamma = jnp.ones((patch_dim,), dtype=jnp.float32)
        beta = jnp.zeros((patch_dim,), dtype=jnp.float32)
        W_ = jax.random.normal(k2, (patch_dim, d_hidn), dtype=jnp.float32) * patch_dim ** (-0.5)
        b = jnp.zeros((d_hidn,), dtype=jnp.float32)
        return {'x': x, 'gamma': gamma, 'beta': beta, 'W': W_, 'b': b}
    _L0_tok_all = _L0_tok_setup()
    _L0_tok_in = {k: v for k, v in _L0_tok_all.items() if k in ('gamma', 'beta', 'W', 'b')}
    del _L0_tok_all

    def _L0_txt_setup():
        import jax, jax.numpy as jnp
        import numpy as np
        VOCAB = 8000
        DIM = 192
        BATCH = 8
        SEQ = 512

        def _sinusoidal_pos(seq_len, dim):
            pos = jnp.arange(seq_len, dtype=jnp.float32)[:, None]
            ids = jnp.arange(dim, dtype=jnp.float32)[None, :]
            even_exp = jnp.floor(ids / 2.0) * 2.0 / dim
            angle = pos / jnp.power(10000.0, even_exp)
            return jnp.where(jnp.arange(dim) % 2 == 0, jnp.sin(angle), jnp.cos(angle))
        key = jax.random.key(seed)
        k1, k2, k3, k4 = jax.random.split(key, 4)
        input_tensor = jax.random.randint(k1, (BATCH, SEQ), 0, VOCAB)
        segment_label = jax.random.randint(k2, (BATCH, SEQ), 0, 3)
        token_table = jax.random.normal(k3, (VOCAB, DIM), dtype=jnp.float32) * 0.02
        segm_table = jax.random.normal(k4, (3, DIM), dtype=jnp.float32) * 0.02
        token_table = token_table.at[0].set(0.0)
        segm_table = segm_table.at[0].set(0.0)
        return {'input_tensor': input_tensor, 'segment_label': segment_label, 'token_table': token_table, 'segm_table': segm_table}
    _L0_txt_all = _L0_txt_setup()
    _L0_txt_in = {k: v for k, v in _L0_txt_all.items() if k in ('token_table', 'segm_table')}
    del _L0_txt_all

    def _L0_attn_setup():
        import jax, jax.numpy as jnp
        import numpy as np
        import math
        B, N, C = (8, 1024, 192)
        H = 12
        DH = C // H
        M = 64
        LN_EPS = 1e-05

        def _phi(t, random_features):
            norm_sq = 0.5 * jnp.sum(t * t, axis=-1, keepdims=True)
            proj = jnp.einsum('bhnd,md->bhnm', t, random_features)
            return jnp.exp(proj - norm_sq) * (1.0 / math.sqrt(M))
        key = jax.random.key(seed)
        ks = jax.random.split(key, 7)
        x = jax.random.normal(ks[0], (B, N, C), dtype=jnp.float32)
        W_qkv = jax.random.normal(ks[1], (C, 3 * C), dtype=jnp.float32) * (1.0 / math.sqrt(C))
        W_proj = jax.random.normal(ks[2], (C, C), dtype=jnp.float32) * (1.0 / math.sqrt(C))
        b_proj = jnp.zeros((C,), dtype=jnp.float32)
        gamma = jnp.ones((C,), dtype=jnp.float32)
        beta = jnp.zeros((C,), dtype=jnp.float32)
        random_features = jax.random.normal(ks[3], (M, DH), dtype=jnp.float32) / math.sqrt(DH)
        return {'x': x, 'W_qkv': W_qkv, 'W_proj': W_proj, 'b_proj': b_proj, 'gamma': gamma, 'beta': beta, 'random_features': random_features}
    _L0_attn_all = _L0_attn_setup()
    _L0_attn_in = {k: v for k, v in _L0_attn_all.items() if k in ('W_qkv', 'W_proj', 'b_proj', 'gamma', 'beta', 'random_features')}
    del _L0_attn_all

    def _L0_ffn_setup():
        import jax, jax.numpy as jnp
        import numpy as np
        DECAY = 0.9
        EPS = 0.01
        TOP_K = 2
        key = jax.random.key(seed)
        k1, k2, k3, k4 = jax.random.split(key, 4)
        B, S, H, I, E = (4, 512, 192, 512, 8)
        return {'hidden_states': jax.random.normal(k1, (B, S, H), jnp.float32), 'router_w': jax.random.normal(k2, (E, H), jnp.float32) * 0.02, 'w1': jax.random.normal(k3, (E, I, H), jnp.float32) * 0.02, 'w2': jax.random.normal(k4, (E, H, I), jnp.float32) * 0.02}
    _L0_ffn_all = _L0_ffn_setup()
    _L0_ffn_in = {k: v for k, v in _L0_ffn_all.items() if k in ('router_w', 'w1', 'w2')}
    del _L0_ffn_all

    def _L1_attn_setup():
        import jax, jax.numpy as jnp
        import numpy as np
        N_HEAD = 12
        N_EMBD = 192
        MASK_VALUE = -1000000000.0
        key = jax.random.key(seed)
        k1, k2, k3 = jax.random.split(key, 3)
        B, T, C = (4, 512, N_EMBD)
        x = jax.random.normal(k1, (B, T, C), dtype=jnp.float32)
        W_attn = jax.random.normal(k2, (C, 3 * C), dtype=jnp.float32) * 0.02
        W_proj = jax.random.normal(k3, (C, C), dtype=jnp.float32) * 0.02
        return {'x': x, 'W_attn': W_attn, 'W_proj': W_proj}
    _L1_attn_all = _L1_attn_setup()
    _L1_attn_in = {k: v for k, v in _L1_attn_all.items() if k in ('W_attn', 'W_proj')}
    del _L1_attn_all

    def _L1_ffn_setup():
        import jax, jax.numpy as jnp
        import numpy as np
        DIM = 192
        HID = 512
        E = 8
        TOP_K = 2

        def _ffn(t, a, b, c):
            return jax.nn.silu(t @ a.T) * (t @ c.T) @ b.T
        key = jax.random.key(seed)
        ks = jax.random.split(key, 9)
        s = 0.02
        return {'x': jax.random.normal(ks[0], (2, 256, DIM), dtype=jnp.float32), 'gate_w': jax.random.normal(ks[1], (E, DIM), dtype=jnp.float32) * s, 'w1': jax.random.normal(ks[2], (E, HID, DIM), dtype=jnp.float32) * s, 'w2': jax.random.normal(ks[3], (E, DIM, HID), dtype=jnp.float32) * s, 'w3': jax.random.normal(ks[4], (E, HID, DIM), dtype=jnp.float32) * s, 'ws1': jax.random.normal(ks[5], (HID, DIM), dtype=jnp.float32) * s, 'ws2': jax.random.normal(ks[6], (DIM, HID), dtype=jnp.float32) * s, 'ws3': jax.random.normal(ks[7], (HID, DIM), dtype=jnp.float32) * s}
    _L1_ffn_all = _L1_ffn_setup()
    _L1_ffn_in = {k: v for k, v in _L1_ffn_all.items() if k in ('gate_w', 'w1', 'w2', 'w3', 'ws1', 'ws2', 'ws3')}
    del _L1_ffn_all
    return {'x': x, 'x_txt': x_txt, 'mask_BS_i2_0': mask_BS_i2_0, 'L0_tok_gamma': _L0_tok_in['gamma'], 'L0_tok_beta': _L0_tok_in['beta'], 'L0_tok_W': _L0_tok_in['W'], 'L0_tok_b': _L0_tok_in['b'], 'L0_txt_token_table': _L0_txt_in['token_table'], 'L0_txt_segm_table': _L0_txt_in['segm_table'], 'L0_attn_W_qkv': _L0_attn_in['W_qkv'], 'L0_attn_W_proj': _L0_attn_in['W_proj'], 'L0_attn_b_proj': _L0_attn_in['b_proj'], 'L0_attn_gamma': _L0_attn_in['gamma'], 'L0_attn_beta': _L0_attn_in['beta'], 'L0_attn_random_features': _L0_attn_in['random_features'], 'L0_ffn_router_w': _L0_ffn_in['router_w'], 'L0_ffn_w1': _L0_ffn_in['w1'], 'L0_ffn_w2': _L0_ffn_in['w2'], 'L1_attn_W_attn': _L1_attn_in['W_attn'], 'L1_attn_W_proj': _L1_attn_in['W_proj'], 'L1_ffn_gate_w': _L1_ffn_in['gate_w'], 'L1_ffn_w1': _L1_ffn_in['w1'], 'L1_ffn_w2': _L1_ffn_in['w2'], 'L1_ffn_w3': _L1_ffn_in['w3'], 'L1_ffn_ws1': _L1_ffn_in['ws1'], 'L1_ffn_ws2': _L1_ffn_in['ws2'], 'L1_ffn_ws3': _L1_ffn_in['ws3']}

def reference(x, x_txt, mask_BS_i2_0, L0_tok_gamma, L0_tok_beta, L0_tok_W, L0_tok_b, L0_txt_token_table, L0_txt_segm_table, L0_attn_W_qkv, L0_attn_W_proj, L0_attn_b_proj, L0_attn_gamma, L0_attn_beta, L0_attn_random_features, L0_ffn_router_w, L0_ffn_w1, L0_ffn_w2, L1_attn_W_attn, L1_attn_W_proj, L1_ffn_gate_w, L1_ffn_w1, L1_ffn_w2, L1_ffn_w3, L1_ffn_ws1, L1_ffn_ws2, L1_ffn_ws3):
    import jax
    import jax.numpy as jnp

    def _L0_tok_ref(x, gamma, beta, W, b):
        import jax, jax.numpy as jnp
        import numpy as np
        PATCH = 16

        def _shifted_concat(x):
            B, C, H, W = x.shape
            xp = jnp.pad(x, ((0, 0), (0, 0), (1, 1), (1, 1)))
            right = xp[:, :, 1:1 + H, 0:W]
            left = xp[:, :, 1:1 + H, 2:2 + W]
            down = xp[:, :, 0:H, 1:1 + W]
            up = xp[:, :, 2:2 + H, 1:1 + W]
            return jnp.concatenate([x, right, left, down, up], axis=1)

        def _patchify(x, p):
            B, C, H, W = x.shape
            h, w = (H // p, W // p)
            x = x.reshape(B, C, h, p, w, p)
            x = x.transpose(0, 2, 4, 3, 5, 1)
            return x.reshape(B, h * w, p * p * C)

        def _layernorm(x, gamma, beta, eps=1e-05):
            mu = jnp.mean(x, axis=-1, keepdims=True)
            var = jnp.var(x, axis=-1, keepdims=True)
            return (x - mu) * jax.lax.rsqrt(var + eps) * gamma + beta
        xs = _shifted_concat(x)
        tokens = _patchify(xs, PATCH)
        normed = _layernorm(tokens, gamma, beta)
        return jnp.einsum('bnd,de->bne', normed, W) + b

    def _L0_txt_ref(input_tensor, segment_label, token_table, segm_table):
        import jax, jax.numpy as jnp
        import numpy as np
        VOCAB = 8000
        DIM = 192
        BATCH = 8
        SEQ = 512

        def _sinusoidal_pos(seq_len, dim):
            pos = jnp.arange(seq_len, dtype=jnp.float32)[:, None]
            ids = jnp.arange(dim, dtype=jnp.float32)[None, :]
            even_exp = jnp.floor(ids / 2.0) * 2.0 / dim
            angle = pos / jnp.power(10000.0, even_exp)
            return jnp.where(jnp.arange(dim) % 2 == 0, jnp.sin(angle), jnp.cos(angle))
        batch, seq = input_tensor.shape
        pos = _sinusoidal_pos(seq, token_table.shape[1])
        tokens_embed = token_table[input_tensor]
        segments_embed = segm_table[segment_label]
        return segments_embed + pos[None, :, :] + tokens_embed

    def _L0_attn_ref(x, W_qkv, W_proj, b_proj, gamma, beta, random_features):
        import jax, jax.numpy as jnp
        import numpy as np
        import math
        B, N, C = (8, 1024, 192)
        H = 12
        DH = C // H
        M = 64
        LN_EPS = 1e-05

        def _phi(t, random_features):
            norm_sq = 0.5 * jnp.sum(t * t, axis=-1, keepdims=True)
            proj = jnp.einsum('bhnd,md->bhnm', t, random_features)
            return jnp.exp(proj - norm_sq) * (1.0 / math.sqrt(M))
        b, n, c = x.shape
        qkv = (x @ W_qkv).reshape(b, n, 3, H, DH)
        qkv = jnp.transpose(qkv, (2, 0, 3, 1, 4))
        q, k, v = (qkv[0], qkv[1], qkv[2])
        q_p = _phi(q, random_features)
        k_p = _phi(k, random_features)
        kv = jnp.einsum('bhnm,bhnd->bhmd', k_p, v)
        out = jnp.einsum('bhnm,bhmd->bhnd', q_p, kv)
        k_sum = jnp.sum(k_p, axis=2)
        normalizer = jnp.einsum('bhnm,bhm->bhn', q_p, k_sum)[..., None]
        out = out / (normalizer + 1e-06)
        x_attn = jnp.transpose(out, (0, 2, 1, 3)).reshape(b, n, c)
        x_attn = x_attn @ W_proj + b_proj
        y = x + x_attn
        mu = jnp.mean(y, axis=-1, keepdims=True)
        var = jnp.mean(jnp.square(y - mu), axis=-1, keepdims=True)
        return (y - mu) * jax.lax.rsqrt(var + LN_EPS) * gamma + beta

    def _L0_ffn_ref(hidden_states, router_w, w1, w2):
        import jax, jax.numpy as jnp
        import numpy as np
        DECAY = 0.9
        EPS = 0.01
        TOP_K = 2
        B, S, H = hidden_states.shape
        E = router_w.shape[0]
        flat = hidden_states.reshape(B * S, H)
        logits = flat @ router_w.T
        probs = jax.nn.softmax(logits, axis=-1)
        topk_probs, topk_idx = jax.lax.top_k(probs, TOP_K)
        importance = jax.lax.stop_gradient(probs).sum(axis=0)
        running = jnp.ones((E,), dtype=flat.dtype)
        blended = running + (1.0 - DECAY) * (importance - running)
        running = blended + EPS
        balance = running[topk_idx]
        balanced = topk_probs / balance
        balanced = balanced / balanced.sum(axis=-1, keepdims=True)
        h = jnp.einsum('th,eih->tei', flat, w1)
        h = jax.nn.silu(h)
        outs = jnp.einsum('tei,ehi->teh', h, w2)
        sel = jnp.take_along_axis(outs, topk_idx[:, :, None], axis=1)
        combined = (sel * balanced[..., None]).sum(axis=1)
        return combined.reshape(B, S, H)

    def _L1_attn_ref(x, W_attn, W_proj):
        import jax, jax.numpy as jnp
        import numpy as np
        N_HEAD = 12
        N_EMBD = 192
        MASK_VALUE = -1000000000.0
        B, T, C = x.shape
        H = N_HEAD
        D = C // H
        qkv = x @ W_attn
        q, k, v = jnp.split(qkv, 3, axis=-1)
        q = q.reshape(B, T, H, D).transpose(0, 2, 1, 3)
        k = k.reshape(B, T, H, D).transpose(0, 2, 1, 3)
        v = v.reshape(B, T, H, D).transpose(0, 2, 1, 3)
        scale = jax.lax.rsqrt(jnp.asarray(D, dtype=x.dtype))
        att = jnp.einsum('bhqd,bhkd->bhqk', q, k) * scale
        causal = jnp.tril(jnp.ones((T, T), dtype=x.dtype))
        att = att * causal + (1.0 - causal) * jnp.asarray(MASK_VALUE, dtype=x.dtype)
        att = jax.nn.softmax(att, axis=-1)
        y = jnp.einsum('bhqk,bhkd->bhqd', att, v)
        y = y.transpose(0, 2, 1, 3).reshape(B, T, C)
        return y @ W_proj

    def _L1_ffn_ref(x, gate_w, w1, w2, w3, ws1, ws2, ws3):
        import jax, jax.numpy as jnp
        import numpy as np
        DIM = 192
        HID = 512
        E = 8
        TOP_K = 2

        def _ffn(t, a, b, c):
            return jax.nn.silu(t @ a.T) * (t @ c.T) @ b.T
        B, S, D = x.shape
        xf = x.reshape(-1, D)
        T = xf.shape[0]
        logits = xf @ gate_w.T
        scores = jax.nn.softmax(logits, axis=-1)
        topk_w, topk_idx = jax.lax.top_k(scores, TOP_K)
        topk_w = topk_w / (topk_w.sum(-1, keepdims=True) + 1e-20)
        cw = jnp.zeros((T, E), xf.dtype).at[jnp.arange(T)[:, None], topk_idx].add(topk_w)
        y = jnp.zeros_like(xf)
        for e in range(E):
            y = y + cw[:, e:e + 1] * _ffn(xf, w1[e], w2[e], w3[e])
        y = y + _ffn(xf, ws1, ws2, ws3)
        return y.reshape(B, S, D)
    h = _L0_tok_ref(x, L0_tok_gamma, L0_tok_beta, L0_tok_W, L0_tok_b)
    h = jnp.concatenate([h, _L0_txt_ref(x_txt, mask_BS_i2_0, L0_txt_token_table, L0_txt_segm_table)], axis=1)
    h = h + _L0_attn_ref(_layernorm(h, axis=-1), L0_attn_W_qkv, L0_attn_W_proj, L0_attn_b_proj, L0_attn_gamma, L0_attn_beta, L0_attn_random_features)
    h = h + _L0_ffn_ref(_layernorm(h, axis=-1), L0_ffn_router_w, L0_ffn_w1, L0_ffn_w2)
    h = h + _L1_attn_ref(_layernorm(h, axis=-1), L1_attn_W_attn, L1_attn_W_proj)
    h = h + _L1_ffn_ref(_layernorm(h, axis=-1), L1_ffn_gate_w, L1_ffn_w1, L1_ffn_w2, L1_ffn_w3, L1_ffn_ws1, L1_ffn_ws2, L1_ffn_ws3)
    return h

_drawn_inputs = setup_inputs


def setup_inputs(seed=0):
    import zlib

    import numpy as np

    out = dict(_drawn_inputs(seed))
    spreads = {'L0_tok_gamma': (1.0, 0.2),
     'L0_tok_beta': (0.0, 0.1),
     'L0_tok_b': (0.0, 0.1),
     'L0_attn_b_proj': (0.0, 0.1),
     'L0_attn_gamma': (1.0, 0.2),
     'L0_attn_beta': (0.0, 0.1)}
    factors = {'L0_attn_random_features': 3.256,
     'L1_attn_W_attn': 3.581,
     'L1_attn_W_proj': 3.669,
     'L1_ffn_gate_w': 8.0,
     'L1_ffn_w1': 8.0,
     'L1_ffn_w2': 8.0,
     'L1_ffn_w3': 8.0,
     'L1_ffn_ws1': 5.969,
     'L1_ffn_ws2': 6.06,
     'L1_ffn_ws3': 5.933}
    for name, (base, spread) in spreads.items():
        noise = np.random.default_rng([zlib.crc32(name.encode()), seed]).standard_normal(out[name].shape)
        drawn = base * np.exp(spread * noise) if base else spread * noise
        out[name] = jnp.asarray(drawn.astype(out[name].dtype))
    for name, factor in factors.items():
        out[name] = (out[name] * factor).astype(out[name].dtype)
    return out
```

```python
from contextlib import ExitStack

import numpy as np
import concourse.bass as bass
from concourse import mybir

ALU = mybir.AluOpType
ACT = mybir.ActivationFunctionType
F32 = mybir.dt.float32
BF16 = mybir.dt.bfloat16
I32 = mybir.dt.int32
AX = mybir.AxisListType.X

B, SIDE, PATCH, CH = 8, 128, 16, 3
NP_ = (SIDE // PATCH) ** 2
VOCAB, NSEG = 8000, 3
NS = 77
C = 192
HC = C // 2
NH, DH, M = 12, 16, 64
NE, HID = 8, 512
HT = HID // 128
HALO = PATCH + 2
KP = 2 * HALO * CH
NJ = HALO // 2
NG = 5
PDIM = PATCH * PATCH * CH * NG
IT = B * NP_ // 128
NT = IT + B
NTOK = B * (NP_ + NS)
ROWS = [128] * IT + [NS] * B
OFF = [128 * t for t in range(IT)] + [IT * 128 + NS * b for b in range(B)]
CHUNK = [(0, 512, (0, 1, 2, 3)), (512, 4 * NS, (4, 5, 6, 7)), (512 + 4 * NS, 4 * NS, (8, 9, 10, 11))]
TEXT_FIRST = [CHUNK[1], CHUNK[2], CHUNK[0]]
PAIR = 2 * (DH + 1)
EPS = 1e-5

TOK = dict(x=(0, NJ * 512), x2=(4608, NJ * 512), w=(9216, NG * NJ * C), weff=(17856, NJ * (C + 1)), seg=(19600, B * C))
A0 = dict(qaug=(0, 2 * NTOK), kaug=(2280, 2 * NTOK), att=(0, NT * C), attT=(2304, 2 * NTOK), qp=(4560, 6 * NTOK),
          kp=(11328, NT * NH * M), v=(20544, NT * NH * 17), kv=(22992, B * 6 * PAIR))
A1 = dict(qT=(0, 2 * NTOK), kE=(2256, 2 * NTOK), kO=(4512, 2 * NTOK), v=(6768, 16 * NH * 17), sx=(10032, 2 * 8 * NS),
          pT=(11724, 2 * 8 * NS), att=(13572, NT * C), attT=(15876, 2 * NTOK))
M0 = dict(h=(0, 2 * HT * 512))
M1 = dict(h=(0, 3 * HT * 512), sa=(6144, 2 * 512), ring=(18176, 3 * (4 * HID + HT * C)))
ARENA = 26624


def build(nc, d, out):
    with ExitStack() as ctx:
        def sb(name, shape, dt=F32):
            return ctx.enter_context(nc.sbuf_tensor(name, shape, dt))

        def sem(name):
            return ctx.enter_context(nc.semaphore(name))

        arena = sb("arena", [128, ARENA])

        def at(place):
            return arena[:, place[0]:place[0] + place[1]]

        PS = ctx.enter_context(nc.psum_tensor("PS", [128, 8, 512], F32))

        H = sb("H", [128, NT, C])
        xn = sb("xn", [128, NT, C])
        xnT = sb("xnT", [HC, 2, NTOK])
        bnst = sb("bnst", [128, NT, 6])
        mv = sb("mv", [128, NT, 2])
        rstd = sb("rstd", [128, 2, NT])
        mhalf = sb("mhalf", [128, NT])
        ident = sb("ident", [128, 128])
        identb = sb("identb", [128, 128], BF16)
        ones = sb("ones", [128, 128])
        pos = sb("pos", [NS, C])
        ids = sb("ids", [NS, 2 * B], I32)
        idx = sb("idx", [NS, 3, 2 * B], I32)
        gb = sb("gb", [KP, 2, NG, NJ])
        mult = sb("mult", [KP, NJ])
        tokb = sb("tokb", [1, C])
        brow = sb("brow", [1, C])
        sgbw = sb("sgbw", [128, 2 * C])
        tst = sb("tst", [128, 6, IT])
        wqkv = sb("wqkv", [HC, 2, 3 * C])
        bd = sb("bd", [HC + 6, 6 * M])
        nb6 = sb("nb6", [HC, 6])
        wproj0 = sb("wproj0", [HC, 2, C])
        rows3 = sb("rows3", [128, 3, C])
        sq = sb("sq", [HC, 2, 512])
        rec = sb("rec", [128, 2, NH])
        wat = sb("wat", [HC, 2, 3 * C])
        wproj1 = sb("wproj1", [HC, 2, C])
        kmask = sb("kmask", [HC, 2])
        cmaskf = sb("cmaskf", [128, 64 + 2 * NS])
        cmask = sb("cmask", [128, 64 + 2 * NS], BF16)
        rw = sb("rw", [HC, 2, 2, NE])
        rank = sb("rank", [128, NE])
        lg = sb("lg", [128, NT, NE])
        rt = sb("rt", [128, 6, NT, NE])
        rs = sb("rs", [128, 6, NT])
        run = sb("run", [128, 3, NE])
        cw = sb("cw", [128, (NE + 1) * NT])
        ring0 = sb("ring0", [128, 2, 2 * HID + HT * C])
        mx = sb("mx", [128, 2, 3, 4])

        ld_x, ld_tokc, ld_const, ld_ids, ld_a0, ld_moe, ld_a1 = (
            sem(n) for n in ("ld_x", "ld_tokc", "ld_const", "ld_ids", "ld_a0", "ld_moe", "ld_a1"))
        ld_w = [sem(f"ld_w{g}") for g in range(NG)]
        ld_r0 = [sem(f"ld_r0_{k}") for k in range(2)]
        ld_r1 = [sem(f"ld_r1_{k}") for k in range(3)]
        gathered, idx_set = sem("gathered"), sem("idx_set")
        stored = sem("stored")
        ones_set, lg_set, v_ones0, v_ones1, kv_zero = (sem(n) for n in ("ones_set", "lg_set", "v_ones0", "v_ones1", "kv_zero"))
        x2_done, fold0, folded, brow_ps, brow_sb, tok_ps, sg_sb, tok_h, text_h = (
            sem(n) for n in ("x2_done", "fold0", "folded", "brow_ps", "brow_sb", "tok_ps", "sg_sb", "tok_h", "text_h"))
        mult_set, var_in, rs_out, mhalf_set = (sem(n) for n in ("mult_set", "var_in", "rs_out", "mhalf_set"))
        xn_ready = [sem(f"xn_ready{k}") for k in range(4)]
        tp_ps, tp_out = sem("tp_ps"), sem("tp_out")
        qk_ps, qk_sq, qk_aug, nm_ps, nm_out = (sem(n) for n in ("qk_ps", "qk_sq", "qk_aug", "nm_ps", "nm_out"))
        v_ps, v_out, ph_ps, ph_out, kv_ps, kv_out = (sem(n) for n in ("v_ps", "v_out", "ph_ps", "ph_out", "kv_ps", "kv_out"))
        o0_ps, att0, y0_ps, y0_out, xnb, yn, hb, h1 = (
            sem(n) for n in ("o0_ps", "att0", "y0_ps", "y0_out", "xnb", "yn", "hb", "h1"))
        lg_ps = [sem(f"lg_ps{k}") for k in range(2)]
        rt_in = [sem(f"rt_in{k}") for k in range(2)]
        rt_exp = [sem(f"rt_exp{k}") for k in range(2)]
        masks_set = sem("masks_set")
        imp_in, imp_ps, imp_read = sem("imp_in"), sem("imp_ps"), sem("imp_read")
        m_h = [sem(f"m_h{k}") for k in range(2)]
        m_a = [sem(f"m_a{k}") for k in range(2)]
        m_g = sem("m_g")
        m_y = [sem(f"m_y{k}") for k in range(2)]
        m_acc = [sem(f"m_acc{k}") for k in range(2)]
        q1_ps, q1_act, q1_dve, v1_ps, v1_out = (sem(n) for n in ("q1_ps", "q1_act", "q1_dve", "v1_ps", "v1_out"))
        s_ps, s_sub, s_exp, t_ps, t_act, t_dve, o1_ps, att1, y1_ps, h3 = (
            sem(n) for n in ("s_ps", "s_sub", "s_exp", "t_ps", "t_act", "t_dve", "o1_ps", "att1", "y1_ps", "h3"))
        dve_step, pool_step = sem("dve_step"), sem("pool_step")

        xT = at(TOK["x"])[0:KP].rearrange("p (j n) -> p j n", j=NJ)
        x2 = at(TOK["x2"])[0:KP].rearrange("p (j n) -> p j n", j=NJ)
        wt = at(TOK["w"])[0:KP].rearrange("p (g j n) -> p g j n", g=NG, j=NJ)
        weff = at(TOK["weff"])[0:KP].rearrange("p (j n) -> p j n", j=NJ)
        seg = at(TOK["seg"])[0:NS].rearrange("p (b n) -> p b n", b=B)
        qkaug = [at(A0[n])[0:HC + 6].rearrange("p (h n) -> p h n", h=2) for n in ("qaug", "kaug")]
        att0b = at(A0["att"]).rearrange("p (t n) -> p t n", t=NT)
        attT0 = at(A0["attT"])[0:HC].rearrange("p (h n) -> p h n", h=2)
        qp = at(A0["qp"]).rearrange("p (r n) -> p r n", r=6)
        kp = at(A0["kp"]).rearrange("p (t n) -> p t n", t=NT)
        v0 = at(A0["v"]).rearrange("p (t h e) -> p t h e", t=NT, h=NH)
        kv = at(A0["kv"]).rearrange("p (b r e) -> p b r e", b=B, r=6)
        qT1 = at(A1["qT"])[0:HC].rearrange("p (h n) -> p h n", h=2)
        kT1 = [at(A1[n])[0:HC].rearrange("p (h n) -> p h n", h=2) for n in ("kE", "kO")]
        v1 = at(A1["v"]).rearrange("p (t h e) -> p t h e", t=16, h=NH)
        sx = at(A1["sx"]).rearrange("p (u n) -> p u n", u=2)
        pT = at(A1["pT"]).rearrange("p (u n) -> p u n", u=2)
        att1b = at(A1["att"]).rearrange("p (t n) -> p t n", t=NT)
        attT1 = at(A1["attT"])[0:HC].rearrange("p (h n) -> p h n", h=2)

        MOE = []
        for k in range(2):
            nslot = 2 + k
            hbuf = at((M0, M1)[k]["h"]).rearrange("p (s i n) -> p s i n", s=nslot, i=HT)
            ring = ring0 if k == 0 else at(M1["ring"]).rearrange("p (s n) -> p s n", s=3)
            nw = 1 + k
            w1 = [[ring[0:HC, s, q * 2 * HID:(q + 1) * 2 * HID].rearrange("p (c n) -> p c n", c=2) for q in range(nw)]
                  for s in range(nslot)]
            w2 = [ring[:, s, nw * 2 * HID:nw * 2 * HID + HT * C].rearrange("p (i n) -> p i n", i=HT) for s in range(nslot)]
            MOE.append(dict(k=k, slots=nslot, h=hbuf, ring=ring, w1=w1, w2=w2, nw=nw, gated=k == 1,
                            iters=(NE + k) // nslot, dw1=d[f"m{k}_w1"], dw2=d[f"m{k}_w2"], ld=(ld_r0, ld_r1)[k]))
        sa = at(M1["sa"]).rearrange("p (s n) -> p s n", s=2)

        UNITS = [(t, None, g) for t in range(IT) for g in range(3)] + [(None, b, g) for b in range(B) for g in range(3)]
        IMG_UNITS = 3 * IT
        AFTER_UNITS = len(UNITS)
        VJ1 = [(t, ROWS[t], [(OFF[t], ROWS[t])]) for t in range(NT)] + [
            (NT + t, 128, [(OFF[t] + 64, 64), (OFF[t], 64)]) for t in range(IT)]

        PHI = [("k", t) for _, _, ts in TEXT_FIRST for t in ts] + [("qt", r) for r in range(6)] + [("qi", r) for r in range(3)]
        QK = [(c, s, h) for c in TEXT_FIRST for s in range(2) for h in range(2)]
        TP_XN0, TP_ATT0, TP_XN1, TP_XN2, TP_ATT1, TP_XN3 = (NT * k for k in range(6))
        TILES_TF = [t for _, _, ts in TEXT_FIRST for t in ts]
        TILES = list(range(NT))

        block = ctx.enter_context(nc.Block())

        @block.sync
        def _(sp):
            def load_expert(m, e, s):
                for q in range(m["nw"]):
                    sp.dma_start(m["ring"][0:HC, s, q * 2 * HID:(q + 1) * 2 * HID],
                                 m["dw1"][bass.ds((e * m["nw"] + q) * HC, HC), :]).then_inc(m["ld"][s], 16)
                sp.dma_start(m["w2"][s].rearrange("p i n -> p (i n)"), m["dw2"][bass.ds(e * 128, 128), :]).then_inc(m["ld"][s], 16)

            def later_experts(m):
                with sp.Fori(1, m["iters"]) as i:
                    for s in range(m["slots"]):
                        e = i * m["slots"] + s
                        sp.wait_ge(m_y[m["k"]], (e - m["slots"] + 1) * NT)
                        load_expert(m, e, s)

            sp.dma_start(ids[:], d["ids"]).then_inc(ld_ids, 16)
            sp.dma_start(gb[:], d["gb"]).then_inc(ld_tokc, 16)
            sp.dma_start(mult[:], d["mult"]).then_inc(ld_tokc, 16)
            sp.dma_start(tokb[:], d["tokb"]).then_inc(ld_tokc, 16)
            sp.dma_start(wt[:, 0], d["wt"][:, 0]).then_inc(ld_w[0], 16)
            sp.dma_start(xT, d["xT"]).then_inc(ld_x, 16)
            for g in range(1, NG):
                sp.dma_start(wt[:, g], d["wt"][:, g]).then_inc(ld_w[g], 16)
            for buf, name in ((ident, "ident"), (pos, "pos")):
                sp.dma_start(buf[:], d[name]).then_inc(ld_const, 16)
            for buf, name in ((wqkv, "wqkv"), (bd, "bd"), (nb6, "nb6"), (wproj0, "wproj0"), (rows3, "rows3")):
                sp.dma_start(buf[:], d[name]).then_inc(ld_a0, 16)
            for buf, name in ((rw, "rw"), (rank, "rank")):
                sp.dma_start(buf[:], d[name]).then_inc(ld_moe, 16)
            for s in range(2):
                load_expert(MOE[0], s, s)
            for buf, name in ((wat, "wat"), (wproj1, "wproj1"), (kmask, "kmask"), (cmaskf, "cmask")):
                sp.dma_start(buf[:], d[name]).then_inc(ld_a1, 16)
            later_experts(MOE[0])
            sp.wait_ge(m_y[0], NT)
            for s in range(3):
                load_expert(MOE[1], s, s)
            later_experts(MOE[1])
            for t in TILES:
                sp.wait_ge(m_acc[1], NE * NT + t + 1)
                sp.dma_start(out[OFF[t]:OFF[t] + ROWS[t], :], H[0:ROWS[t], t, :]).then_inc(stored, 16)
            sp.wait_ge(stored, 16 * NT)

        @block.gpsimd
        def _(pool):
            steps = [0]

            def step(ins):
                steps[0] += 1
                ins.then_inc(pool_step, 1)
                pool.wait_ge(pool_step, steps[0])

            turns = [0]

            def rsqrt(rows, cols):
                turns[0] += 1
                pool.wait_ge(var_in, turns[0])
                pool.tensor_tensor(out=rstd[0:rows, 1, cols], in0=rstd[0:rows, 0, cols], in1=mhalf[0:rows, cols],
                                   op=ALU.pow).then_inc(rs_out, 1)

            def rsqrt_tiles(tiles):
                rsqrt(ROWS[tiles[0]], slice(tiles[0], tiles[0] + len(tiles)))

            pool.memset(ones[:], 1.0).then_inc(ones_set, 1)
            pool.memset(mhalf[:], -0.5).then_inc(mhalf_set, 1)
            pool.wait_ge(idx_set, 2)
            for b in range(B):
                pool.indirect_dma_start(out=H[0:NS, IT + b, :], out_offset=None, in_=d["table"],
                                        in_offset=bass.IndirectOffsetOnAxis(ap=idx[:, 2, b:b + 1], axis=0)).then_inc(gathered, 16)
                pool.indirect_dma_start(out=seg[:, b, :], out_offset=None, in_=d["segt"],
                                        in_offset=bass.IndirectOffsetOnAxis(ap=idx[:, 2, B + b:B + b + 1], axis=0)).then_inc(gathered, 16)
            pool.memset(lg[:], 0.0).then_inc(lg_set, 1)
            pool.wait_ge(ld_const, 32)
            pool.wait_ge(gathered, 32 * B)
            step(pool.tensor_tensor(out=seg, in0=seg, in1=pos[:].unsqueeze(1).broadcast_to([NS, B, C]), op=ALU.add))
            pool.tensor_tensor(out=H[0:NS, IT:NT, :], in0=H[0:NS, IT:NT, :], in1=seg, op=ALU.add).then_inc(text_h, 1)
            pool.wait_ge(mhalf_set, 1)
            rsqrt(128, slice(0, IT))
            for _, _, tiles in TEXT_FIRST:
                rsqrt_tiles(tiles)
            pool.wait_ge(tok_h, IT)
            pool.wait_ge(text_h, 1)
            pool.memset(v0[:, :, :, DH:DH + 1], 1.0).then_inc(v_ones0, 1)
            pool.memset(at(A0["kv"]), 0.0).then_inc(kv_zero, 1)
            pool.wait_ge(ld_a0, 80)
            for n, t in enumerate(TILES_TF):
                P = ROWS[t]
                pool.wait_ge(tp_ps, TP_XN0 + n + 1)
                pool.tensor_tensor(out=xn[0:P, t, :], in0=xn[0:P, t, :], in1=rows3[0:P, 0, :], op=ALU.add).then_inc(xnb, 1)
                pool.tensor_tensor(out=H[0:P, t, :], in0=H[0:P, t, :], in1=rows3[0:P, 2, :], op=ALU.add).then_inc(hb, 1)
            pool.wait_ge(hb, NT)
            for _, _, tiles in CHUNK:
                rsqrt_tiles(tiles)
                for t in tiles:
                    P = ROWS[t]
                    pool.wait_ge(yn, t + 1)
                    step(pool.tensor_tensor(out=xn[0:P, t, :], in0=xn[0:P, t, :], in1=rows3[0:P, 1, :], op=ALU.mult))
                    pool.tensor_tensor(out=H[0:P, t, :], in0=H[0:P, t, :], in1=xn[0:P, t, :], op=ALU.add).then_inc(h1, 1)
            for _, _, tiles in CHUNK:
                rsqrt_tiles(tiles)
            pool.wait_ge(m_y[0], 1)
            pool.memset(v1[:, :, :, DH:DH + 1], 1.0).then_inc(v_ones1, 1)
            pool.wait_ge(ld_a1, 64)
            pool.tensor_copy(identb[:], ident[:]).then_inc(masks_set, 1)
            pool.tensor_copy(cmask[:], cmaskf[:]).then_inc(masks_set, 1)
            for _, _, tiles in CHUNK * 2:
                rsqrt_tiles(tiles)

        @block.scalar
        def _(act):
            A = nc.scalar.activation

            def tp_evac(n, t, dst):
                act.wait_ge(tp_ps, n + 1)
                A(dst[:, :, OFF[t]:OFF[t] + ROWS[t]],
                  PS[0:HC, 6 + n % 2, 0:256].rearrange("p (h n) -> p h n", h=2)[:, :, 0:ROWS[t]], ACT.Copy).then_inc(tp_out, 1)

            act.wait_ge(ld_tokc, 48)
            A(weff[:, :, C:C + 1], mult[:].unsqueeze(2), ACT.Copy).then_inc(mult_set, 1)
            act.wait_ge(ld_w[0], 16)
            for j in range(NJ):
                A(weff[:, j, 0:C], wt[:, 0, j, :], ACT.Copy, scale=gb[:, 0, 0, j:j + 1]).then_inc(fold0, 1)
            act.wait_ge(ld_x, 16)
            A(x2, xT, ACT.Square).then_inc(x2_done, 1)
            act.wait_ge(tok_ps, 3)
            A(sgbw[:], PS[:, 4, 0:2 * C], ACT.Copy).then_inc(sg_sb, 1)

            for n, t in enumerate(TILES_TF):
                tp_evac(TP_XN0 + n, t, xnT)
            for n, ((off, N, _), s, h) in enumerate(QK):
                act.wait_ge(qk_aug, n + 1)
                if n >= 2:
                    act.wait_ge(nm_ps, n - 1)
                A(sq[:, n % 2, 0:N], qkaug[s][0:HC, h, off:off + N], ACT.Square).then_inc(qk_sq, 1)
            act.wait_ge(v_ones0, 1)
            for n, t in enumerate(TILES_TF):
                act.wait_ge(v_ps, n + 1)
                A(v0[0:ROWS[t], t, :, 0:DH], PS[0:ROWS[t], 4 + n % 2, 0:C].rearrange("p (h e) -> p h e", h=NH),
                  ACT.Copy).then_inc(v_out, 1)
            for n, (kind, r) in enumerate(PHI):
                act.wait_ge(ph_ps, n + 1)
                b0 = 2 * (n % 2)
                if kind == "k":
                    A(kp[0:ROWS[r], r, :].rearrange("p (u n) -> p u n", u=2), PS[0:ROWS[r], b0:b0 + 2, 0:384],
                      ACT.Exp).then_inc(ph_out, 1)
                elif kind == "qt":
                    A(qp[:, r, 512:NTOK].rearrange("p (u n) -> p u n", u=2), PS[:, b0:b0 + 2, 0:4 * NS],
                      ACT.Exp).then_inc(ph_out, 1)
                else:
                    A(qp[:, 2 * r:2 * r + 2, 0:512], PS[:, b0:b0 + 2, :], ACT.Exp).then_inc(ph_out, 1)
            for n, t in enumerate(TILES):
                tp_evac(TP_ATT0 + n, t, attT0)

            def moe(m):
                k, S0 = m["k"], 3 * m["slots"]
                act.wait_ge(rt_in[k], 1)
                A(rt[:, 0], rt[:, 0], ACT.Exp).then_inc(rt_exp[k], 1)

                def body(i, first):
                    for s in range(S0):
                        N = CHUNK[s % 3][1]
                        S = i * S0 + s
                        if not m["gated"] and (not first or s >= m["slots"]):
                            act.wait_ge(m_y[k], 4 * (S - m["slots"]) + 4)
                        for it in range(HT):
                            act.wait_ge(m_h[k], 4 * S + it + 1)
                            if m["gated"]:
                                if not first or 4 * s + it >= 2:
                                    act.wait_ge(m_g, 4 * S + it - 1)
                                A(sa[:, it % 2, 0:N], PS[:, 2 * (it % 2), 0:N], ACT.Silu).then_inc(m_a[k], 1)
                            else:
                                A(m["h"][:, s % m["slots"], it, 0:N], PS[:, it, 0:N], ACT.Silu).then_inc(m_a[k], 1)

                body(0, True)
                with act.Fori(1, m["iters"]) as i:
                    body(i, False)

            for t in TILES:
                tp_evac(TP_XN1 + t, t, xnT)
            moe(MOE[0])
            for t in TILES:
                tp_evac(TP_XN2 + t, t, xnT)
            act.wait_ge(ld_a1, 64)
            for c, (off, N, _) in enumerate(CHUNK):
                for h in range(2):
                    act.wait_ge(q1_ps, 4 * c + h + 1)
                    A(qT1[:, h, off:off + N], PS[0:HC, h, 0:N], ACT.Copy).then_inc(q1_act, 1)
            act.wait_ge(v_ones1, 1)
            for n, (slot, P, _) in enumerate(VJ1):
                act.wait_ge(v1_ps, n + 1)
                A(v1[0:P, slot, :, 0:DH], PS[0:P, 4 + n % 2, 0:C].rearrange("p (h e) -> p h e", h=NH), ACT.Copy).then_inc(v1_out, 1)

            def probs(u):
                P, w = (128, 256) if u < IMG_UNITS else (NS, 8 * NS)
                act.wait_ge(s_sub, u + 1)
                A(sx[0:P, u % 2, 0:w], sx[0:P, u % 2, 0:w], ACT.Exp).then_inc(s_exp, 1)

            def turned(u):
                P, w = (128, 128) if u < IMG_UNITS else (64, 4 * NS)
                act.wait_ge(t_ps, u + 1)
                if u >= 2:
                    act.wait_ge(o1_ps, u - 1)
                A(pT[0:P, u % 2, 0:w], PS[0:P, 4, 0:w], ACT.Copy).then_inc(t_act, 1)

            for u in range(AFTER_UNITS + 1):
                if u < AFTER_UNITS:
                    probs(u)
                if u >= 1:
                    turned(u - 1)
            for t in TILES:
                tp_evac(TP_ATT1 + t, t, attT1)
            for t in TILES:
                tp_evac(TP_XN3 + t, t, xnT)
            moe(MOE[1])

        @block.vector
        def _(dve):
            V = nc.vector
            steps, norms = [0], [1]

            def step(ins):
                steps[0] += 1
                ins.then_inc(dve_step, 1)
                dve.wait_ge(dve_step, steps[0])

            def layernorm(tiles, src, ready, done):
                P, t0, n = ROWS[tiles[0]], tiles[0], len(tiles)
                for i, t in enumerate(tiles):
                    ready(t)
                    last = V.bn_stats(bnst[0:P, t, :], src[0:P, t, :])
                    if i < n - 1:
                        last.then_inc(dve_step, 1)
                        steps[0] += 1
                step(last)
                for i, t in enumerate(tiles):
                    last = V.bn_aggr(mv[0:P, t, :], bnst[0:P, t, :])
                    if i < n - 1:
                        last.then_inc(dve_step, 1)
                        steps[0] += 1
                step(last)
                V.tensor_scalar(rstd[0:P, 0, t0:t0 + n], mv[0:P, t0:t0 + n, 1], EPS, None, ALU.add).then_inc(var_in, 1)
                norms[0] += 1
                dve.wait_ge(rs_out, norms[0])
                for t in tiles:
                    V.tensor_scalar(xn[0:P, t, :], src[0:P, t, :], mv[0:P, t, 0:1], rstd[0:P, 1, t:t + 1],
                                    ALU.subtract, ALU.mult).then_inc(done, 1)

            dve.wait_ge(ld_ids, 16)
            for k, size in enumerate((VOCAB, NSEG)):
                own = slice(B * k, B * k + B)
                step(V.tensor_scalar(idx[:, 0, own], ids[:, own], 0.0, float(size), ALU.is_lt, ALU.mult))
                step(V.tensor_tensor(out=idx[:, 1, own], in0=idx[:, 0, own], in1=ids[:, own], op=ALU.add))
                V.tensor_scalar(idx[:, 2, own], idx[:, 1, own], 0.0, float(size - 1), ALU.max, ALU.min).then_inc(idx_set, 1)
            dve.wait_ge(ld_tokc, 48)
            for g in range(1, NG):
                dve.wait_ge(ld_w[g], 16)
                for j in range(NJ):
                    if g == 1:
                        dve.wait_ge(fold0, j + 1)
                    else:
                        dve.wait_ge(folded, NJ * (g - 2) + j + 1)
                    V.scalar_tensor_tensor(out=weff[:, j, 0:C], in0=wt[:, g, j, :], scalar=gb[:, 0, g, j:j + 1],
                                           in1=weff[:, j, 0:C], op0=ALU.mult, op1=ALU.add).then_inc(folded, 1)
            dve.wait_ge(brow_ps, 1)
            V.tensor_tensor(out=brow[:], in0=PS[0:1, 5, 0:C], in1=tokb[:], op=ALU.add).then_inc(brow_sb, 1)
            dve.wait_ge(tok_ps, 2)
            step(V.tensor_scalar(tst[:, 0, :], PS[:, 0:IT, C], 1.0 / PDIM, None, ALU.mult))
            step(V.tensor_tensor(out=tst[:, 1, :], in0=tst[:, 0, :], in1=tst[:, 0, :], op=ALU.mult))
            step(V.scalar_tensor_tensor(out=tst[:, 2, :], in0=PS[:, 5, C:C + IT], scalar=1.0 / PDIM, in1=tst[:, 1, :],
                                        op0=ALU.mult, op1=ALU.subtract))
            V.tensor_scalar(rstd[:, 0, 0:IT], tst[:, 2, :], EPS, None, ALU.add).then_inc(var_in, 1)
            dve.wait_ge(rs_out, 1)
            step(V.scalar_tensor_tensor(out=tst[:, 4, :], in0=tst[:, 0, :], scalar=-1.0, in1=rstd[:, 1, 0:IT],
                                        op0=ALU.mult, op1=ALU.mult))
            dve.wait_ge(sg_sb, 1)
            for t in range(IT):
                step(V.scalar_tensor_tensor(out=H[:, t, :], in0=PS[:, t, 0:C], scalar=rstd[:, 1, t:t + 1],
                                            in1=sgbw[:, C:2 * C], op0=ALU.mult, op1=ALU.add))
                V.scalar_tensor_tensor(out=H[:, t, :], in0=sgbw[:, 0:C], scalar=tst[:, 4, t:t + 1],
                                       in1=H[:, t, :], op0=ALU.mult, op1=ALU.add).then_inc(tok_h, 1)

            def in_stream(t):
                if t < IT:
                    dve.wait_ge(tok_h, t + 1)
                else:
                    dve.wait_ge(text_h, 1)
            for _, _, tiles in TEXT_FIRST:
                layernorm(tiles, H, in_stream, xn_ready[0])

            def norm_rows(n):
                (off, N, _), s, h = QK[n]
                dve.wait_ge(nm_ps, n + 1)
                V.tensor_copy(qkaug[s][HC:HC + 6, h, off:off + N], PS[HC:HC + 6, 2 + n % 2, 0:N]).then_inc(nm_out, 1)
            for n, ((off, N, _), s, h) in enumerate(QK):
                dve.wait_ge(qk_ps, n + 1)
                V.tensor_copy(qkaug[s][0:HC, h, off:off + N], PS[0:HC, n % 2, 0:N]).then_inc(qk_aug, 1)
                if n >= 1:
                    norm_rows(n - 1)
            norm_rows(len(QK) - 1)

            dve.wait_ge(kv_zero, 1)
            for b in range(B):
                dve.wait_ge(kv_ps, b + 1)
                src = PS[:, 4 + b % 2, 0:6 * PAIR].rearrange("p (r e) -> p r e", r=6)
                V.tensor_copy(kv[0:64, b, :, 0:17], src[0:64, :, 0:17]).then_inc(kv_out, 1)
                V.tensor_copy(kv[64:128, b, :, 17:34], src[64:128, :, 17:34]).then_inc(kv_out, 1)

            for n, t in enumerate(TILES):
                P = ROWS[t]
                dve.wait_ge(o0_ps, n + 1)
                o = PS[0:P, n % 2, 0:NH * 17].rearrange("p (h e) -> p h e", h=NH)
                step(V.tensor_scalar(rec[0:P, 0, :], o[:, :, DH], float(M) * 1e-6, None, ALU.add))
                step(V.reciprocal(rec[0:P, 1, :], rec[0:P, 0, :]))
                V.tensor_tensor(out=att0b[0:P, t, :].rearrange("p (h e) -> p h e", h=NH), in0=o[:, :, 0:DH],
                                in1=rec[0:P, 1, :].unsqueeze(2).broadcast_to([P, NH, DH]), op=ALU.mult).then_inc(att0, 1)
            dve.wait_ge(xnb, NT)
            for n, t in enumerate(TILES):
                P = ROWS[t]
                dve.wait_ge(y0_ps, n + 1)
                V.tensor_tensor(out=xn[0:P, t, :], in0=PS[0:P, 2 + n % 2, 0:C], in1=xn[0:P, t, :], op=ALU.add).then_inc(y0_out, 1)
            for _, _, tiles in CHUNK:
                layernorm(tiles, xn, lambda t: dve.wait_ge(y0_out, t + 1), yn)

            def bc(ap):
                return ap.unsqueeze(2).broadcast_to([128, NT, NE])

            def route(k):
                dve.wait_ge(lg_ps[k], 1)
                dve.wait_ge(lg_set, 1)
                dve.wait_ge(ld_moe, 32)
                step(V.tensor_copy(lg[:, 0:IT, :], PS[:, 5, 0:IT * NE].rearrange("p (t e) -> p t e", t=IT)))
                step(V.tensor_copy(lg[0:NS, IT:NT, :], PS[0:NS, 5, IT * NE:NT * NE].rearrange("p (t e) -> p t e", t=B)))
                step(V.tensor_reduce(out=rs[:, 0, :], in_=lg[:], axis=AX, op=ALU.max))
                V.tensor_tensor(out=rt[:, 0], in0=lg[:], in1=bc(rs[:, 0, :]), op=ALU.subtract).then_inc(rt_in[k], 1)
                dve.wait_ge(rt_exp[k], 1)
                step(V.tensor_reduce(out=rs[:, 1, :], in_=rt[:, 0], axis=AX, op=ALU.add))
                step(V.reciprocal(rs[:, 2, :], rs[:, 1, :]))
                if k == 0:
                    V.tensor_tensor(out=rt[:, 1], in0=rt[:, 0], in1=bc(rs[:, 2, :]), op=ALU.mult).then_inc(imp_in, 1)
                    dve.wait_ge(imp_in, 1)
                else:
                    step(V.tensor_tensor(out=rt[:, 1], in0=rt[:, 0], in1=bc(rs[:, 2, :]), op=ALU.mult))
                rk = rank[:].unsqueeze(1).broadcast_to([128, NT, NE])
                for pick, src in ((2, 1), (3, 0)):
                    step(V.tensor_reduce(out=rs[:, 3, :], in_=rt[:, src], axis=AX, op=ALU.max))
                    step(V.tensor_tensor(out=rt[:, 4], in0=rt[:, src], in1=bc(rs[:, 3, :]), op=ALU.is_equal))
                    step(V.tensor_tensor(out=rt[:, 5], in0=rt[:, 4], in1=rk, op=ALU.mult))
                    step(V.tensor_reduce(out=rs[:, 4, :], in_=rt[:, 5], axis=AX, op=ALU.max))
                    step(V.tensor_tensor(out=rt[:, pick], in0=rk, in1=bc(rs[:, 4, :]), op=ALU.is_equal))
                    if pick == 2:
                        step(V.scalar_tensor_tensor(out=rt[:, 0], in0=rt[:, 2], scalar=-2.0, in1=rt[:, 1],
                                                    op0=ALU.mult, op1=ALU.add))
                step(V.tensor_tensor(out=rt[:, 4], in0=rt[:, 2], in1=rt[:, 3], op=ALU.add))
                step(V.tensor_tensor(out=rt[:, 5], in0=rt[:, 4], in1=rt[:, 1], op=ALU.mult))
                if k == 0:
                    dve.wait_ge(imp_ps, 1)
                    V.tensor_reduce(out=run[:, 0, :], in_=PS[:, 5, 0:NT * NE].rearrange("p (t e) -> p e t", t=NT),
                                    axis=AX, op=ALU.add).then_inc(imp_read, 1)
                    dve.wait_ge(imp_read, 1)
                    step(V.tensor_scalar(run[:, 1, :], run[:, 0, :], 1.0, 0.1, ALU.subtract, ALU.mult))
                    step(V.tensor_scalar(run[:, 2, :], run[:, 1, :], 1.0, 0.01, ALU.add, ALU.add))
                    step(V.reciprocal(run[:, 0, :], run[:, 2, :]))
                    step(V.tensor_tensor(out=rt[:, 5], in0=rt[:, 5], in1=run[:, 0, :].unsqueeze(1).broadcast_to([128, NT, NE]),
                                         op=ALU.mult))
                step(V.tensor_reduce(out=rs[:, 3, :], in_=rt[:, 5], axis=AX, op=ALU.add))
                if k == 1:
                    step(V.tensor_scalar(rs[:, 3, :], rs[:, 3, :], 1e-20, None, ALU.add))
                    step(V.memset(cw[:, NE * NT:(NE + 1) * NT], 1.0))
                step(V.reciprocal(rs[:, 4, :], rs[:, 3, :]))
                step(V.tensor_tensor(out=cw[:, 0:NE * NT].rearrange("p (e t) -> p t e", e=NE), in0=rt[:, 5],
                                     in1=bc(rs[:, 4, :]), op=ALU.mult))

            def moe(m):
                k, S0 = m["k"], 3 * m["slots"]
                route(k)

                def gate(i, s, first):
                    if not m["gated"]:
                        return
                    S, N = i * S0 + s, CHUNK[s % 3][1]
                    if not first or s >= m["slots"]:
                        dve.wait_ge(m_y[k], 4 * (S - m["slots"]) + 4)
                    for it in range(HT):
                        dve.wait_ge(m_a[k], 4 * S + it + 1)
                        V.tensor_tensor(out=m["h"][:, s % m["slots"], it, 0:N], in0=sa[:, it % 2, 0:N],
                                        in1=PS[:, 2 * (it % 2) + 1, 0:N], op=ALU.mult).then_inc(m_g, 1)

                def accumulate(i, s, first):
                    S = i * S0 + s
                    for n, t in enumerate(CHUNK[s % 3][2]):
                        P = ROWS[t]
                        dve.wait_ge(m_y[k], 4 * S + n + 1)
                        if not first or s >= 3:
                            dve.wait_ge(m_acc[k], 4 * S + n + 1 - NT)
                        w = cw[0:P, bass.ds((i * m["slots"] + s // 3) * NT + t, 1)]
                        V.scalar_tensor_tensor(out=H[0:P, t, :], in0=PS[0:P, 4 + n % 2, 0:C], scalar=w, in1=H[0:P, t, :],
                                               op0=ALU.mult, op1=ALU.add).then_inc(m_acc[k], 1)

                def body(i, first):
                    gate(i, 0, first)
                    for s in range(S0):
                        if s + 1 < S0:
                            gate(i, s + 1, first)
                        accumulate(i, s, first)

                body(0, True)
                with dve.Fori(1, m["iters"]) as i:
                    body(i, False)

            for _, _, tiles in CHUNK:
                layernorm(tiles, H, lambda t: dve.wait_ge(h1, t + 1), xn_ready[1])
            moe(MOE[0])

            for _, _, tiles in CHUNK:
                layernorm(tiles, H, lambda t: dve.wait_ge(m_acc[0], (NE - 1) * NT + t + 1), xn_ready[2])
            dve.wait_ge(ld_a1, 64)
            for c, (off, N, _) in enumerate(CHUNK):
                for h in range(2):
                    dve.wait_ge(q1_ps, 4 * c + 2 + h + 1)
                    for odd in range(2):
                        V.tensor_scalar(kT1[odd][:, h, off:off + N], PS[0:HC, 2 + h, 0:N], kmask[:, odd:odd + 1], None,
                                        ALU.mult).then_inc(q1_dve, 1)

            def scores_out(u):
                P, w = (128, 64) if u < IMG_UNITS else (NS, NS)
                banks = 1 if u < IMG_UNITS else 2
                dve.wait_ge(s_ps, u + 1)
                b0 = 2 * (u % 2)
                src = PS[0:P, b0:b0 + banks, 0:4 * w].rearrange("p a (h e) -> p a h e", h=4)
                if u >= 2:
                    dve.wait_ge(s_sub, u - 1)
                m = mx[0:P, u % 2]
                step(V.tensor_reduce(out=m[:, 0:banks, :], in_=src, axis=AX, op=ALU.max))
                if banks == 2:
                    step(V.tensor_tensor(out=m[:, 2, :], in0=m[:, 0, :], in1=m[:, 1, :], op=ALU.max))
                top = m[:, 2 * (banks - 1), :].unsqueeze(1).unsqueeze(3).broadcast_to([P, banks, 4, w])
                if u >= 2:
                    dve.wait_ge(t_ps, u - 1)
                V.tensor_tensor(out=sx[0:P, u % 2, 0:banks * 4 * w].rearrange("p (a h e) -> p a h e", a=banks, h=4), in0=src,
                                in1=top, op=ALU.subtract).then_inc(s_sub, 1)

            def turned(u):
                P, w = (128, 128) if u < IMG_UNITS else (NS, 4 * NS)
                dve.wait_ge(t_ps, u + 1)
                if u >= 2:
                    dve.wait_ge(o1_ps, u - 1)
                V.tensor_copy(pT[0:P, u % 2, 4 * NS:4 * NS + w], PS[0:P, 5, 0:w]).then_inc(t_dve, 1)

            def divide(u):
                t, b, g = UNITS[u]
                dve.wait_ge(o1_ps, u + 1)
                if t is not None:
                    P, tile, o = 128, t, PS[:, 6:8, 0:34].rearrange("p z (y e) -> p y z e", y=2)
                else:
                    P, tile, o = NS, IT + b, PS[0:NS, 6 + u % 2, 0:68].rearrange("p (y z e) -> p y z e", y=2, z=2)
                r = rec[0:P, u % 2, 0:4].rearrange("p (y z) -> p y z", y=2)
                if u >= 2:
                    dve.wait_ge(att1, u - 1)
                step(V.reciprocal(r, o[:, :, :, DH]))
                dst = att1b[0:P, tile, :].rearrange("p (y g z e) -> p y g z e", y=2, g=3, z=2)[:, :, g]
                V.tensor_tensor(out=dst, in0=o[:, :, :, 0:DH], in1=r.unsqueeze(3).broadcast_to([P, 2, 2, DH]),
                                op=ALU.mult).then_inc(att1, 1)

            for u in range(AFTER_UNITS + 2):
                if u < AFTER_UNITS:
                    scores_out(u)
                if 1 <= u <= AFTER_UNITS:
                    turned(u - 1)
                if u >= 2:
                    divide(u - 2)
            for n, t in enumerate(TILES):
                P = ROWS[t]
                dve.wait_ge(y1_ps, n + 1)
                V.tensor_tensor(out=H[0:P, t, :], in0=PS[0:P, n % 2, 0:C], in1=H[0:P, t, :], op=ALU.add).then_inc(h3, 1)
            for _, _, tiles in CHUNK:
                layernorm(tiles, H, lambda t: dve.wait_ge(h3, t + 1), xn_ready[3])
            moe(MOE[1])

        @block.tensor
        def _(pe):
            mm = nc.tensor.matmul

            def turn(n, t, src):
                if n >= 2:
                    pe.wait_ge(tp_out, n - 1)
                P = ROWS[t]
                for h in range(2):
                    last = nc.tensor.transpose(PS[0:HC, 6 + n % 2, 128 * h:128 * h + P], src[0:P, t, h * HC:(h + 1) * HC],
                                               ident[0:P, 0:P])
                last.then_inc(tp_ps, 1)

            pe.wait_ge(ld_tokc, 48)
            for g in range(NG):
                pe.wait_ge(ld_w[g], 16)
                for j in range(NJ):
                    last = mm(PS[0:1, 5, 0:C], gb[:, 1, g, j:j + 1], wt[:, g, j, :], start=(g + j == 0), stop=(g == NG - 1 and j == NJ - 1))
            last.then_inc(brow_ps, 1)
            pe.wait_ge(x2_done, 1)
            pe.wait_ge(brow_sb, 1)
            for t in range(IT):
                for j in range(NJ):
                    last = mm(PS[:, 5, C + t:C + t + 1], x2[:, j, 128 * t:128 * t + 128], mult[:, j:j + 1],
                              start=(j == 0), stop=(j == NJ - 1))
            last.then_inc(tok_ps, 1)
            pe.wait_ge(ld_x, 16)
            pe.wait_ge(mult_set, 1)
            for j in range(NJ):
                pe.wait_ge(folded, NJ * (NG - 2) + j + 1)
                for t in range(IT):
                    last = mm(PS[:, t, 0:C + 1], xT[:, j, 128 * t:128 * t + 128], weff[:, j, :], start=(j == 0), stop=(j == NJ - 1))
            last.then_inc(tok_ps, 1)
            pe.wait_ge(ones_set, 1)
            for j in range(NJ):
                mm(PS[:, 4, 0:C], ones[0:KP, :], weff[:, j, 0:C], start=(j == 0), stop=(j == NJ - 1))
            mm(PS[:, 4, C:2 * C], ones[0:1, :], brow[:], start=True, stop=True).then_inc(tok_ps, 1)

            pe.wait_ge(ld_const, 32)
            for n, t in enumerate(TILES_TF):
                pe.wait_ge(xn_ready[0], n + 1)
                turn(TP_XN0 + n, t, xn)

            pe.wait_ge(ld_a0, 80)
            pe.wait_ge(tok_h, IT)

            def norms(n):
                (off, N, _), s, h = QK[n]
                pe.wait_ge(qk_sq, n + 1)
                if n >= 2:
                    pe.wait_ge(nm_out, n - 1)
                mm(PS[HC:HC + 6, 2 + n % 2, 0:N], nb6[:], sq[:, n % 2, 0:N], start=True, stop=True).then_inc(nm_ps, 1)
            for n, ((off, N, _), s, h) in enumerate(QK):
                pe.wait_ge(tp_out, TP_XN0 + 4 * (n // 4) + 4)
                if n >= 2:
                    pe.wait_ge(qk_aug, n - 1)
                for c in range(2):
                    last = mm(PS[0:HC, n % 2, 0:N], wqkv[:, c, s * C + h * HC:s * C + (h + 1) * HC], xnT[:, c, off:off + N],
                              start=(c == 0), stop=(c == 1))
                last.then_inc(qk_ps, 1)
                if n >= 1:
                    norms(n - 1)
            norms(len(QK) - 1)
            for n, t in enumerate(TILES_TF):
                if n >= 2:
                    pe.wait_ge(v_out, n - 1)
                for c in range(2):
                    last = mm(PS[0:ROWS[t], 4 + n % 2, 0:C], xnT[:, c, OFF[t]:OFF[t] + ROWS[t]], wqkv[:, c, 2 * C:3 * C],
                              start=(c == 0), stop=(c == 1))
                last.then_inc(v_ps, 1)
            pe.wait_ge(nm_out, len(QK))
            for n, (kind, r) in enumerate(PHI):
                b0 = 2 * (n % 2)
                if n >= 2:
                    pe.wait_ge(ph_out, n - 1)
                for u in range(2):
                    if kind == "k":
                        last = mm(PS[0:ROWS[r], b0 + u, 0:384], qkaug[1][:, u, OFF[r]:OFF[r] + ROWS[r]], bd[:], start=True, stop=True)
                    elif kind == "qt":
                        off, N, _ = CHUNK[1 + u]
                        last = mm(PS[:, b0 + u, 0:N], bd[:, (r % 3) * 128:(r % 3) * 128 + 128], qkaug[0][:, r // 3, off:off + N],
                                  start=True, stop=True)
                    else:
                        r2 = 2 * r + u
                        last = mm(PS[:, b0 + u, :], bd[:, (r2 % 3) * 128:(r2 % 3) * 128 + 128], qkaug[0][:, r2 // 3, 0:512],
                                  start=True, stop=True)
                last.then_inc(ph_ps, 1)
            pe.wait_ge(v_out, NT)
            pe.wait_ge(ph_out, NT)
            for b in range(B):
                if b >= 2:
                    pe.wait_ge(kv_out, 2 * (b - 1))
                p0 = 64 * (b % 2)
                for r in range(6):
                    o = PS[:, 4 + b % 2, r * PAIR:(r + 1) * PAIR]
                    mm(o, kp[p0:p0 + 64, b // 2, r * 128:(r + 1) * 128], v0[p0:p0 + 64, b // 2, 2 * r:2 * r + 2, :],
                       start=True, stop=False)
                    last = mm(o, kp[0:NS, IT + b, r * 128:(r + 1) * 128], v0[0:NS, IT + b, 2 * r:2 * r + 2, :],
                              start=False, stop=True)
                last.then_inc(kv_ps, 1)
            pe.wait_ge(ph_out, len(PHI))
            for n, t in enumerate(TILES):
                pe.wait_ge(kv_out, 2 * (2 * t + 2) if t < IT else 2 * (t - IT + 1))
                if n >= 2:
                    pe.wait_ge(att0, n - 1)
                parts = [(0, 64, 2 * t, OFF[t]), (64, 64, 2 * t + 1, OFF[t] + 64)] if t < IT else [(0, NS, t - IT, OFF[t])]
                for p0, P, b, off in parts:
                    for r in range(6):
                        last = mm(PS[p0:p0 + P, n % 2, r * PAIR:(r + 1) * PAIR], qp[:, r, off:off + P], kv[:, b, r, :],
                                  start=True, stop=True)
                last.then_inc(o0_ps, 1)

            def project0(n, t):
                P = ROWS[t]
                pe.wait_ge(tp_out, TP_ATT0 + n + 1)
                if n >= 2:
                    pe.wait_ge(y0_out, n - 1)
                for c in range(2):
                    last = mm(PS[0:P, 2 + n % 2, 0:C], attT0[:, c, OFF[t]:OFF[t] + P], wproj0[:, c, :], start=(c == 0), stop=(c == 1))
                last.then_inc(y0_ps, 1)
            for n, t in enumerate(TILES):
                pe.wait_ge(att0, n + 1)
                turn(TP_ATT0 + n, t, att0b)
                if n >= 1:
                    project0(n - 1, t - 1)
            project0(NT - 1, NT - 1)

            def moe(m, base):
                k, S0 = m["k"], 3 * m["slots"]
                pe.wait_ge(xn_ready[1 + 2 * k], 1)
                for t in TILES:
                    pe.wait_ge(xn_ready[1 + 2 * k], t + 1)
                    turn(base + t, t, xn)
                pe.wait_ge(tp_out, base + NT)
                pe.wait_ge(ld_moe, 32)
                for t in TILES:
                    for c in range(2):
                        last = mm(PS[0:ROWS[t], 5, t * NE:(t + 1) * NE], xnT[:, c, OFF[t]:OFF[t] + ROWS[t]], rw[:, k, c, :],
                                  start=(c == 0), stop=(c == 1))
                last.then_inc(lg_ps[k], 1)

                def hidden(i, s, first):
                    S = i * S0 + s
                    off, N, _ = CHUNK[s % 3]
                    slot = s // 3
                    if s % 3 == 0:
                        pe.wait_ge(m["ld"][slot], 16 * (m["nw"] + 1) * (i + 1))
                    for it in range(HT):
                        if m["gated"]:
                            if not first or 4 * s + it >= 2:
                                pe.wait_ge(m_g, 4 * S + it - 1)
                        elif not first or s >= 1:
                            pe.wait_ge(m_a[k], 4 * (S - 1) + it + 1)
                        for q in range(m["nw"]):
                            bank = 2 * (it % 2) + q if m["gated"] else it
                            for c in range(2):
                                last = mm(PS[:, bank, 0:N], m["w1"][slot][q][:, c, it * 128:(it + 1) * 128],
                                          xnT[:, c, off:off + N], start=(c == 0), stop=(c == 1))
                        last.then_inc(m_h[k], 1)

                def outputs(i, s, first):
                    S = i * S0 + s
                    pe.wait_ge(m_g if m["gated"] else m_a[k], 4 * S + 4)
                    o0 = CHUNK[s % 3][0]
                    for n, t in enumerate(CHUNK[s % 3][2]):
                        P, o = ROWS[t], OFF[t] - o0
                        if not first or 4 * s + n >= 2:
                            pe.wait_ge(m_acc[k], 4 * S + n - 1)
                        elif k == 0 and n == 1:
                            pe.wait_ge(imp_read, 1)
                        for it in range(HT):
                            last = mm(PS[0:P, 4 + n % 2, 0:C], m["h"][:, s % m["slots"], it, o:o + P], m["w2"][s // 3][:, it, :],
                                      start=(it == 0), stop=(it == HT - 1))
                        last.then_inc(m_y[k], 1)

                def body(i, first):
                    hidden(i, 0, first)
                    for s in range(S0):
                        if s + 1 < S0:
                            hidden(i, s + 1, first)
                        if first and s == 0:
                            if k == 0:
                                pe.wait_ge(imp_in, 1)
                                mm(PS[:, 5, 0:IT * NE], ones[:], rt[:, 1, 0:IT, :], start=True, stop=True)
                                mm(PS[:, 5, IT * NE:NT * NE], ones[0:NS, :], rt[0:NS, 1, IT:NT, :], start=True, stop=True).then_inc(imp_ps, 1)
                            pe.wait_ge(rt_in[k], 1)
                        outputs(i, s, first)

                body(0, True)
                with pe.Fori(1, m["iters"]) as i:
                    body(i, False)

            moe(MOE[0], TP_XN1)

            for t in TILES:
                pe.wait_ge(xn_ready[2], t + 1)
                turn(TP_XN2 + t, t, xn)
            pe.wait_ge(ld_a1, 64)
            n = 0
            for ci, (off, N, _) in enumerate(CHUNK):
                pe.wait_ge(tp_out, TP_XN2 + 4 * ci + 4)
                for s in range(2):
                    for h in range(2):
                        if ci >= 1:
                            if s == 0:
                                pe.wait_ge(q1_act, 2 * (ci - 1) + h + 1)
                            else:
                                pe.wait_ge(q1_dve, 4 * (ci - 1) + 2 * h + 2)
                        for c in range(2):
                            last = mm(PS[0:HC, n % 4, 0:N], wat[:, c, s * C + h * HC:s * C + (h + 1) * HC], xnT[:, c, off:off + N],
                                      start=(c == 0), stop=(c == 1))
                        last.then_inc(q1_ps, 1)
                        n += 1
            for n, (slot, P, cols) in enumerate(VJ1):
                if n >= 2:
                    pe.wait_ge(v1_out, n - 1)
                else:
                    pe.wait_ge(m_acc[0], NE * NT)
                p0 = 0
                for off, w in cols:
                    for c in range(2):
                        last = mm(PS[p0:p0 + w, 4 + n % 2, 0:C], xnT[:, c, off:off + w], wat[:, c, 2 * C:3 * C],
                                  start=(c == 0), stop=(c == 1))
                    p0 += w
                last.then_inc(v1_ps, 1)

            def score(p0, P, bank, col, g, x, qoff, koff, w):
                rows = slice(32 * g, 32 * g + 32)
                return mm(PS[p0:p0 + P, bank, col:col + w], qT1[rows, x // 2, qoff:qoff + P],
                          kT1[x % 2][rows, x // 2, koff:koff + w], start=False, stop=True, skip_group_check=True)

            def scores(u):
                t, b, g = UNITS[u]
                b0 = 2 * (u % 2)
                if u >= 2:
                    pe.wait_ge(s_sub, u - 1)
                P, masks = (128, [(0, 64)]) if t is not None else (NS, [(64, NS), (64 + NS, NS)])
                for a, (m0, w) in enumerate(masks):
                    mm(PS[0:P, b0 + a, 0:4 * w].rearrange("p (h e) -> p h e", h=4), identb[0:P, 0:P],
                       cmask[0:P, m0:m0 + w].unsqueeze(1).broadcast_to([P, 4, w]), start=True, stop=False, skip_group_check=True)
                for x in range(4):
                    if t is not None:
                        for z in range(2):
                            off = OFF[t] + 64 * z
                            last = score(64 * z, 64, b0, x * 64, g, x, off, off, 64)
                    else:
                        qoff = OFF[IT + b]
                        score(0, NS, b0, x * NS, g, x, qoff, 64 * b, 64)
                        last = score(0, NS, b0 + 1, x * NS, g, x, qoff, qoff, NS)
                last.then_inc(s_ps, 1)

            def turn_probs(u):
                pe.wait_ge(s_exp, u + 1)
                if u >= 1:
                    pe.wait_ge(t_act, u)
                    pe.wait_ge(t_dve, u)
                if u < IMG_UNITS:
                    for y in range(2):
                        last = nc.tensor.transpose(PS[:, 4 + y, 0:128], sx[:, u % 2, 128 * y:128 * y + 128], ident[:])
                else:
                    for x in range(4):
                        nc.tensor.transpose(PS[0:64, 4, NS * x:NS * x + NS], sx[0:NS, u % 2, NS * x:NS * x + 64],
                                            ident[0:NS, 0:NS])
                        last = nc.tensor.transpose(PS[0:NS, 5, NS * x:NS * x + NS], sx[0:NS, u % 2, NS * (4 + x):NS * (5 + x)],
                                                   ident[0:NS, 0:NS])
                last.then_inc(t_ps, 1)

            def weigh(u):
                t, b, g = UNITS[u]
                pe.wait_ge(t_act, u + 1)
                pe.wait_ge(t_dve, u + 1)
                if u == 0:
                    pe.wait_ge(tp_out, TP_XN2 + NT)
                else:
                    pe.wait_ge(att1, u if u <= IMG_UNITS else u - 1)
                for x in range(4):
                    y, z = x // 2, x % 2
                    h = 6 * y + 2 * g + z
                    if t is not None:
                        rows = slice(64 * z, 64 * z + 64)
                        for k in range(2):
                            c0 = 4 * NS * y + 64 * k
                            last = mm(PS[64 * k:64 * k + 64, 6 + z, 17 * y:17 * y + 17], pT[rows, u % 2, c0:c0 + 64],
                                      v1[rows, t if k == z else NT + t, h, :], start=True, stop=True)
                    else:
                        o = PS[0:NS, 6 + u % 2, 17 * x:17 * x + 17]
                        vt = b // 2 if b % 2 == 0 else NT + b // 2
                        mm(o, pT[0:64, u % 2, NS * x:NS * x + NS], v1[0:64, vt, h, :], start=True, stop=False)
                        last = mm(o, pT[0:NS, u % 2, NS * (4 + x):NS * (5 + x)], v1[0:NS, IT + b, h, :], start=False, stop=True)
                last.then_inc(o1_ps, 1)

            pe.wait_ge(masks_set, 2)
            pe.wait_ge(q1_act, 6)
            pe.wait_ge(q1_dve, 12)
            pe.wait_ge(v1_out, len(VJ1))
            for u in range(AFTER_UNITS + 2):
                if u < AFTER_UNITS:
                    scores(u)
                if 1 <= u <= AFTER_UNITS:
                    turn_probs(u - 1)
                if u >= 2:
                    weigh(u - 2)
            pe.wait_ge(att1, AFTER_UNITS)

            def project1(t):
                P = ROWS[t]
                pe.wait_ge(tp_out, TP_ATT1 + t + 1)
                if t >= 2:
                    pe.wait_ge(h3, t - 1)
                for c in range(2):
                    last = mm(PS[0:P, t % 2, 0:C], attT1[:, c, OFF[t]:OFF[t] + P], wproj1[:, c, :], start=(c == 0), stop=(c == 1))
                last.then_inc(y1_ps, 1)
            for t in TILES:
                turn(TP_ATT1 + t, t, att1b)
                if t >= 1:
                    project1(t - 1)
            project1(NT - 1)
            moe(MOE[1], TP_XN3)


def arrange(x, x_txt, mask_BS_i2_0, L0_tok_gamma, L0_tok_beta, L0_tok_W, L0_tok_b, L0_txt_token_table, L0_txt_segm_table,
            L0_attn_W_qkv, L0_attn_W_proj, L0_attn_b_proj, L0_attn_gamma, L0_attn_beta, L0_attn_random_features,
            L0_ffn_router_w, L0_ffn_w1, L0_ffn_w2, L1_attn_W_attn, L1_attn_W_proj, L1_ffn_gate_w, L1_ffn_w1, L1_ffn_w2,
            L1_ffn_w3, L1_ffn_ws1, L1_ffn_ws2, L1_ffn_ws3):
    f = np.float32
    a = {}
    n = SIDE // PATCH
    xp = np.zeros((B, CH, SIDE + 2, SIDE + 2), f)
    xp[:, :, 1:-1, 1:-1] = x
    win = np.zeros((HALO, CH, HALO, B, n, n), f)
    for r in range(HALO):
        for q in range(HALO):
            win[r, :, q] = xp[:, :, r:r + PATCH * (n - 1) + 1:PATCH, q:q + PATCH * (n - 1) + 1:PATCH].transpose(1, 0, 2, 3)
    a["xT"] = win.reshape(HALO, CH, 2, NJ, B * n * n).transpose(2, 0, 1, 3, 4).reshape(KP, NJ, B * n * n)

    def by_pixel(w):
        w = np.asarray(w).reshape(PATCH, PATCH, NG, CH, -1)
        o = np.zeros((NG, HALO, CH, HALO, w.shape[-1]), w.dtype)
        for g, (dr, dq) in enumerate(((1, 1), (1, 0), (1, 2), (0, 1), (2, 1))):
            o[g, dr:dr + PATCH, :, dq:dq + PATCH] = w[:, :, g].transpose(0, 2, 1, 3)
        o = o.reshape(NG, HALO, CH, 2, NJ, -1).transpose(3, 1, 2, 0, 4, 5)
        return o.reshape(KP, NG, NJ, -1)
    a["wt"] = by_pixel(L0_tok_W)
    a["gb"] = np.stack([by_pixel(L0_tok_gamma)[..., 0], by_pixel(L0_tok_beta)[..., 0]], 1)
    a["mult"] = by_pixel(np.ones(PDIM, f))[..., 0].sum(1)
    a["tokb"] = L0_tok_b[None, :]
    a["ident"] = np.eye(128, dtype=f)
    p_, i_ = np.arange(NS, dtype=np.float64)[:, None], np.arange(C, dtype=np.float64)[None, :]
    ang = p_ / np.power(10000.0, np.floor(i_ / 2) * 2 / C)
    a["pos"] = np.where(np.arange(C) % 2 == 0, np.sin(ang), np.cos(ang)).astype(f)
    a["ids"] = np.concatenate([x_txt.T, mask_BS_i2_0.T], 1)
    a["table"] = L0_txt_token_table
    a["segt"] = L0_txt_segm_table

    def halves(w):
        return np.asarray(w).reshape(2, HC, -1).transpose(1, 0, 2)
    a["wqkv"] = halves(L0_attn_W_qkv)
    bd = np.zeros((HC + 6, 6 * M), f)
    nb = np.zeros((HC, 6), f)
    for h in range(6):
        bd[h * DH:(h + 1) * DH, h * M:(h + 1) * M] = L0_attn_random_features.T
        bd[HC + h, h * M:(h + 1) * M] = 1.0
        nb[h * DH:(h + 1) * DH, h] = -0.5
    a["bd"], a["nb6"] = bd, nb
    a["wproj0"] = halves(L0_attn_W_proj)
    a["rows3"] = np.stack([np.broadcast_to(v, (128, C)) for v in (L0_attn_b_proj, L0_attn_gamma, L0_attn_beta)], 1)
    a["rw"] = np.stack([halves(L0_ffn_router_w.T), halves(L1_ffn_gate_w.T)], 1)
    a["rank"] = np.broadcast_to(np.arange(NE, 0, -1).astype(f), (128, NE))
    a["wat"] = halves(L1_attn_W_attn)
    a["wproj1"] = halves(L1_attn_W_proj)
    odd = (np.arange(HC) // DH) % 2
    a["kmask"] = np.stack([0.25 * (1 - odd), 0.25 * odd], 1).astype(f)
    ci = np.where(np.arange(64)[None, :] <= (np.arange(128) % 64)[:, None], 0.0, -1e9)
    ct = np.where(np.arange(NS)[None, :] <= np.arange(128)[:, None], 0.0, -1e9)
    pad = np.where(np.arange(NS)[None, :] < 64, 0.0, -1e9) * np.ones((128, 1))
    a["cmask"] = np.concatenate([ci, pad, ct], 1).astype(f)

    def up(w):
        return halves(w.T).reshape(HC, 2 * HID)

    def down(w):
        return np.asarray(w).T.reshape(HT, 128, C).transpose(1, 0, 2).reshape(128, HT * C)
    a["m0_w1"] = np.concatenate([up(L0_ffn_w1[e]) for e in range(NE)])
    a["m0_w2"] = np.concatenate([down(L0_ffn_w2[e]) for e in range(NE)])
    g1 = list(L1_ffn_w1) + [L1_ffn_ws1]
    g3 = list(L1_ffn_w3) + [L1_ffn_ws3]
    g2 = list(L1_ffn_w2) + [L1_ffn_ws2]
    a["m1_w1"] = np.concatenate([up(w) for e in range(NE + 1) for w in (g1[e], g3[e])])
    a["m1_w2"] = np.concatenate([down(w) for w in g2])
    return a


def kernel(**inputs):
    import concourse.bacc as _bacc
    from concourse.bass_utils import run_bass_kernel_spmd as _run

    nc = _bacc.Bacc("TRN2", target_bir_lowering=False, num_devices=1)
    arrays, aps = {}, {}
    for name, v in arrange(**{k: np.asarray(v) for k, v in inputs.items()}).items():
        v = np.ascontiguousarray(v)
        arrays[f"in_{name}"] = v
        aps[name] = nc.dram_tensor(f"in_{name}", v.shape, mybir.dt.from_np(v.dtype), kind="ExternalInput").ap()
    out = nc.dram_tensor("out_h", (NTOK, C), F32, kind="ExternalOutput").ap()
    build(nc, aps, out)
    r = _run(nc, [arrays], core_ids=[0])
    got = np.asarray(r.results[0]["out_h"])
    return np.concatenate([got[:B * NP_].reshape(B, NP_, C), got[B * NP_:].reshape(B, NS, C)], 1)
```

```python
from contextlib import ExitStack

import numpy as np
import concourse.bass as bass
from concourse import mybir

ALU = mybir.AluOpType
ACT = mybir.ActivationFunctionType
F32 = mybir.dt.float32
BF16 = mybir.dt.bfloat16
I32 = mybir.dt.int32
AX = mybir.AxisListType.X

B, SIDE, PATCH, CH = 8, 128, 16, 3
NP_ = (SIDE // PATCH) ** 2
VOCAB, NSEG = 8000, 3
NS = 77
C = 192
HC = C // 2
NH, DH, M = 12, 16, 64
NE, HID = 8, 512
HT = HID // 128
HALO = PATCH + 2
KP = 2 * HALO * CH
NJ = HALO // 2
NG = 5
PDIM = PATCH * PATCH * CH * NG
IT = B * NP_ // 128
NTOK = B * (NP_ + NS)
NT = -(-NTOK // 128)
ROWS = [min(128, NTOK - 128 * t) for t in range(NT)]
OFF = [128 * t for t in range(NT)]
TT = NT - IT
NB = IT + B
BROWS = [128] * IT + [NS] * B
BOFF = [128 * t for t in range(IT)] + [IT * 128 + NS * b for b in range(B)]
CHUNK = [(0, 512, (0, 1, 2, 3)), (512, 512, (4, 5, 6, 7)), (1024, NTOK - 1024, (8,))]
TEXT_FIRST = [CHUNK[1], CHUNK[2], CHUNK[0]]
PAIR = 2 * (DH + 1)
NK = NP_ + NS
CHUNK1 = [(0, 512, 4), (512, 4 * NS, -(-(512 + 4 * NS) // 128)), (512 + 4 * NS, 4 * NS, NT)]
EPS = 1e-5

TOK = dict(x=(0, NJ * 512), x2=(4608, NJ * 512), w=(9216, NG * NJ * C), weff=(17856, NJ * (C + 1)), seg=(19600, TT * C),
           pos=(20560, TT * C), beta=(21520, 2 * NJ * C))
A0 = dict(qaug=(0, 2 * NTOK), kaug=(2280, 2 * NTOK), att=(0, NB * C), attT=(2304, 2 * NTOK), qp=(4560, 6 * NTOK),
          kp=(11328, NB * NH * M), v=(20544, NB * NH * 17), kv=(22992, B * 6 * PAIR))
A1 = dict(qT=(0, 2 * NTOK), kT=(2256, 2 * NTOK), ko=(4512, 3 * 4 * NK), v=(6768, B * NH * 17), vi=(8400, B * NH * 17), sx=(10032, 3 * 4 * NK),
          att=(11880, NB * C), attT=(14184, 2 * NTOK))
ES = (2 * HID + HT * C, 4 * HID + HT * C)
ARENA = A0["kv"][0] + A0["kv"][1] + 6 * ES[0]
WBASE = (ARENA - NE * ES[0], ARENA - NE * ES[1])
MB = dict(xs=(0, 2 * (C + 1)), xsT=(386, 4 * 128), act=(898, 2 * HID), hT=(1922, 2 * HID), ys=(2946, 2 * C),
          back=(3330, 2 * NT * C), sh=(3330, 3 * HT * 512), sa=(9474, 2 * 512))
CAP = 128
NSLOT = (2 * NTOK + NE * (CAP - 1)) // CAP
MAXT = -(-NTOK // CAP)
CHOICE = 128 * NT
NY = 1 + 2 * CHOICE
SENT_A = 5


def build(nc, d, out):
    with ExitStack() as ctx:
        def sb(name, shape, dt=F32):
            return ctx.enter_context(nc.sbuf_tensor(name, shape, dt))

        def sem(name):
            return ctx.enter_context(nc.semaphore(name))

        arena = sb("arena", [128, ARENA])

        def at(place):
            return arena[:, place[0]:place[0] + place[1]]

        PS = ctx.enter_context(nc.psum_tensor("PS", [128, 8, 512], F32))

        H = sb("H", [128, NT, C])
        xnd = sb("xnd", [128, NT, C + 1])
        xn = xnd[:, :, 0:C]
        xnT = sb("xnT", [HC, 2, NTOK])
        bnst = sb("bnst", [128, NT, 6])
        mv = sb("mv", [128, NT, 2])
        rstd = sb("rstd", [128, 2, NT])
        mhalf = sb("mhalf", [128, NT])
        ident = sb("ident", [128, 128])
        identb = sb("identb", [128, 128], BF16)
        ones = sb("ones", [128, 128])
        ids = sb("ids", [128, 2 * TT], I32)
        idx = sb("idx", [128, 3, 2 * TT], I32)
        gb = sb("gb", [KP, 2, NG, NJ])
        mult = sb("mult", [KP, NJ])
        tokb = sb("tokb", [1, C])
        sgbw = sb("sgbw", [128, 2 * C])
        tst = sb("tst", [128, 6, IT])
        wqkv = sb("wqkv", [HC, 2, 3 * C])
        bd = sb("bd", [HC + 6, 6 * M])
        nb6 = sb("nb6", [HC, 6])
        wproj0 = sb("wproj0", [HC, 2, C])
        rows3 = sb("rows3", [128, 3, C])
        rec = sb("rec", [128, 2, NH])
        wat = sb("wat", [HC, 2, 3 * C])
        wproj1 = sb("wproj1", [HC, 2, C])
        kmask = sb("kmask", [HC, 6])
        cmaskf = sb("cmaskf", [128, NP_ + NS])
        cmask = sb("cmask", [128, NP_ + NS], BF16)
        rw = sb("rw", [HC, 2, 2, NE])
        rank = sb("rank", [128, NE])
        lg = sb("lg", [128, NT, NE])
        rt = sb("rt", [128, 6, NT, NE])
        rs = sb("rs", [128, 6, NT])
        run = sb("run", [128, 3, NE])
        cw = sb("cw", [128, 3, NT])
        cnt = sb("cnt", [128, 4, NE * NT])
        tiles_of = sb("tiles_of", [128, 4, NE])
        place = sb("place", [128, 2, NT], I32)
        eidf = sb("eidf", [1, NSLOT, NE])
        eids = sb("eids", [1, NSLOT])
        eid = sb("eid", [1, NSLOT], I32)
        routec = sb("routec", [128, NE * NT + NE + NE * MAXT + NSLOT + NT + 128])
        zero = sb("zero", [128, C + 1])
        dest = sb("dest", [128, 4], I32)
        wsh = sb("wsh", [128, ES[1]])
        mx = sb("mx", [128, 2, 4])

        ld_x, ld_tokc, ld_const, ld_ids, ld_a0, ld_moe, ld_a1 = (
            sem(n) for n in ("ld_x", "ld_tokc", "ld_const", "ld_ids", "ld_a0", "ld_moe", "ld_a1"))
        ld_w = [sem(f"ld_w{g}") for g in range(NG)]
        ld_e = [sem("ld_e0"), sem("ld_e1")]
        ld_sh, zero_set, slots_zero = sem("ld_sh"), sem("zero_set"), sem("slots_zero")
        gathered, idx_set = sem("gathered"), sem("idx_set")
        stored = sem("stored")
        ones_set, lg_set, v_ones0, v_ones1, kv_zero = (sem(n) for n in ("ones_set", "lg_set", "v_ones0", "v_ones1", "kv_zero"))
        x2_done, fold0, folded, beta_sum, tok_ps, sg_sb, tok_h, text_h = (
            sem(n) for n in ("x2_done", "fold0", "folded", "beta_sum", "tok_ps", "sg_sb", "tok_h", "text_h"))
        mult_set, var_in, rs_out, mhalf_set = (sem(n) for n in ("mult_set", "var_in", "rs_out", "mhalf_set"))
        xn_ready = [sem(f"xn_ready{k}") for k in range(4)]
        tp_ps, tp_out = sem("tp_ps"), sem("tp_out")
        qk_ps, qk_sq, qk_aug, nm_ps, nm_out = (sem(n) for n in ("qk_ps", "qk_sq", "qk_aug", "nm_ps", "nm_out"))
        v_ps, v_out, ph_ps, ph_out, kv_ps, kv_out = (sem(n) for n in ("v_ps", "v_out", "ph_ps", "ph_out", "kv_ps", "kv_out"))
        o0_ps, att0, y0_ps, y0_out, xnb, yn, hb, h1 = (
            sem(n) for n in ("o0_ps", "att0", "y0_ps", "y0_out", "xnb", "yn", "hb", "h1"))
        lg_ps = [sem(f"lg_ps{k}") for k in range(2)]
        rt_in = [sem(f"rt_in{k}") for k in range(2)]
        rt_exp = [sem(f"rt_exp{k}") for k in range(2)]
        masks_set = sem("masks_set")
        imp_in, imp_ps, imp_read = sem("imp_in"), sem("imp_ps"), sem("imp_read")
        rank_ps, sel_in, placed = ([sem(f"{n}{k}") for k in range(2)] for n in ("rank_ps", "sel_in", "placed"))
        u_ps, u_act, g_out = sem("u_ps"), sem("u_act"), sem("g_out")
        ysh_ps, ysh_acc = sem("ysh_ps"), sem("ysh_acc")
        sent_a, sent_b, sent, rows_set, dest_set = (
            [sem(f"{n}{k}") for k in range(2)] for n in ("sent_a", "sent_b", "sent", "rows_set", "dest_set"))
        xs_in = [[sem(f"xs_in{k}_{z}") for z in range(2)] for k in range(2)]
        ys_out = [[sem(f"ys_out{k}_{z}") for z in range(2)] for k in range(2)]
        xt_ps, xt_sb, up_ps, up_act, up_sb, ht_ps, ht_sb, dn_ps, dn_sb, added = (
            [sem(f"{n}{k}") for k in range(2)] for n in ("xt_ps", "xt_sb", "up_ps", "up_act", "up_sb", "ht_ps", "ht_sb",
                                                         "dn_ps", "dn_sb", "added"))
        back = [[sem(f"back{k}_{t}") for t in range(NT)] for k in range(2)]
        q1_ps, q1_act, q1_dve, v1_ps, v1_out = (sem(n) for n in ("q1_ps", "q1_act", "q1_dve", "v1_ps", "v1_out"))
        own_set, s_ps, s_sub, s_exp, t_ps, t_act, o1_ps, att1, y1_ps, h3 = (
            sem(n) for n in ("own_set", "s_ps", "s_sub", "s_exp", "t_ps", "t_act", "o1_ps", "att1", "y1_ps", "h3"))
        dve_step, pool_step = sem("dve_step"), sem("pool_step")

        xT = at(TOK["x"])[0:KP].rearrange("p (j n) -> p j n", j=NJ)
        x2 = at(TOK["x2"])[0:KP].rearrange("p (j n) -> p j n", j=NJ)
        wt = at(TOK["w"])[0:KP].rearrange("p (g j n) -> p g j n", g=NG, j=NJ)
        weff = at(TOK["weff"])[0:KP].rearrange("p (j n) -> p j n", j=NJ)
        seg = at(TOK["seg"]).rearrange("p (b n) -> p b n", b=TT)
        pos = at(TOK["pos"]).rearrange("p (b n) -> p b n", b=TT)
        betaw = at(TOK["beta"])[0:KP].rearrange("p (u j n) -> p u j n", u=2, j=NJ)
        qkaug = [at(A0[n])[0:HC + 6].rearrange("p (h n) -> p h n", h=2) for n in ("qaug", "kaug")]
        att0b = at(A0["att"]).rearrange("p (t n) -> p t n", t=NB)
        attT0 = at(A0["attT"])[0:HC].rearrange("p (h n) -> p h n", h=2)
        qp = at(A0["qp"]).rearrange("p (r n) -> p r n", r=6)
        sq = at((A0["kp"][0], 1024))[0:HC].rearrange("p (u n) -> p u n", u=2)
        kp = at(A0["kp"]).rearrange("p (t n) -> p t n", t=NB)
        v0 = at(A0["v"]).rearrange("p (t h e) -> p t h e", t=NB, h=NH)
        kv = at(A0["kv"]).rearrange("p (b r e) -> p b r e", b=B, r=6)
        qT1 = at(A1["qT"])[0:HC].rearrange("p (h n) -> p h n", h=2)
        kT1 = at(A1["kT"])[0:HC].rearrange("p (h n) -> p h n", h=2)
        kown = at(A1["ko"])[0:HC].rearrange("p (u x n) -> p u x n", u=3, x=4)
        v1 = at(A1["v"]).rearrange("p (b h e) -> p b h e", b=B, h=NH)
        vi = at(A1["vi"]).rearrange("p (b r e) -> p b r e", b=B, r=NH // 2)
        sx = at(A1["sx"]).rearrange("p (u n) -> p u n", u=3)
        pT = xnd[:].rearrange("p t n -> p (t n)")[:, 0:2 * 6 * NS].rearrange("p (u n) -> p u n", u=2)
        att1b = at(A1["att"]).rearrange("p (t n) -> p t n", t=NB)
        attT1 = at(A1["attT"])[0:HC].rearrange("p (h n) -> p h n", h=2)

        tri = routec[:, NE * NT + NE + NE * MAXT + NSLOT + NT:]
        token = routec[:, NE * NT + NE + NE * MAXT + NSLOT:NE * NT + NE + NE * MAXT + NSLOT + NT]
        xs = at(MB["xs"]).rearrange("p (z n) -> p z n", z=2)
        xsT = at(MB["xsT"])[0:HC].rearrange("p (z c n) -> p z c n", z=2, c=2)
        hact = at(MB["act"]).rearrange("p (z n) -> p z n", z=2)
        hT = at(MB["hT"]).rearrange("p (z i n) -> p z i n", z=2, i=HT)
        ys = at(MB["ys"]).rearrange("p (z n) -> p z n", z=2)
        yback = at(MB["back"]).rearrange("p (k t n) -> p k t n", k=2, t=NT)
        shT = at(MB["sh"]).rearrange("p (s i n) -> p s i n", s=3, i=HT)
        sa = at(MB["sa"]).rearrange("p (s n) -> p s n", s=2)
        wsh1 = [wsh[0:HC, q * 2 * HID:(q + 1) * 2 * HID].rearrange("p (c n) -> p c n", c=2) for q in range(2)]
        wsh2 = wsh[:, 4 * HID:].rearrange("p (i n) -> p i n", i=HT)
        Xs, Ys = (d["Xs0"], d["Xs1"]), d["Ys"]
        LAST = NSLOT - 1
        PIPE0, PAIRS = 2, (NSLOT - 5) // 2

        UNITS = [(t, None, v) for t in range(IT) for v in range(3)] + [(None, b, v) for b in range(B) for v in range(3)]
        IMG_UNITS = 3 * IT
        AFTER_UNITS = len(UNITS)

        def parts_by(u):
            return min(u + 1, IMG_UNITS) + 2 * max(0, u + 1 - IMG_UNITS)

        BTILES = list(range(IT, NB)) + list(range(IT))
        PHI = [("k", t) for t in BTILES] + [("qt", r) for r in range(6)] + [("qi", r) for r in range(3)]
        QK = [(c, s, h) for c in TEXT_FIRST for s in range(2) for h in range(2)]
        TP_XN0, TP_ATT0, TP_XN1, TP_XN2, TP_ATT1, TP_XN3 = 0, NT, NT + NB, 2 * NT + NB, 3 * NT + NB, 3 * NT + 2 * NB
        TILES_TF = [t for _, _, ts in TEXT_FIRST for t in ts]
        TILES = list(range(NT))
        NEED = [sum(BOFF[b] < OFF[t] + ROWS[t] for b in range(NB)) for t in TILES]

        block = ctx.enter_context(nc.Block())

        @block.sync
        def _(sp):
            def load_expert(k, e, dst=None):
                w = arena[:, WBASE[k] + e * ES[k]:WBASE[k] + (e + 1) * ES[k]] if dst is None else dst[:]
                done = ld_e[k] if dst is None else ld_sh
                n = 2 * HID * (1 + k)
                sp.dma_start(w[0:HC, 0:n], d[f"m{k}_w1"][e]).then_inc(done, 16)
                sp.dma_start(w[:, n:], d[f"m{k}_w2"][e]).then_inc(done, 16)

            def load_slots(k, j, z):
                if not isinstance(j, int) or j >= 2:
                    sp.wait_ge(xt_ps[k], j - 1)
                    sp.wait_ge(dest_set[k], j - 1)
                sp.dma_start(xs[:, z, :], Xs[k][bass.ds(j * CAP, CAP), :]).then_inc(xs_in[k][z], 16)

            def slots(k):
                sp.wait_ge(sent_a[k], 16 * SENT_A)
                sp.wait_ge(sent_b[k], 16 * (NT - SENT_A))
                sp.wait_ge(sent[k], 16 * NT)
                for j in range(PIPE0 + 4):
                    load_slots(k, j, j % 2)
                with sp.Fori(0, PAIRS - 1) as i:
                    for z in range(2):
                        load_slots(k, PIPE0 + 4 + 2 * i + z, z)
                for j in range(PIPE0 + 4 + 2 * (PAIRS - 1), NSLOT):
                    load_slots(k, j, j % 2)
                for z in range(2):
                    sp.wait_ge(ys_out[k][z], 16 * ((NSLOT + 1 - z) // 2))
                rows = Ys[1:NY, :].rearrange("(c t p) n -> t p c n", c=2, p=128)
                for t in TILES:
                    P = ROWS[t]
                    sp.dma_start(yback[0:P, :, t, :], rows[t, 0:P]).then_inc(back[k][t], 16)

            sp.dma_start(ids[:], d["ids"]).then_inc(ld_ids, 16)
            sp.dma_start(gb[:], d["gb"]).then_inc(ld_tokc, 16)
            sp.dma_start(mult[:], d["mult"]).then_inc(ld_tokc, 16)
            sp.dma_start(tokb[:], d["tokb"]).then_inc(ld_tokc, 16)
            sp.dma_start(xT, d["xT"]).then_inc(ld_x, 16)
            sp.dma_start(wt[:, 0], d["wt"][:, 0]).then_inc(ld_w[0], 16)
            for g in range(1, NG):
                sp.dma_start(wt[:, g], d["wt"][:, g]).then_inc(ld_w[g], 16)
            for buf, name in ((ident[:], "ident"), (pos, "pos")):
                sp.dma_start(buf, d[name]).then_inc(ld_const, 16)
            for buf, name in ((wqkv, "wqkv"), (bd, "bd"), (nb6, "nb6"), (wproj0, "wproj0"), (rows3, "rows3")):
                sp.dma_start(buf[:], d[name]).then_inc(ld_a0, 16)
            for buf, name in ((rw, "rw"), (rank, "rank")):
                sp.dma_start(buf[:], d[name]).then_inc(ld_moe, 16)
            sp.dma_start(routec[:], d["routec"]).then_inc(ld_moe, 16)
            load_expert(1, NE, wsh)
            sp.wait_ge(zero_set, 1)
            for k in range(2):
                sp.dma_start(Xs[k].rearrange("(j p) c -> p j c", p=CAP),
                             zero[:].unsqueeze(1).broadcast_to([128, NSLOT, C + 1])).then_inc(slots_zero, 16)
            for buf, name in ((wat, "wat"), (wproj1, "wproj1"), (kmask, "kmask"), (cmaskf, "cmask")):
                sp.dma_start(buf[:], d[name]).then_inc(ld_a1, 16)
            sp.wait_ge(tok_ps, 3)
            for e in range(2, NE):
                load_expert(0, e)
            sp.wait_ge(kv_ps, 2 * B)
            load_expert(0, 0)
            sp.wait_ge(o0_ps, NB)
            load_expert(0, 1)
            slots(0)
            for e in range(2, NE):
                load_expert(1, e)
            sp.wait_ge(y1_ps, NT)
            for e in range(2):
                load_expert(1, e)
            slots(1)
            for t in TILES:
                sp.wait_ge(added[1], 2 * t + 2)
                sp.dma_start(out[OFF[t]:OFF[t] + ROWS[t], :], H[0:ROWS[t], t, :]).then_inc(stored, 16)
            sp.wait_ge(stored, 16 * NT)

        @block.gpsimd
        def _(pool):
            steps = [0]

            def step(ins):
                steps[0] += 1
                ins.then_inc(pool_step, 1)
                pool.wait_ge(pool_step, steps[0])

            turns = [0]

            def rsqrt(rows, cols):
                turns[0] += 1
                pool.wait_ge(var_in, turns[0])
                pool.tensor_tensor(out=rstd[0:rows, 1, cols], in0=rstd[0:rows, 0, cols], in1=mhalf[0:rows, cols],
                                   op=ALU.pow).then_inc(rs_out, 1)

            def rsqrt_tiles(tiles):
                rsqrt(ROWS[tiles[0]], slice(tiles[0], tiles[0] + len(tiles)))

            pool.memset(ones[:], 1.0).then_inc(ones_set, 1)
            pool.memset(mhalf[:], -0.5).then_inc(mhalf_set, 1)
            pool.wait_ge(idx_set, 2)
            for b in range(TT):
                P = ROWS[IT + b]
                pool.indirect_dma_start(out=H[0:P, IT + b, :], out_offset=None, in_=d["table"],
                                        in_offset=bass.IndirectOffsetOnAxis(ap=idx[0:P, 2, b:b + 1], axis=0)).then_inc(gathered, 16)
                pool.indirect_dma_start(out=seg[0:P, b, :], out_offset=None, in_=d["segt"],
                                        in_offset=bass.IndirectOffsetOnAxis(ap=idx[0:P, 2, TT + b:TT + b + 1], axis=0)).then_inc(gathered, 16)
            pool.memset(lg[:], 0.0).then_inc(lg_set, 1)
            pool.memset(zero[:], 0.0).then_inc(zero_set, 1)
            pool.wait_ge(ld_tokc, 48)
            for g in range(NG):
                pool.wait_ge(ld_w[g], 16)
                u = min(g, 1)
                step(pool.tensor_tensor(out=betaw[:, u], in0=wt[:, g], in1=gb[:, 1, g, :].unsqueeze(2).broadcast_to([KP, NJ, C]),
                                        op=ALU.mult))
                if g >= 1:
                    ins = pool.tensor_tensor(out=betaw[:, 0], in0=betaw[:, 0], in1=betaw[:, 1], op=ALU.add)
                    step(ins) if g < NG - 1 else ins.then_inc(beta_sum, 1)
            pool.wait_ge(mhalf_set, 1)
            rsqrt_tiles(CHUNK[1][2])
            rsqrt_tiles(CHUNK[2][2])
            rsqrt(128, slice(0, IT))
            rsqrt_tiles(CHUNK[0][2])
            pool.wait_ge(tok_h, IT)
            pool.wait_ge(text_h, 2)
            pool.memset(v0[:, :, :, DH:DH + 1], 1.0).then_inc(v_ones0, 1)
            pool.memset(at(A0["kv"]), 0.0).then_inc(kv_zero, 1)
            pool.wait_ge(ld_a0, 80)
            for n, t in enumerate(TILES_TF):
                P = ROWS[t]
                pool.wait_ge(tp_ps, TP_XN0 + n + 1)
                pool.tensor_tensor(out=xn[0:P, t, :], in0=xn[0:P, t, :], in1=rows3[0:P, 0, :], op=ALU.add).then_inc(xnb, 1)
                pool.tensor_tensor(out=H[0:P, t, :], in0=H[0:P, t, :], in1=rows3[0:P, 2, :], op=ALU.add).then_inc(hb, 1)
            for c in (0, 0, 1, 2):
                rsqrt_tiles(CHUNK[c][2])

            def dispatch(k):
                pool.wait_ge(placed[k], 2)
                pool.wait_ge(slots_zero, 32)
                for c, tiles, done in ((0, TILES[:SENT_A], sent_a), (0, TILES[SENT_A:], sent_b), (1, TILES[:SENT_A], sent),
                                       (1, TILES[SENT_A:], sent)):
                    pool.wait_ge(rows_set[k], 1 if c == 0 else 2 if tiles[0] == 0 else 3)
                    for t in tiles:
                        pool.indirect_dma_start(out=Xs[k], out_offset=bass.IndirectOffsetOnAxis(ap=place[0:ROWS[t], c, t:t + 1], axis=0),
                                                in_=xnd[0:ROWS[t], t, :], in_offset=None).then_inc(done[k], 16)

            def keep_rows(k, j):
                if j >= 4:
                    pool.wait_ge(ys_out[k][j % 2], 16 * (j // 2 - 1))
                pool.wait_ge(xs_in[k][j % 2], 16 * (j // 2 + 1))
                pool.tensor_copy(dest[:, j % 4:j % 4 + 1], xs[:, j % 2, C:C + 1]).then_inc(dest_set[k], 1)

            def scatter(k, j):
                pool.wait_ge(dest_set[k], j + 1)
                if j >= 1:
                    pool.wait_ge(ys_out[k][(j - 1) % 2], 16 * ((j - 1) // 2 + 1))
                pool.wait_ge(dn_sb[k], j + 1)
                pool.indirect_dma_start(out=Ys, out_offset=bass.IndirectOffsetOnAxis(ap=dest[:, j % 4:j % 4 + 1], axis=0),
                                        in_=ys[:, j % 2, :], in_offset=None).then_inc(ys_out[k][j % 2], 16)

            def slots(k):
                for j in range(3):
                    keep_rows(k, j)
                for s in range(1, NSLOT + 1):
                    if s + 2 <= LAST:
                        keep_rows(k, s + 2)
                    scatter(k, s - 1)

            for _, _, tiles in CHUNK[1:]:
                rsqrt_tiles(tiles)
            dispatch(0)
            slots(0)
            for _, _, tiles in CHUNK:
                rsqrt_tiles(tiles)
            pool.wait_ge(added[0], 2 * NT)
            for buf, value in ((vi[0:64, :, :, DH:DH + 1], 1.0), (vi[64:128, :, :, PAIR - 1:PAIR], 1.0), (vi[0:64, :, :, DH + 1:], 0.0),
                               (vi[64:128, :, :, 0:DH + 1], 0.0)):
                step(pool.memset(buf, value))
            pool.memset(v1[:, :, :, DH:DH + 1], 1.0).then_inc(v_ones1, 1)
            pool.wait_ge(ld_a1, 64)
            pool.tensor_copy(identb[:], ident[:]).then_inc(masks_set, 1)
            pool.tensor_copy(cmask[:], cmaskf[:]).then_inc(masks_set, 1)
            pool.wait_ge(q1_dve, 6)
            for u, (t, b, v) in enumerate(UNITS):
                if u >= 3:
                    pool.wait_ge(s_ps, u - 2)
                for a in range(2):
                    half, h = (2 * v + a) // 3, 2 * ((2 * v + a) % 3)
                    if t is not None:
                        dst = kown[:, u % 3, 2 * a:2 * a + 2, 0:2 * NP_].rearrange("p z (k n) -> p z k n", k=2)
                        src = kT1[:, half, :].rearrange("p (b n) -> p b n", b=B)[:, 2 * t:2 * t + 2, 0:NP_]
                        src = src.unsqueeze(1).broadcast_to([HC, 2, 2, NP_])
                        own = kmask[:, h:h + 2].unsqueeze(2).unsqueeze(3).broadcast_to([HC, 2, 2, NP_])
                    else:
                        dst = kown[:, u % 3, 2 * a:2 * a + 2, :]
                        src = kT1[:, half, NK * b:NK * (b + 1)].unsqueeze(1).broadcast_to([HC, 2, NK])
                        own = kmask[:, h:h + 2].unsqueeze(2).broadcast_to([HC, 2, NK])
                    pool.tensor_tensor(out=dst, in0=src, in1=own, op=ALU.mult).then_inc(own_set, 1)
            for _, _, tiles in CHUNK:
                rsqrt_tiles(tiles)
            dispatch(1)
            slots(1)

        @block.scalar
        def _(act):
            A = nc.scalar.activation

            def tp_evac(n, t, dst):
                off, P = t if isinstance(t, tuple) else (OFF[t], ROWS[t])
                act.wait_ge(tp_ps, n + 1)
                A(dst[:, :, off:off + P],
                  PS[0:HC, 6 + n % 2, 0:256].rearrange("p (h n) -> p h n", h=2)[:, :, 0:P], ACT.Copy).then_inc(tp_out, 1)

            act.wait_ge(ld_tokc, 48)
            A(weff[:, :, C:C + 1], mult[:].unsqueeze(2), ACT.Copy).then_inc(mult_set, 1)
            act.wait_ge(ld_x, 16)
            A(x2, xT, ACT.Square).then_inc(x2_done, 1)
            act.wait_ge(ld_w[0], 16)
            for j in range(NJ):
                A(weff[:, j, 0:C], wt[:, 0, j, :], ACT.Copy, scale=gb[:, 0, 0, j:j + 1]).then_inc(fold0, 1)
            act.wait_ge(tok_ps, 3)
            A(sgbw[:], PS[:, 4, 0:2 * C], ACT.Copy).then_inc(sg_sb, 1)

            for n, t in enumerate(TILES_TF):
                tp_evac(TP_XN0 + n, t, xnT)
            for n, ((off, N, _), s, h) in enumerate(QK):
                act.wait_ge(qk_aug, n + 1)
                if n >= 2:
                    act.wait_ge(nm_ps, n - 1)
                A(sq[:, n % 2, 0:N], qkaug[s][0:HC, h, off:off + N], ACT.Square).then_inc(qk_sq, 1)
            act.wait_ge(v_ones0, 1)
            for n, t in enumerate(BTILES):
                act.wait_ge(v_ps, n + 1)
                A(v0[0:BROWS[t], t, :, 0:DH], PS[0:BROWS[t], 4 + n % 2, 0:C].rearrange("p (h e) -> p h e", h=NH),
                  ACT.Copy).then_inc(v_out, 1)
            for n, (kind, r) in enumerate(PHI):
                act.wait_ge(ph_ps, n + 1)
                b0 = 2 * (n % 2)
                if kind == "k":
                    A(kp[0:BROWS[r], r, :].rearrange("p (u n) -> p u n", u=2), PS[0:BROWS[r], b0:b0 + 2, 0:384],
                      ACT.Exp).then_inc(ph_out, 1)
                elif kind == "qt":
                    A(qp[:, r, 512:NTOK].rearrange("p (u n) -> p u n", u=2), PS[:, b0:b0 + 2, 0:4 * NS],
                      ACT.Exp).then_inc(ph_out, 1)
                else:
                    A(qp[:, 2 * r:2 * r + 2, 0:512], PS[:, b0:b0 + 2, :], ACT.Exp).then_inc(ph_out, 1)
            for t in range(NB):
                tp_evac(TP_ATT0 + t, (BOFF[t], BROWS[t]), attT0)

            def turned_rows(k, j, z):
                act.wait_ge(xt_ps[k], j + 1)
                if not isinstance(j, int) or j >= 2:
                    act.wait_ge(up_ps[k], j - 1)
                A(xsT[:, z, :, :], PS[0:HC, 6, 0:256].rearrange("p (c n) -> p c n", c=2), ACT.Copy).then_inc(xt_sb[k], 1)

            def activate(k, j, z):
                act.wait_ge(up_ps[k], j + 1)
                if not isinstance(j, int) or j >= 2:
                    act.wait_ge(ht_ps[k], j - 1)
                bank = z if k == 0 else 2 * z
                A(hact[:, z, :], PS[:, bank, :], ACT.Silu).then_inc(up_act[k], 1)

            def result(k, j, z, round_):
                act.wait_ge(dn_ps[k], j + 1)
                if round_ is not None:
                    act.wait_ge(ys_out[k][z], 16 * round_)
                A(ys[:, z, :], PS[:, 7, 0:C], ACT.Copy).then_inc(dn_sb[k], 1)

            def slots(k):
                turned_rows(k, 0, 0)
                activate(k, 0, 0)
                turned_rows(k, 1, 1)
                activate(k, 1, 1)
                turned_rows(k, 2, 0)
                activate(k, 2, 0)
                turned_rows(k, 3, 1)
                result(k, 0, 0, None)
                with act.Fori(0, PAIRS) as i:
                    for z in range(2):
                        s = PIPE0 + 2 * i + z
                        activate(k, s + 1, 1 - z)
                        turned_rows(k, s + 2, z)
                        if z == 0:
                            act.wait_ge(ys_out[k][0], 16 * i + 16)
                            result(k, s - 1, 1, None)
                        else:
                            act.wait_ge(ys_out[k][1], 16 * i + 16)
                            result(k, s - 1, 0, i + 1)
                for s in range(PIPE0 + 2 * PAIRS, NSLOT + 1):
                    if s + 1 <= LAST:
                        activate(k, s + 1, (s + 1) % 2)
                    if s + 2 <= LAST:
                        turned_rows(k, s + 2, s % 2)
                    result(k, s - 1, (s - 1) % 2, (s - 1) // 2)

            def route_exp(k):
                act.wait_ge(rt_in[k], 1)
                A(rt[:, 0], rt[:, 0], ACT.Exp).then_inc(rt_exp[k], 1)

            for t in TILES:
                tp_evac(TP_XN1 + t, t, xnT)
            route_exp(0)
            slots(0)
            for t in TILES:
                tp_evac(TP_XN2 + t, t, xnT)
            act.wait_ge(ld_a1, 64)
            for c, (off, N, _) in enumerate(CHUNK1):
                for h in range(2):
                    act.wait_ge(q1_ps, 4 * c + h + 1)
                    A(qT1[:, h, off:off + N], PS[0:HC, h, 0:N], ACT.Copy).then_inc(q1_act, 1)
            act.wait_ge(v_ones1, 1)
            for n in range(2 * B):
                act.wait_ge(v1_ps, n + 1)
                b, src = n % B, PS[:, 4 + n % 2, 0:C]
                if n < B:
                    for z in range(2):
                        rows = slice(64 * z, 64 * z + 64)
                        A(vi[rows, b, :, 17 * z:17 * z + DH], src[rows, 0:HC].rearrange("p (r e) -> p r e", e=DH),
                          ACT.Copy).then_inc(v1_out, 1)
                else:
                    A(v1[0:NS, b, :, 0:DH].rearrange("p (r z) e -> p z r e", z=2),
                      src[0:NS].rearrange("p (z r e) -> p z r e", z=2, e=DH), ACT.Copy).then_inc(v1_out, 1)

            def probs(u):
                P, w = (128, 256) if u < IMG_UNITS else (NS, 4 * NK)
                act.wait_ge(s_sub, parts_by(u))
                A(sx[0:P, u % 3, 0:w], sx[0:P, u % 3, 0:w], ACT.Exp).then_inc(s_exp, 1)

            def turned(u):
                act.wait_ge(t_ps, u + 1)
                if u >= 2:
                    act.wait_ge(o1_ps, u - 1)
                if u < IMG_UNITS:
                    A(pT[:, u % 2, 0:256], PS[:, 4 + u % 2, 0:256], ACT.Copy).then_inc(t_act, 1)
                else:
                    A(pT[:, u % 2, 0:2 * NS], PS[:, 4 + u % 2, 0:2 * NS], ACT.Copy).then_inc(t_act, 1)
                    A(pT[0:NS, u % 2, 2 * NS:6 * NS], PS[0:NS, 4 + u % 2, 2 * NS:6 * NS], ACT.Copy).then_inc(t_act, 1)

            for u in range(AFTER_UNITS + 2):
                if u < AFTER_UNITS:
                    probs(u)
                if u >= 2:
                    turned(u - 2)
            for t in range(NB):
                tp_evac(TP_ATT1 + t, (BOFF[t], BROWS[t]), attT1)
            for t in TILES:
                tp_evac(TP_XN3 + t, t, xnT)
            route_exp(1)
            for n in range(3 * HT):
                N = CHUNK[n // HT][1]
                act.wait_ge(u_ps, n + 1)
                if n >= 2:
                    act.wait_ge(g_out, n - 1)
                A(sa[:, n % 2, 0:N], PS[:, 2 * (n % 2), 0:N], ACT.Silu).then_inc(u_act, 1)
            slots(1)

        @block.vector
        def _(dve):
            V = nc.vector
            steps, norms = [0], [0]

            def step(ins):
                steps[0] += 1
                ins.then_inc(dve_step, 1)
                dve.wait_ge(dve_step, steps[0])

            def ln_stats(tiles, src, ready):
                P, t0, n = ROWS[tiles[0]], tiles[0], len(tiles)
                for t in tiles:
                    ready(t)
                    steps[0] += 1
                    V.bn_stats(bnst[0:P, t, :], src[0:P, t, :]).then_inc(dve_step, 1)
                dve.wait_ge(dve_step, steps[0])
                for t in tiles:
                    steps[0] += 1
                    V.bn_aggr(mv[0:P, t, :], bnst[0:P, t, :]).then_inc(dve_step, 1)
                dve.wait_ge(dve_step, steps[0])
                V.tensor_scalar(rstd[0:P, 0, t0:t0 + n], mv[0:P, t0:t0 + n, 1], EPS, None, ALU.add).then_inc(var_in, 1)

            def ln_scale(tiles, src, done):
                P = ROWS[tiles[0]]
                norms[0] += 1
                dve.wait_ge(rs_out, norms[0])
                for t in tiles:
                    V.tensor_scalar(xn[0:P, t, :], src[0:P, t, :], mv[0:P, t, 0:1], rstd[0:P, 1, t:t + 1],
                                    ALU.subtract, ALU.mult).then_inc(done, 1)

            def layernorm(chunks, src, ready, done, scaled=lambda tiles: None):
                tiles = [c[2] for c in chunks]
                ln_stats(tiles[0], src, ready)
                for n in range(len(tiles)):
                    if n + 1 < len(tiles):
                        ln_stats(tiles[n + 1], src, ready)
                    ln_scale(tiles[n], src, done)
                    scaled(tiles[n])

            dve.wait_ge(ld_ids, 16)
            for k, size in enumerate((VOCAB, NSEG)):
                own = slice(TT * k, TT * k + TT)
                step(V.tensor_scalar(idx[:, 0, own], ids[:, own], 0.0, float(size), ALU.is_lt, ALU.mult))
                step(V.tensor_tensor(out=idx[:, 1, own], in0=idx[:, 0, own], in1=ids[:, own], op=ALU.add))
                V.tensor_scalar(idx[:, 2, own], idx[:, 1, own], 0.0, float(size - 1), ALU.max, ALU.min).then_inc(idx_set, 1)
            dve.wait_ge(ld_tokc, 48)
            for g in range(1, NG):
                dve.wait_ge(ld_w[g], 16)
                for j in range(NJ):
                    if g == 1:
                        dve.wait_ge(fold0, j + 1)
                    else:
                        dve.wait_ge(folded, NJ * (g - 2) + j + 1)
                    V.scalar_tensor_tensor(out=weff[:, j, 0:C], in0=wt[:, g, j, :], scalar=gb[:, 0, g, j:j + 1],
                                           in1=weff[:, j, 0:C], op0=ALU.mult, op1=ALU.add).then_inc(folded, 1)
            dve.wait_ge(ld_const, 32)
            dve.wait_ge(gathered, 32 * TT)
            for P, b in ((128, slice(0, TT - 1)), (ROWS[-1], slice(TT - 1, TT))):
                step(V.tensor_tensor(out=seg[0:P, b], in0=seg[0:P, b], in1=pos[0:P, b], op=ALU.add))
                t = slice(IT + b.start, IT + b.stop)
                V.tensor_tensor(out=H[0:P, t, :], in0=H[0:P, t, :], in1=seg[0:P, b], op=ALU.add).then_inc(text_h, 1)
            layernorm(CHUNK[1:], H, lambda t: dve.wait_ge(text_h, 2), xn_ready[0])
            dve.wait_ge(tok_ps, 2)
            step(V.tensor_scalar(tst[:, 0, :], PS[:, 0:IT, C], 1.0 / PDIM, None, ALU.mult))
            step(V.tensor_tensor(out=tst[:, 1, :], in0=tst[:, 0, :], in1=tst[:, 0, :], op=ALU.mult))
            step(V.scalar_tensor_tensor(out=tst[:, 2, :], in0=PS[:, 5, C:C + IT], scalar=1.0 / PDIM, in1=tst[:, 1, :],
                                        op0=ALU.mult, op1=ALU.subtract))
            V.tensor_scalar(rstd[:, 0, 0:IT], tst[:, 2, :], EPS, None, ALU.add).then_inc(var_in, 1)
            norms[0] += 1
            dve.wait_ge(rs_out, norms[0])
            step(V.scalar_tensor_tensor(out=tst[:, 4, :], in0=tst[:, 0, :], scalar=-1.0, in1=rstd[:, 1, 0:IT],
                                        op0=ALU.mult, op1=ALU.mult))
            dve.wait_ge(sg_sb, 1)
            for t in range(IT):
                step(V.scalar_tensor_tensor(out=H[:, t, :], in0=PS[:, t, 0:C], scalar=rstd[:, 1, t:t + 1],
                                            in1=sgbw[:, C:2 * C], op0=ALU.mult, op1=ALU.add))
                V.scalar_tensor_tensor(out=H[:, t, :], in0=sgbw[:, 0:C], scalar=tst[:, 4, t:t + 1],
                                       in1=H[:, t, :], op0=ALU.mult, op1=ALU.add).then_inc(tok_h, 1)

            layernorm(CHUNK[:1], H, lambda t: dve.wait_ge(tok_h, t + 1), xn_ready[0])

            def norm_rows(n):
                (off, N, _), s, h = QK[n]
                dve.wait_ge(nm_ps, n + 1)
                V.tensor_copy(qkaug[s][HC:HC + 6, h, off:off + N], PS[HC:HC + 6, 2 + n % 2, 0:N]).then_inc(nm_out, 1)
            for n, ((off, N, _), s, h) in enumerate(QK):
                dve.wait_ge(qk_ps, n + 1)
                V.tensor_copy(qkaug[s][0:HC, h, off:off + N], PS[0:HC, n % 2, 0:N]).then_inc(qk_aug, 1)
                if n >= 1:
                    norm_rows(n - 1)
            norm_rows(len(QK) - 1)

            dve.wait_ge(kv_zero, 1)
            for n in range(2 * B):
                b, y = n // 2, n % 2
                dve.wait_ge(kv_ps, n + 1)
                src = PS[:, 4 + y, 0:3 * 4 * PAIR].rearrange("p (r e) -> p r e", r=3)
                for rows, c0 in ((slice(0, 64), 0), (slice(64, 128), 17)):
                    V.tensor_copy(kv[rows, b, 3 * y:3 * y + 3, c0:c0 + 17], src[rows, :, c0:c0 + 17]).then_inc(kv_out, 1)

            def divide0(n):
                P = BROWS[n]
                dve.wait_ge(o0_ps, n + 1)
                o = PS[0:P, n % 2, 0:NH * 17].rearrange("p (h e) -> p h e", h=NH)
                step(V.tensor_scalar(rec[0:P, 0, :], o[:, :, DH], float(M) * 1e-6, None, ALU.add))
                step(V.reciprocal(rec[0:P, 1, :], rec[0:P, 0, :]))
                V.tensor_tensor(out=att0b[0:P, n, :].rearrange("p (h e) -> p h e", h=NH), in0=o[:, :, 0:DH],
                                in1=rec[0:P, 1, :].unsqueeze(2).broadcast_to([P, NH, DH]), op=ALU.mult).then_inc(att0, 1)

            def projected0(t):
                P = ROWS[t]
                dve.wait_ge(y0_ps, t + 1)
                V.tensor_tensor(out=xn[0:P, t, :], in0=PS[0:P, 2 + t % 2, 0:C], in1=xn[0:P, t, :], op=ALU.add).then_inc(y0_out, 1)

            def affine(tiles):
                P, ts = ROWS[tiles[0]], slice(tiles[0], tiles[0] + len(tiles))
                dve.wait_ge(yn, tiles[-1] + 1)
                step(V.tensor_tensor(out=xn[0:P, ts, :], in0=xn[0:P, ts, :],
                                     in1=rows3[0:P, 1, :].unsqueeze(1).broadcast_to([P, len(tiles), C]), op=ALU.mult))
                for t in tiles:
                    V.tensor_tensor(out=H[0:P, t, :], in0=H[0:P, t, :], in1=xn[0:P, t, :], op=ALU.add).then_inc(h1, 1)

            def y_in(t):
                dve.wait_ge(y0_out, t + 1)

            def h_in(t):
                dve.wait_ge(h1, t + 1)

            dve.wait_ge(xnb, NT)
            dve.wait_ge(hb, NT)
            t, image_at = 0, None
            for n in range(NB):
                divide0(n)
                while t < NT and NEED[t] + 3 <= n:
                    projected0(t)
                    t += 1
                    image_at = n if t == IT else image_at
                if t >= IT:
                    tiles = CHUNK[0][2]
                    if n == image_at:
                        ln_stats(tiles, xn, y_in)
                    elif n == image_at + 1:
                        ln_scale(tiles, xn, yn)
                        affine(tiles)
                    elif n == image_at + 2:
                        ln_stats(tiles, H, h_in)
                    elif n == image_at + 3:
                        ln_scale(tiles, H, xn_ready[1])
            while t < NT:
                projected0(t)
                t += 1
            layernorm(CHUNK[1:], xn, y_in, yn, affine)

            def bc(ap):
                return ap.unsqueeze(2).broadcast_to([128, NT, NE])

            def route_softmax(k):
                dve.wait_ge(lg_ps[k], 1)
                dve.wait_ge(lg_set, 1)
                dve.wait_ge(ld_moe, 48)
                step(V.tensor_copy(lg[:, 0:NT - 1, :], PS[:, 4, 0:(NT - 1) * NE].rearrange("p (t e) -> p t e", t=NT - 1)))
                step(V.tensor_copy(lg[0:ROWS[-1], NT - 1, :], PS[0:ROWS[-1], 4, (NT - 1) * NE:NT * NE]))
                step(V.tensor_reduce(out=rs[:, 0, :], in_=lg[:], axis=AX, op=ALU.max))
                V.tensor_tensor(out=rt[:, 0], in0=lg[:], in1=bc(rs[:, 0, :]), op=ALU.subtract).then_inc(rt_in[k], 1)
                dve.wait_ge(rt_exp[k], 1)
                step(V.tensor_reduce(out=rs[:, 1, :], in_=rt[:, 0], axis=AX, op=ALU.add))
                step(V.reciprocal(rs[:, 2, :], rs[:, 1, :]))
                if k == 0:
                    V.tensor_tensor(out=rt[:, 1], in0=rt[:, 0], in1=bc(rs[:, 2, :]), op=ALU.mult).then_inc(imp_in, 1)
                    dve.wait_ge(imp_in, 1)
                else:
                    step(V.tensor_tensor(out=rt[:, 1], in0=rt[:, 0], in1=bc(rs[:, 2, :]), op=ALU.mult))

            def route_pick(k):
                rk = rank[:].unsqueeze(1).broadcast_to([128, NT, NE])
                for pick, src in ((2, 1), (3, 0)):
                    step(V.tensor_reduce(out=rs[:, 3, :], in_=rt[:, src], axis=AX, op=ALU.max))
                    step(V.tensor_tensor(out=rt[:, 4], in0=rt[:, src], in1=bc(rs[:, 3, :]), op=ALU.is_equal))
                    step(V.tensor_tensor(out=rt[:, 5], in0=rt[:, 4], in1=rk, op=ALU.mult))
                    step(V.tensor_reduce(out=rs[:, 4, :], in_=rt[:, 5], axis=AX, op=ALU.max))
                    step(V.tensor_tensor(out=rt[:, pick], in0=rk, in1=bc(rs[:, 4, :]), op=ALU.is_equal))
                    if pick == 2:
                        step(V.scalar_tensor_tensor(out=rt[:, 0], in0=rt[:, 2], scalar=-2.0, in1=rt[:, 1],
                                                    op0=ALU.mult, op1=ALU.add))
                V.tensor_tensor(out=rt[:, 4], in0=rt[:, 2], in1=rt[:, 3], op=ALU.add).then_inc(sel_in[k], 1)
                dve.wait_ge(sel_in[k], 1)

            def by_expert(ap):
                return ap.rearrange("p (e t) -> p e t", e=NE)

            def route_place(k):
                dve.wait_ge(rank_ps[k], 1)
                step(V.tensor_copy(by_expert(cnt[:, 0, :]), PS[:, 7, NE * NT:2 * NE * NT].rearrange("p (t e) -> p e t", t=NT)))
                step(V.tensor_tensor_scan(cnt[:, 1, :], routec[:, 0:NE * NT], cnt[:, 0, :], 0.0, ALU.mult, ALU.add))
                total = by_expert(cnt[:, 1, :])[:, :, NT - 1]
                c0 = NE * NT + NE
                steps_m = rt[:, 5].rearrange("p t e -> p (t e)")[:, 0:NE * MAXT].rearrange("p (e m) -> p e m", e=NE)
                step(V.tensor_tensor(out=steps_m, in0=total.unsqueeze(2).broadcast_to([128, NE, MAXT]),
                                     in1=routec[:, c0:c0 + NE * MAXT].rearrange("p (e m) -> p e m", e=NE), op=ALU.is_gt))
                step(V.tensor_reduce(out=tiles_of[:, 0, :], in_=steps_m, axis=AX, op=ALU.add))
                step(V.tensor_tensor_scan(tiles_of[:, 1, :], routec[:, NE * NT:c0], tiles_of[:, 0, :], 0.0, ALU.mult, ALU.add))
                step(V.tensor_tensor(out=tiles_of[:, 2, :], in0=tiles_of[:, 1, :], in1=tiles_of[:, 0, :], op=ALU.subtract))
                step(V.tensor_tensor(out=cnt[:, 2, :], in0=cnt[:, 1, :], in1=cnt[:, 0, :], op=ALU.subtract))
                step(V.scalar_tensor_tensor(out=by_expert(cnt[:, 3, :]), in0=tiles_of[:, 2, :].unsqueeze(2).broadcast_to([128, NE, NT]),
                                            scalar=float(CAP), in1=by_expert(cnt[:, 2, :]), op0=ALU.mult, op1=ALU.add))
                step(V.tensor_tensor(out=rt[:, 0], in0=PS[:, 7, 0:NE * NT].rearrange("p (t e) -> p t e", t=NT),
                                     in1=cnt[:, 3, :].rearrange("p (e t) -> p t e", e=NE), op=ALU.add))
                for c in range(2):
                    step(V.tensor_tensor(out=rt[:, 5], in0=rt[:, 0], in1=rt[:, 2 + c], op=ALU.mult))
                    step(V.tensor_reduce(out=rs[:, 3 + c, :], in_=rt[:, 5], axis=AX, op=ALU.add))
                    V.tensor_copy(place[:, c, :], rs[:, 3 + c, :]).then_inc(placed[k], 1)
                step(V.tensor_tensor(out=eidf[:], in0=routec[0:1, c0 + NE * MAXT:c0 + NE * MAXT + NSLOT].unsqueeze(2).broadcast_to([1, NSLOT, NE]),
                                     in1=tiles_of[0:1, 1, :].unsqueeze(1).broadcast_to([1, NSLOT, NE]), op=ALU.is_ge))
                step(V.tensor_reduce(out=eids[:], in_=eidf[:], axis=AX, op=ALU.add))
                V.tensor_scalar(eid[:], eids[:], float(NE - 1), None, ALU.min).then_inc(placed[k], 1)

            def number_rows(k):
                V.tensor_copy(xnd[:, :, C], token).then_inc(rows_set[k], 1)

            def second_rows(k, half):
                ts = (slice(0, SENT_A), slice(SENT_A, NT))[half]
                dve.wait_ge((sent_a, sent_b)[half][k], 16 * (ts.stop - ts.start))
                V.tensor_scalar(xnd[:, ts, C], token[:, ts], float(CHOICE), None, ALU.add).then_inc(rows_set[k], 1)

            def route_weights(k):
                if k == 0:
                    dve.wait_ge(imp_ps, 1)
                    V.tensor_reduce(out=run[:, 0, :], in_=PS[:, 5, 0:NT * NE].rearrange("p (t e) -> p e t", t=NT),
                                    axis=AX, op=ALU.add).then_inc(imp_read, 1)
                    dve.wait_ge(imp_read, 1)
                    step(V.tensor_scalar(run[:, 1, :], run[:, 0, :], 1.0, 0.1, ALU.subtract, ALU.mult))
                    step(V.tensor_scalar(run[:, 2, :], run[:, 1, :], 1.0, 0.01, ALU.add, ALU.add))
                    step(V.reciprocal(run[:, 0, :], run[:, 2, :]))
                    step(V.tensor_tensor(out=rt[:, 1], in0=rt[:, 1], in1=run[:, 0, :].unsqueeze(1).broadcast_to([128, NT, NE]),
                                         op=ALU.mult))
                for c in range(2):
                    step(V.tensor_tensor(out=rt[:, 5], in0=rt[:, 1], in1=rt[:, 2 + c], op=ALU.mult))
                    step(V.tensor_reduce(out=cw[:, c, :], in_=rt[:, 5], axis=AX, op=ALU.add))
                step(V.tensor_tensor(out=cw[:, 2, :], in0=cw[:, 0, :], in1=cw[:, 1, :], op=ALU.add))
                if k == 1:
                    step(V.tensor_scalar(cw[:, 2, :], cw[:, 2, :], 1e-20, None, ALU.add))
                step(V.reciprocal(rs[:, 5, :], cw[:, 2, :]))
                for c in range(2):
                    step(V.tensor_tensor(out=cw[:, c, :], in0=cw[:, c, :], in1=rs[:, 5, :], op=ALU.mult))

            def gate(k, j, z):
                dve.wait_ge(up_act[k], j + 1)
                V.tensor_tensor(out=hact[:, z, :], in0=hact[:, z, :], in1=PS[:, 2 * z + 1, :], op=ALU.mult).then_inc(up_sb[k], 1)

            def turned_hidden(k, j, z):
                dve.wait_ge(ht_ps[k], j + 1)
                if not isinstance(j, int) or j >= 2:
                    dve.wait_ge(dn_ps[k], j - 1)
                V.tensor_copy(hT[:, z].rearrange("p i n -> p (i n)"), PS[:, 4 + z, :]).then_inc(ht_sb[k], 1)

            def slots(k):
                for s in range(-1, 2):
                    if k == 1:
                        gate(k, s + 1, (s + 1) % 2)
                    if s >= 0:
                        turned_hidden(k, s, s % 2)
                with dve.Fori(0, PAIRS) as i:
                    for z in range(2):
                        s = PIPE0 + 2 * i + z
                        if k == 1:
                            gate(k, s + 1, 1 - z)
                        turned_hidden(k, s, z)
                for s in range(PIPE0 + 2 * PAIRS, NSLOT):
                    if k == 1 and s + 1 <= LAST:
                        gate(k, s + 1, (s + 1) % 2)
                    turned_hidden(k, s, s % 2)

            def combine(k, t):
                P = ROWS[t]
                dve.wait_ge(back[k][t], 16)
                for c in range(2):
                    V.scalar_tensor_tensor(out=H[0:P, t, :], in0=yback[0:P, c, t, :], scalar=cw[0:P, c, t:t + 1],
                                           in1=H[0:P, t, :], op0=ALU.mult, op1=ALU.add).then_inc(added[k], 1)
                    dve.wait_ge(added[k], 2 * t + c + 1)

            layernorm(CHUNK[1:], H, h_in, xn_ready[1])
            dve.wait_ge(ld_moe, 48)
            number_rows(0)
            route_softmax(0)
            route_pick(0)
            route_place(0)
            route_weights(0)
            second_rows(0, 0)
            second_rows(0, 1)
            slots(0)

            layernorm(CHUNK, H, lambda t: combine(0, t), xn_ready[2])
            dve.wait_ge(ld_a1, 64)
            for c, (off, N, _) in enumerate(CHUNK1):
                for h in range(2):
                    dve.wait_ge(q1_ps, 4 * c + 2 + h + 1)
                    bs, ks = (slice(0, B), slice(0, NP_)) if c == 0 else (slice(4 * c - 4, 4 * c), slice(NP_, NK))
                    dst = kT1[:, h, :].rearrange("p (b n) -> p b n", b=B)[:, bs, ks]
                    V.tensor_copy(dst, PS[0:HC, 2 + h, 0:N].rearrange("p (b n) -> p b n", n=ks.stop - ks.start)).then_inc(q1_dve, 1)

            def scores_out(u):
                P, parts, w = (128, 1, NP_) if u < IMG_UNITS else (NS, 2, NK)
                dve.wait_ge(s_ps, u + 1)
                b0 = 2 * (u % 2)
                src = PS[0:P, b0:b0 + 2, 0:2 * w].rearrange("p a (h e) -> p a h e", e=w)
                if u >= 2:
                    dve.wait_ge(s_sub, parts_by(u - 2))
                m = mx[0:P, u % 2].rearrange("p (a h) -> p a h", a=2)
                step(V.tensor_reduce(out=m, in_=src, axis=AX, op=ALU.max))
                if u >= 3:
                    dve.wait_ge(t_ps, u - 2)
                for c0, k0, n in ((0, 0, NP_), (4 * NP_, NP_, NS))[0:parts]:
                    V.tensor_tensor(out=sx[0:P, u % 3, c0:c0 + 4 * n].rearrange("p (a h e) -> p a h e", a=2, e=n),
                                    in0=src[:, :, :, k0:k0 + n], in1=m.unsqueeze(3).broadcast_to([P, 2, 2, n]),
                                    op=ALU.subtract).then_inc(s_sub, 1)

            def divide(u):
                t, b, v = UNITS[u]
                dve.wait_ge(o1_ps, u + 1)
                P, tile = (128, t) if t is not None else (NS, IT + b)
                o = PS[0:P, 6 + u % 2, 0:4 * 17].rearrange("p (y z e) -> p y z e", y=2, z=2)
                r = rec[0:P, u % 2, 0:4].rearrange("p (y z) -> p y z", y=2)
                if u >= 2:
                    dve.wait_ge(att1, u - 1)
                step(V.reciprocal(r, o[:, :, :, DH]))
                dst = att1b[0:P, tile, 64 * v:64 * v + 64].rearrange("p (y z e) -> p y z e", y=2, z=2)
                V.tensor_tensor(out=dst, in0=o[:, :, :, 0:DH], in1=r.unsqueeze(3).broadcast_to([P, 2, 2, DH]),
                                op=ALU.mult).then_inc(att1, 1)

            for u in range(AFTER_UNITS + 3):
                if u < AFTER_UNITS:
                    scores_out(u)
                if u >= 3:
                    divide(u - 3)
            for n, t in enumerate(TILES):
                P = ROWS[t]
                dve.wait_ge(y1_ps, n + 1)
                V.tensor_tensor(out=H[0:P, t, :], in0=PS[0:P, n % 2, 0:C], in1=H[0:P, t, :], op=ALU.add).then_inc(h3, 1)
            layernorm(CHUNK, H, lambda t: dve.wait_ge(h3, t + 1), xn_ready[3])

            def gate_shared(s):
                N = CHUNK[s][1]
                for n in range(HT * s, HT * s + HT):
                    dve.wait_ge(u_act, n + 1)
                    V.tensor_tensor(out=shT[:, s, n % HT, 0:N], in0=sa[:, n % 2, 0:N], in1=PS[:, 2 * (n % 2) + 1, 0:N],
                                    op=ALU.mult).then_inc(g_out, 1)

            def add_shared(s):
                for t in CHUNK[s][2]:
                    P = ROWS[t]
                    dve.wait_ge(ysh_ps, t + 1)
                    V.tensor_tensor(out=H[0:P, t, :], in0=PS[0:P, 4 + t % 2, 0:C], in1=H[0:P, t, :], op=ALU.add).then_inc(ysh_acc, 1)

            number_rows(1)
            route_softmax(1)
            route_pick(1)
            gate_shared(0)
            route_place(1)
            gate_shared(1)
            second_rows(1, 0)
            route_weights(1)
            second_rows(1, 1)
            add_shared(0)
            gate_shared(2)
            add_shared(1)
            add_shared(2)
            slots(1)
            for t in TILES:
                combine(1, t)

        @block.tensor
        def _(pe):
            mm = nc.tensor.matmul

            def turn(n, t, src, rows=None):
                if n >= 2:
                    pe.wait_ge(tp_out, n - 1)
                P = rows or ROWS[t]
                for h in range(2):
                    last = nc.tensor.transpose(PS[0:HC, 6 + n % 2, 128 * h:128 * h + P], src[0:P, t, h * HC:(h + 1) * HC],
                                               ident[0:P, 0:P])
                last.then_inc(tp_ps, 1)

            pe.wait_ge(ld_tokc, 48)
            pe.wait_ge(x2_done, 1)
            for t in range(IT):
                for j in range(NJ):
                    last = mm(PS[:, 5, C + t:C + t + 1], x2[:, j, 128 * t:128 * t + 128], mult[:, j:j + 1],
                              start=(j == 0), stop=(j == NJ - 1))
            last.then_inc(tok_ps, 1)
            pe.wait_ge(ld_x, 16)
            pe.wait_ge(mult_set, 1)
            for j in range(NJ):
                pe.wait_ge(folded, NJ * (NG - 2) + j + 1)
                for t in range(IT):
                    last = mm(PS[:, t, 0:C + 1], xT[:, j, 128 * t:128 * t + 128], weff[:, j, :], start=(j == 0), stop=(j == NJ - 1))
            last.then_inc(tok_ps, 1)
            pe.wait_ge(ones_set, 1)
            for j in range(NJ):
                mm(PS[:, 4, 0:C], ones[0:KP, :], weff[:, j, 0:C], start=(j == 0), stop=(j == NJ - 1))
            pe.wait_ge(beta_sum, 1)
            for j in range(NJ):
                mm(PS[:, 4, C:2 * C], ones[0:KP, :], betaw[:, 0, j, :], start=(j == 0), stop=False)
            mm(PS[:, 4, C:2 * C], ones[0:1, :], tokb[:], start=False, stop=True).then_inc(tok_ps, 1)

            pe.wait_ge(ld_const, 32)
            for n, t in enumerate(TILES_TF):
                pe.wait_ge(xn_ready[0], n + 1)
                turn(TP_XN0 + n, t, xn)

            pe.wait_ge(ld_a0, 80)
            pe.wait_ge(tok_h, IT)

            def norms(n):
                (off, N, _), s, h = QK[n]
                pe.wait_ge(qk_sq, n + 1)
                if n >= 2:
                    pe.wait_ge(nm_out, n - 1)
                mm(PS[HC:HC + 6, 2 + n % 2, 0:N], nb6[:], sq[:, n % 2, 0:N], start=True, stop=True).then_inc(nm_ps, 1)
            for n, ((off, N, _), s, h) in enumerate(QK):
                pe.wait_ge(tp_out, TP_XN0 + (4, 5, 9)[n // 4])
                if n >= 2:
                    pe.wait_ge(qk_aug, n - 1)
                for c in range(2):
                    last = mm(PS[0:HC, n % 2, 0:N], wqkv[:, c, s * C + h * HC:s * C + (h + 1) * HC], xnT[:, c, off:off + N],
                              start=(c == 0), stop=(c == 1))
                last.then_inc(qk_ps, 1)
                if n >= 1:
                    norms(n - 1)
            norms(len(QK) - 1)
            for n, t in enumerate(BTILES):
                if n >= 2:
                    pe.wait_ge(v_out, n - 1)
                for c in range(2):
                    last = mm(PS[0:BROWS[t], 4 + n % 2, 0:C], xnT[:, c, BOFF[t]:BOFF[t] + BROWS[t]], wqkv[:, c, 2 * C:3 * C],
                              start=(c == 0), stop=(c == 1))
                last.then_inc(v_ps, 1)
            pe.wait_ge(nm_out, len(QK))
            for n, (kind, r) in enumerate(PHI):
                b0 = 2 * (n % 2)
                if n >= 2:
                    pe.wait_ge(ph_out, n - 1)
                for u in range(2):
                    if kind == "k":
                        last = mm(PS[0:BROWS[r], b0 + u, 0:384], qkaug[1][:, u, BOFF[r]:BOFF[r] + BROWS[r]], bd[:], start=True, stop=True)
                    elif kind == "qt":
                        off, N = IT * 128 + 4 * NS * u, 4 * NS
                        last = mm(PS[:, b0 + u, 0:N], bd[:, (r % 3) * 128:(r % 3) * 128 + 128], qkaug[0][:, r // 3, off:off + N],
                                  start=True, stop=True)
                    else:
                        r2 = 2 * r + u
                        last = mm(PS[:, b0 + u, :], bd[:, (r2 % 3) * 128:(r2 % 3) * 128 + 128], qkaug[0][:, r2 // 3, 0:512],
                                  start=True, stop=True)
                last.then_inc(ph_ps, 1)
            pe.wait_ge(v_out, NB)
            pe.wait_ge(ph_out, NB)
            for n in range(2 * B):
                b, y = n // 2, n % 2
                if n >= 2:
                    pe.wait_ge(kv_out, 2 * (n - 1))
                p0 = 64 * (b % 2)
                for r in range(3):
                    o, f, h = PS[:, 4 + y, 3 * PAIR * r:3 * PAIR * (r + 1)], (3 * y + r) * 128, 6 * y
                    mm(o, kp[p0:p0 + 64, b // 2, f:f + 128], v0[p0:p0 + 64, b // 2, h:h + 6, :], start=True, stop=False)
                    last = mm(o, kp[0:NS, IT + b, f:f + 128], v0[0:NS, IT + b, h:h + 6, :], start=False, stop=True)
                last.then_inc(kv_ps, 1)
            pe.wait_ge(ph_out, len(PHI))
            def products(n):
                t = n
                pe.wait_ge(kv_out, 4 * (2 * t + 2) if t < IT else 4 * (t - IT + 1))
                if n >= 2:
                    pe.wait_ge(att0, n - 1)
                parts = [(0, 64, 2 * t, BOFF[t]), (64, 64, 2 * t + 1, BOFF[t] + 64)] if t < IT else [(0, NS, t - IT, BOFF[t])]
                for p0, P, b, off in parts:
                    for r in range(6):
                        last = mm(PS[p0:p0 + P, n % 2, r * PAIR:(r + 1) * PAIR], qp[:, r, off:off + P], kv[:, b, r, :],
                                  start=True, stop=True)
                last.then_inc(o0_ps, 1)

            def project0(t):
                P = ROWS[t]
                pe.wait_ge(tp_out, TP_ATT0 + NEED[t])
                if t >= 2:
                    pe.wait_ge(y0_out, t - 1)
                for c in range(2):
                    last = mm(PS[0:P, 2 + t % 2, 0:C], attT0[:, c, OFF[t]:OFF[t] + P], wproj0[:, c, :], start=(c == 0), stop=(c == 1))
                last.then_inc(y0_ps, 1)

            def turn_and_project(base, src, project):
                t = 0
                for b in range(NB):
                    turn(base + b, b, src, BROWS[b])
                    while t < NT and NEED[t] < b + 1:
                        project(t)
                        t += 1
                while t < NT:
                    project(t)
                    t += 1
            t = 0
            for n in range(NB + 2):
                if n < NB:
                    products(n)
                if n >= 2:
                    pe.wait_ge(att0, n - 1)
                    turn(TP_ATT0 + n - 2, n - 2, att0b, BROWS[n - 2])
                    while t < NT and NEED[t] + 2 <= n:
                        project0(t)
                        t += 1
            while t < NT:
                project0(t)
                t += 1

            def logits(k, base):
                def route(t):
                    pe.wait_ge(tp_out, base + t + 1)
                    for c in range(2):
                        last = mm(PS[0:ROWS[t], 4, t * NE:(t + 1) * NE], xnT[:, c, OFF[t]:OFF[t] + ROWS[t]], rw[:, k, c, :],
                                  start=(c == 0), stop=(c == 1))
                    if t == NT - 1:
                        last.then_inc(lg_ps[k], 1)
                pe.wait_ge(ld_moe, 48)
                for t in TILES:
                    pe.wait_ge(xn_ready[1 + 2 * k], t + 1)
                    turn(base + t, t, xn)
                    if t >= 1:
                        route(t - 1)
                route(NT - 1)

            def summed(bank, col, rows, src, last_sem):
                P, m = ROWS[-1], (NT - 1) * NE
                mm(PS[:, bank, col:col + m], rows, src[:, 0:NT - 1, :], start=True, stop=True)
                last = mm(PS[:, bank, col + m:col + NT * NE], rows[0:P, :], src[0:P, NT - 1, :], start=True, stop=True)
                if last_sem is not None:
                    last.then_inc(last_sem, 1)

            def ranks(k):
                pe.wait_ge(sel_in[k], 1)
                summed(7, 0, tri, rt[:, 4], None)
                summed(7, NE * NT, ones[:], rt[:, 4], rank_ps[k])

            def expert(j):
                return pe.value_load(eid[0:1, bass.ds(j, 1)], min_val=0, max_val=NE - 1)

            def turn_rows(k, j, z, round_):
                pe.wait_ge(xs_in[k][z], 16 * round_ + 16)
                if not isinstance(j, int) or j >= 1:
                    pe.wait_ge(xt_sb[k], j)
                for c in range(2):
                    last = nc.tensor.transpose(PS[0:HC, 6, 128 * c:128 * c + 128], xs[:, z, c * HC:(c + 1) * HC], ident[:])
                last.then_inc(xt_ps[k], 1)

            def up(k, j, z):
                pe.wait_ge(xt_sb[k], j + 1)
                if not isinstance(j, int) or j >= 2:
                    pe.wait_ge((up_act, up_sb)[k][k], j - 1)
                e = expert(j)
                for q in range(1 + k):
                    bank = 2 * z + q if k else z
                    for c in range(2):
                        w = arena[0:HC, bass.ds(e * ES[k] + (WBASE[k] + (2 * q + c) * HID), HID)]
                        last = mm(PS[:, bank, :], xsT[:, z, c, :], w, start=(c == 0), stop=(c == 1))
                last.then_inc(up_ps[k], 1)

            def turn_hidden(k, j, z):
                pe.wait_ge((up_act, up_sb)[k][k], j + 1)
                if not isinstance(j, int) or j >= 2:
                    pe.wait_ge(ht_sb[k], j - 1)
                for it in range(HT):
                    last = nc.tensor.transpose(PS[:, 4 + z, 128 * it:128 * it + 128], hact[:, z, 128 * it:128 * it + 128], ident[:])
                last.then_inc(ht_ps[k], 1)

            def down(k, j, z):
                pe.wait_ge(ht_sb[k], j + 1)
                if not isinstance(j, int) or j >= 1:
                    pe.wait_ge(dn_sb[k], j)
                e = expert(j)
                for it in range(HT):
                    w = arena[:, bass.ds(e * ES[k] + (WBASE[k] + 2 * HID * (1 + k) + it * C), C)]
                    last = mm(PS[:, 7, 0:C], hT[:, z, it, :], w, start=(it == 0), stop=(it == HT - 1))
                last.then_inc(dn_ps[k], 1)

            def slots(k):
                pe.wait_ge(placed[k], 3)
                turn_rows(k, 0, 0, 0)
                pe.wait_ge(ld_e[k], 32 * NE)
                up(k, 0, 0)
                turn_rows(k, 1, 1, 0)
                up(k, 1, 1)
                turn_rows(k, 2, 0, 1)
                turn_hidden(k, 0, 0)
                up(k, 2, 0)
                turn_rows(k, 3, 1, 1)
                down(k, 0, 0)
                turn_hidden(k, 1, 1)
                with pe.Fori(0, PAIRS) as i:
                    for z in range(2):
                        s = PIPE0 + 2 * i + z
                        up(k, s + 1, 1 - z)
                        turn_rows(k, s + 2, z, i + 2)
                        down(k, s - 1, 1 - z)
                        turn_hidden(k, s, z)
                for s in range(PIPE0 + 2 * PAIRS, NSLOT + 1):
                    if s + 1 <= LAST:
                        up(k, s + 1, (s + 1) % 2)
                    if s + 2 <= LAST:
                        turn_rows(k, s + 2, s % 2, (s + 2) // 2)
                    down(k, s - 1, (s - 1) % 2)
                    if s <= LAST:
                        turn_hidden(k, s, s % 2)

            logits(0, TP_XN1)
            pe.wait_ge(imp_in, 1)
            summed(5, 0, ones[:], rt[:, 1], imp_ps)
            ranks(0)
            pe.wait_ge(imp_read, 1)
            slots(0)

            for t in TILES:
                pe.wait_ge(xn_ready[2], t + 1)
                turn(TP_XN2 + t, t, xn)
            pe.wait_ge(ld_a1, 64)
            n = 0
            for ci, (off, N, need) in enumerate(CHUNK1):
                pe.wait_ge(tp_out, TP_XN2 + need)
                for s in range(2):
                    for h in range(2):
                        if ci >= 1:
                            if s == 0:
                                pe.wait_ge(q1_act, 2 * (ci - 1) + h + 1)
                            else:
                                pe.wait_ge(q1_dve, 2 * (ci - 1) + h + 1)
                        for c in range(2):
                            last = mm(PS[0:HC, n % 4, 0:N], wat[:, c, s * C + h * HC:s * C + (h + 1) * HC], xnT[:, c, off:off + N],
                                      start=(c == 0), stop=(c == 1))
                        last.then_inc(q1_ps, 1)
                        n += 1
            for n in range(2 * B):
                if n >= 2:
                    pe.wait_ge(v1_out, 2 * (n - 1) if n - 2 < B else B + n - 1)
                else:
                    pe.wait_ge(ht_sb[0], NSLOT)
                b, bank = n % B, PS[:, 4 + n % 2, :]
                parts = [(0, 64 * b, 64, 0, HC), (64, 64 * b, 64, HC, HC)] if n < B else [(0, BOFF[IT + b], NS, 0, C)]
                for p0, off, w, c0, N in parts:
                    for c in range(2):
                        last = mm(bank[p0:p0 + w, 0:N], xnT[:, c, off:off + w], wat[:, c, 2 * C + c0:2 * C + c0 + N],
                                  start=(c == 0), stop=(c == 1))
                last.then_inc(v1_ps, 1)

            def score(u, p0, P, x, qoff, k0, w):
                return mm(PS[p0:p0 + P, 2 * (u % 2) + x // 2, (x % 2) * w:(x % 2) * w + w], qT1[:, (2 * UNITS[u][2] + x // 2) // 3, qoff:qoff + P],
                          kown[:, u % 3, x, k0:k0 + w], start=False, stop=True, skip_group_check=True)

            def scores(u):
                t, b, v = UNITS[u]
                b0 = 2 * (u % 2)
                if u >= 2:
                    pe.wait_ge(s_sub, parts_by(u - 2))
                P, c0, w, m0, n = (128, 0, NP_, 0, NP_) if t is not None else (NS, NP_, NK, NP_, NS)
                for a in range(2):
                    mm(PS[0:P, b0 + a, 0:2 * w].rearrange("p (h e) -> p h e", h=2)[:, :, c0:], identb[0:P, 0:P],
                       cmask[0:P, m0:m0 + n].unsqueeze(1).broadcast_to([P, 2, n]), start=True, stop=False, skip_group_check=True)
                pe.wait_ge(own_set, 2 * u + 2)
                for x in range(4):
                    if t is not None:
                        for k in range(2):
                            last = score(u, 64 * k, 64, x, BOFF[t] + 64 * k, NP_ * k, NP_)
                    else:
                        last = score(u, 0, NS, x, BOFF[IT + b], 0, NK)
                last.then_inc(s_ps, 1)

            def turn_probs(u):
                pe.wait_ge(s_exp, u + 1)
                if u >= 2:
                    pe.wait_ge(t_act, parts_by(u - 2))
                bank = PS[:, 4 + u % 2, :]
                if u < IMG_UNITS:
                    for y in range(2):
                        last = nc.tensor.transpose(bank[:, 128 * y:128 * y + 128], sx[:, u % 3, 128 * y:128 * y + 128], ident[:])
                else:
                    for y in range(2):
                        nc.tensor.transpose(bank[:, NS * y:NS * y + NS], sx[0:NS, u % 3, 2 * NP_ * y:2 * NP_ * (y + 1)], ident[0:NS, 0:NS])
                    for x in range(4):
                        c0, k0 = NS * (2 + x), 4 * NP_ + NS * x
                        last = nc.tensor.transpose(bank[0:NS, c0:c0 + NS], sx[0:NS, u % 3, k0:k0 + NS], ident[0:NS, 0:NS])
                last.then_inc(t_ps, 1)

            def weigh(u):
                t, b, v = UNITS[u]
                pe.wait_ge(t_act, parts_by(u))
                if u == 0:
                    pe.wait_ge(tp_out, TP_XN2 + NT)
                elif u >= 2:
                    pe.wait_ge(att1, u - 1)
                for y in range(2):
                    o = PS[:, 6 + u % 2, PAIR * y:PAIR * (y + 1)]
                    if t is not None:
                        for k in range(2):
                            c0 = 128 * y + 64 * k
                            last = mm(o[64 * k:64 * k + 64], pT[:, u % 2, c0:c0 + 64], vi[:, 2 * t + k, 2 * v + y, :], start=True, stop=True)
                    else:
                        mm(o[0:NS], pT[:, u % 2, NS * y:NS * y + NS], vi[:, b, 2 * v + y, :], start=True, stop=False,
                           skip_group_check=True)
                        for z in range(2):
                            c0 = NS * (2 + 2 * y + z)
                            last = mm(o[0:NS, 17 * z:17 * z + 17], pT[0:NS, u % 2, c0:c0 + NS], v1[0:NS, b, 4 * v + 2 * y + z, :],
                                      start=False, stop=True, skip_group_check=True)
                last.then_inc(o1_ps, 1)

            pe.wait_ge(masks_set, 2)
            pe.wait_ge(q1_act, 6)
            pe.wait_ge(v1_out, 3 * B)
            for u in range(AFTER_UNITS + 3):
                if u < AFTER_UNITS:
                    scores(u)
                if 2 <= u <= AFTER_UNITS + 1:
                    turn_probs(u - 2)
                if u >= 3:
                    weigh(u - 3)
            pe.wait_ge(att1, AFTER_UNITS)

            def project1(t):
                P = ROWS[t]
                pe.wait_ge(tp_out, TP_ATT1 + NEED[t])
                if t >= 2:
                    pe.wait_ge(h3, t - 1)
                for c in range(2):
                    last = mm(PS[0:P, t % 2, 0:C], attT1[:, c, OFF[t]:OFF[t] + P], wproj1[:, c, :], start=(c == 0), stop=(c == 1))
                last.then_inc(y1_ps, 1)
            turn_and_project(TP_ATT1, att1b, project1)

            def hidden_shared(s):
                off, N, _ = CHUNK[s]
                for n in range(HT * s, HT * s + HT):
                    if n >= 2:
                        pe.wait_ge(g_out, n - 1)
                    for q in range(2):
                        for c in range(2):
                            last = mm(PS[:, 2 * (n % 2) + q, 0:N], wsh1[q][:, c, (n % HT) * 128:(n % HT) * 128 + 128],
                                      xnT[:, c, off:off + N], start=(c == 0), stop=(c == 1))
                    last.then_inc(u_ps, 1)

            def out_shared(s):
                pe.wait_ge(g_out, HT * s + HT)
                for t in CHUNK[s][2]:
                    P, o = ROWS[t], OFF[t] - CHUNK[s][0]
                    if t >= 2:
                        pe.wait_ge(ysh_acc, t - 1)
                    for it in range(HT):
                        last = mm(PS[0:P, 4 + t % 2, 0:C], shT[:, s, it, o:o + P], wsh2[:, it, :], start=(it == 0), stop=(it == HT - 1))
                    last.then_inc(ysh_ps, 1)

            logits(1, TP_XN3)
            pe.wait_ge(ld_sh, 32)
            pe.wait_ge(h3, NT)
            hidden_shared(0)
            ranks(1)
            hidden_shared(1)
            out_shared(0)
            hidden_shared(2)
            out_shared(1)
            out_shared(2)
            pe.wait_ge(ysh_acc, NT)
            slots(1)


def arrange(x, x_txt, mask_BS_i2_0, L0_tok_gamma, L0_tok_beta, L0_tok_W, L0_tok_b, L0_txt_token_table, L0_txt_segm_table,
            L0_attn_W_qkv, L0_attn_W_proj, L0_attn_b_proj, L0_attn_gamma, L0_attn_beta, L0_attn_random_features,
            L0_ffn_router_w, L0_ffn_w1, L0_ffn_w2, L1_attn_W_attn, L1_attn_W_proj, L1_ffn_gate_w, L1_ffn_w1, L1_ffn_w2,
            L1_ffn_w3, L1_ffn_ws1, L1_ffn_ws2, L1_ffn_ws3):
    f = np.float32
    a = {}
    n = SIDE // PATCH
    xp = np.zeros((B, CH, SIDE + 2, SIDE + 2), f)
    xp[:, :, 1:-1, 1:-1] = x
    win = np.zeros((HALO, CH, HALO, B, n, n), f)
    for r in range(HALO):
        for q in range(HALO):
            win[r, :, q] = xp[:, :, r:r + PATCH * (n - 1) + 1:PATCH, q:q + PATCH * (n - 1) + 1:PATCH].transpose(1, 0, 2, 3)
    a["xT"] = win.reshape(HALO, CH, 2, NJ, B * n * n).transpose(2, 0, 1, 3, 4).reshape(KP, NJ, B * n * n)

    def by_pixel(w):
        w = np.asarray(w).reshape(PATCH, PATCH, NG, CH, -1)
        o = np.zeros((NG, HALO, CH, HALO, w.shape[-1]), w.dtype)
        for g, (dr, dq) in enumerate(((1, 1), (1, 0), (1, 2), (0, 1), (2, 1))):
            o[g, dr:dr + PATCH, :, dq:dq + PATCH] = w[:, :, g].transpose(0, 2, 1, 3)
        o = o.reshape(NG, HALO, CH, 2, NJ, -1).transpose(3, 1, 2, 0, 4, 5)
        return o.reshape(KP, NG, NJ, -1)
    a["wt"] = by_pixel(L0_tok_W)
    a["gb"] = np.stack([by_pixel(L0_tok_gamma)[..., 0], by_pixel(L0_tok_beta)[..., 0]], 1)
    a["mult"] = by_pixel(np.ones(PDIM, f))[..., 0].sum(1)
    a["tokb"] = L0_tok_b[None, :]
    a["ident"] = np.eye(128, dtype=f)
    p_, i_ = np.arange(NS, dtype=np.float64)[:, None], np.arange(C, dtype=np.float64)[None, :]
    ang = p_ / np.power(10000.0, np.floor(i_ / 2) * 2 / C)
    pos = np.where(np.arange(C) % 2 == 0, np.sin(ang), np.cos(ang)).astype(f)

    def in_tiles(v):
        o = np.zeros((TT * 128,) + v.shape[1:], v.dtype)
        o[:B * NS] = v
        return o.reshape((TT, 128) + v.shape[1:]).swapaxes(0, 1)
    a["pos"] = in_tiles(np.tile(pos, (B, 1)))
    a["ids"] = np.concatenate([in_tiles(v.reshape(-1)) for v in (x_txt, mask_BS_i2_0)], 1)
    a["table"] = L0_txt_token_table
    a["segt"] = L0_txt_segm_table

    def halves(w):
        return np.asarray(w).reshape(2, HC, -1).transpose(1, 0, 2)
    a["wqkv"] = halves(L0_attn_W_qkv)
    bd = np.zeros((HC + 6, 6 * M), f)
    nb = np.zeros((HC, 6), f)
    for h in range(6):
        bd[h * DH:(h + 1) * DH, h * M:(h + 1) * M] = L0_attn_random_features.T
        bd[HC + h, h * M:(h + 1) * M] = 1.0
        nb[h * DH:(h + 1) * DH, h] = -0.5
    a["bd"], a["nb6"] = bd, nb
    a["wproj0"] = halves(L0_attn_W_proj)
    a["rows3"] = np.stack([np.broadcast_to(v, (128, C)) for v in (L0_attn_b_proj, L0_attn_gamma, L0_attn_beta)], 1)
    a["rw"] = np.stack([halves(L0_ffn_router_w.T), halves(L1_ffn_gate_w.T)], 1)
    a["rank"] = np.broadcast_to(np.arange(NE, 0, -1).astype(f), (128, NE))
    wv = np.asarray(L1_attn_W_attn)[:, 2 * C:].reshape(C, NH // 2, 2, DH).transpose(0, 2, 1, 3).reshape(C, C)
    a["wat"] = halves(np.concatenate([np.asarray(L1_attn_W_attn)[:, :2 * C], wv], 1))
    a["wproj1"] = halves(L1_attn_W_proj)
    a["kmask"] = (0.25 * (np.arange(HC)[:, None] // DH == np.arange(6)[None, :])).astype(f)
    ci = np.where(np.arange(64)[None, :] <= (np.arange(128) % 64)[:, None], 0.0, -1e9)
    ct = np.where(np.arange(NS)[None, :] <= np.arange(128)[:, None], 0.0, -1e9)
    a["cmask"] = np.concatenate([ci, ct], 1).astype(f)

    def up(w):
        return halves(w.T).reshape(HC, 2 * HID)

    def down(w):
        return np.asarray(w).T.reshape(HT, 128, C).transpose(1, 0, 2).reshape(128, HT * C)
    a["m0_w1"] = np.stack([up(L0_ffn_w1[e]) for e in range(NE)])
    a["m0_w2"] = np.stack([down(L0_ffn_w2[e]) for e in range(NE)])
    g1 = list(L1_ffn_w1) + [L1_ffn_ws1]
    g3 = list(L1_ffn_w3) + [L1_ffn_ws3]
    g2 = list(L1_ffn_w2) + [L1_ffn_ws2]
    a["m1_w1"] = np.stack([np.concatenate([up(g1[e]), up(g3[e])], 1) for e in range(NE + 1)])
    a["m1_w2"] = np.stack([down(w) for w in g2])
    row = [(np.arange(NE * NT) % NT != 0), np.ones(NE), np.tile(CAP * np.arange(MAXT), NE), np.arange(NSLOT)]
    row = np.broadcast_to(np.concatenate(row).astype(f), (128, NE * NT + NE + NE * MAXT + NSLOT))
    token = 1 + np.arange(128, dtype=f)[:, None] + 128 * np.arange(NT, dtype=f)[None, :]
    a["routec"] = np.concatenate([row, token, np.triu(np.ones((128, 128), f), 1)], 1)
    return a


def kernel(**inputs):
    import concourse.bacc as _bacc
    from concourse.bass_utils import run_bass_kernel_spmd as _run

    nc = _bacc.Bacc("TRN2", target_bir_lowering=False, num_devices=1)
    arrays, aps = {}, {}
    for name, v in arrange(**{k: np.asarray(v) for k, v in inputs.items()}).items():
        v = np.ascontiguousarray(v)
        arrays[f"in_{name}"] = v
        aps[name] = nc.dram_tensor(f"in_{name}", v.shape, mybir.dt.from_np(v.dtype), kind="ExternalInput").ap()
    out = nc.dram_tensor("out_h", (NTOK, C), F32, kind="ExternalOutput").ap()
    for name, shape in (("Xs0", (NSLOT * CAP, C + 1)), ("Xs1", (NSLOT * CAP, C + 1)), ("Ys", (NY, C))):
        aps[name] = nc.dram_tensor(name, shape, F32).ap()
    build(nc, aps, out)
    r = _run(nc, [arrays], core_ids=[0])
    got = np.asarray(r.results[0]["out_h"])
    return np.concatenate([got[:B * NP_].reshape(B, NP_, C), got[B * NP_:].reshape(B, NS, C)], 1)
```

```python
from contextlib import ExitStack

import numpy as np
import concourse.bass as bass
from concourse import mybir

ALU = mybir.AluOpType
ACT = mybir.ActivationFunctionType
F32 = mybir.dt.float32
BF16 = mybir.dt.bfloat16
I32 = mybir.dt.int32
AX = mybir.AxisListType.X

B, SIDE, PATCH, CH = 8, 128, 16, 3
NP_ = (SIDE // PATCH) ** 2
VOCAB, NSEG = 8000, 3
NS = 77
C = 192
HC = C // 2
NH, DH, M = 12, 16, 64
NE, HID = 8, 512
HT = HID // 128
HALO = PATCH + 2
KP = 2 * HALO * CH
NJ = HALO // 2
NG = 5
PDIM = PATCH * PATCH * CH * NG
IT = B * NP_ // 128
NTOK = B * (NP_ + NS)
NT = -(-NTOK // 128)
ROWS = [min(128, NTOK - 128 * t) for t in range(NT)]
OFF = [128 * t for t in range(NT)]
TT = NT - IT
NB = IT + B
BROWS = [128] * IT + [NS] * B
BOFF = [128 * t for t in range(IT)] + [IT * 128 + NS * b for b in range(B)]
CHUNK = [(0, 512, (0, 1, 2, 3)), (512, 512, (4, 5, 6, 7)), (1024, NTOK - 1024, (8,))]
TEXT_FIRST = [CHUNK[1], CHUNK[2], CHUNK[0]]
PAIR = 2 * (DH + 1)
NK = NP_ + NS
CHUNK1 = [(0, 512, 4), (512, 4 * NS, -(-(512 + 4 * NS) // 128)), (512 + 4 * NS, 4 * NS, NT)]
EPS = 1e-5

TOK = dict(x=(0, NJ * 512), x2=(4608, NJ * 512), w=(9216, NG * NJ * C), weff=(17856, NJ * (C + 1)), seg=(19600, TT * C),
           pos=(20560, TT * C), beta=(21520, 3 * NJ * C))
A0 = dict(qaug=(0, 2 * NTOK), kaug=(2280, 2 * NTOK), att=(0, NB * C), attT=(2304, 2 * NTOK), qp=(4560, 6 * NTOK),
          kp=(11328, NB * NH * M), v=(20544, NB * NH * 17), kv=(22992, (B * 6 + 1) * PAIR))
A1 = dict(qT=(0, 2 * NTOK), kT=(2256, 2 * NTOK), ko=(4512, 3 * 4 * NK), v=(6768, B * NH * 17), vi=(8400, B * NH * 17), sx=(10032, 3 * 4 * NK),
          att=(11880, NB * C), attT=(14184, 2 * NTOK), pT=(16440, 2 * 6 * NS))
ES = (2 * HID + HT * C, 4 * HID + HT * C)
ARENA = A0["kv"][0] + A0["kv"][1] + 6 * ES[0]
WBASE = (ARENA - NE * ES[0], ARENA - NE * ES[1])
MB = dict(xs=(0, 2 * (C + 1)), xsT=(386, 4 * 128), act=(898, 2 * HID), hT=(1922, 2 * HID), ys=(2946, 2 * C),
          back=(3330, 2 * NT * C), sh=(3330, 3 * HT * 512), sa=(9474, 2 * 512))
CAP = 128
NSLOT = (2 * NTOK + NE * (CAP - 1)) // CAP
MAXT = -(-NTOK // CAP)
CHOICE = 128 * NT
NY = 128 + 2 * CHOICE
SENT_A = 5


def build(nc, d, out):
    with ExitStack() as ctx:
        def sb(name, shape, dt=F32):
            return ctx.enter_context(nc.sbuf_tensor(name, shape, dt))

        def sem(name):
            return ctx.enter_context(nc.semaphore(name))

        arena = sb("arena", [128, ARENA])

        def at(place):
            return arena[:, place[0]:place[0] + place[1]]

        PS = ctx.enter_context(nc.psum_tensor("PS", [128, 8, 512], F32))

        H = sb("H", [128, NT, C])
        xnd = sb("xnd", [128, NT, C + 1])
        xn = xnd[:, :, 0:C]
        xnT = sb("xnT", [HC, 2, NTOK])
        bnst = sb("bnst", [128, NT, 6])
        mv = sb("mv", [128, NT, 2])
        rstd = sb("rstd", [128, 2, NT])
        mhalf = sb("mhalf", [128, NT])
        ident = sb("ident", [128, 128])
        identb = sb("identb", [128, 128], BF16)
        ones = sb("ones", [128, 128])
        ids = sb("ids", [128, 2 * TT], I32)
        idx = sb("idx", [128, 3, 2 * TT], I32)
        gb = sb("gb", [KP, 2, NG, NJ])
        mult = sb("mult", [KP, NJ])
        tokb = sb("tokb", [1, C])
        sgbw = sb("sgbw", [128, 2 * C])
        tst = sb("tst", [128, 6, IT])
        wqkv = sb("wqkv", [HC, 2, 3 * C])
        bd = sb("bd", [HC + 6, 6 * M])
        nb6 = sb("nb6", [HC, 6])
        wproj0 = sb("wproj0", [HC, 2, C])
        rows3 = sb("rows3", [128, 3, C])
        rec = sb("rec", [128, 2, NH])
        wat = sb("wat", [HC, 2, 3 * C])
        wproj1 = sb("wproj1", [HC, 2, C])
        kmask = sb("kmask", [HC, 6])
        cmaskf = sb("cmaskf", [128, NP_ + NS])
        cmask = sb("cmask", [128, NP_ + NS], BF16)
        rw = sb("rw", [HC, 2, 2, NE])
        rank = sb("rank", [128, NE])
        lg = sb("lg", [128, NT, NE])
        rt = sb("rt", [128, 6, NT, NE])
        rs = sb("rs", [128, 6, NT])
        run = sb("run", [128, 3, NE])
        cw = sb("cw", [128, 3, NT])
        cnt = sb("cnt", [128, 4, NE * NT])
        tiles_of = sb("tiles_of", [128, 4, NE])
        place = sb("place", [128, 2, NT], I32)
        eidf = sb("eidf", [1, NSLOT, NE])
        eids = sb("eids", [1, NSLOT])
        eid = sb("eid", [1, NSLOT], I32)
        routec = sb("routec", [128, NE * NT + NE + NE * MAXT + NSLOT + NT + 128])
        blank = sb("blank", [128, C + 1])
        dest = sb("dest", [128, 4], I32)
        wsh = sb("wsh", [128, ES[1]])
        mx = sb("mx", [128, 2, 4])

        ld_x, ld_tokc, ld_const, ld_ids, ld_a0, ld_moe, ld_a1 = (
            sem(n) for n in ("ld_x", "ld_tokc", "ld_const", "ld_ids", "ld_a0", "ld_moe", "ld_a1"))
        ld_w = [sem(f"ld_w{g}") for g in range(NG)]
        ld_e = [sem("ld_e0"), sem("ld_e1")]
        ld_sh, ld_blank, slots_zero = sem("ld_sh"), sem("ld_blank"), sem("slots_zero")
        gathered, idx_set = sem("gathered"), sem("idx_set")
        stored = sem("stored")
        ones_set, lg_set, v_ones0, v_ones1, kv_zero = (sem(n) for n in ("ones_set", "lg_set", "v_ones0", "v_ones1", "kv_zero"))
        x2_done, fold0, folded, beta_prod, beta_sum, tok_ps, sg_sb, tok_h, text_h = (
            sem(n) for n in ("x2_done", "fold0", "folded", "beta_prod", "beta_sum", "tok_ps", "sg_sb", "tok_h", "text_h"))
        mult_set, var_in, rs_out, mhalf_set = (sem(n) for n in ("mult_set", "var_in", "rs_out", "mhalf_set"))
        xn_ready = [sem(f"xn_ready{k}") for k in range(4)]
        tp_ps, tp_out = sem("tp_ps"), sem("tp_out")
        qk_ps, qk_sq, qk_aug, nm_ps, nm_out = (sem(n) for n in ("qk_ps", "qk_sq", "qk_aug", "nm_ps", "nm_out"))
        v_ps, v_out, ph_ps, ph_out, kv_ps, kv_out = (sem(n) for n in ("v_ps", "v_out", "ph_ps", "ph_out", "kv_ps", "kv_out"))
        o0_ps, att0, y0_ps, y0_out, xnb, yn, hb, h1 = (
            sem(n) for n in ("o0_ps", "att0", "y0_ps", "y0_out", "xnb", "yn", "hb", "h1"))
        lg_ps = [sem(f"lg_ps{k}") for k in range(2)]
        rt_in = [sem(f"rt_in{k}") for k in range(2)]
        rt_exp = [sem(f"rt_exp{k}") for k in range(2)]
        masks_set = sem("masks_set")
        imp_in, imp_ps, imp_read = sem("imp_in"), sem("imp_ps"), sem("imp_read")
        rank_ps, sel_in, placed = ([sem(f"{n}{k}") for k in range(2)] for n in ("rank_ps", "sel_in", "placed"))
        u_ps, u_act, g_out = sem("u_ps"), sem("u_act"), sem("g_out")
        ysh_ps, ysh_acc = sem("ysh_ps"), sem("ysh_acc")
        sent_a, sent_b, sent, rows_set, dest_set = (
            [sem(f"{n}{k}") for k in range(2)] for n in ("sent_a", "sent_b", "sent", "rows_set", "dest_set"))
        xs_in = [[sem(f"xs_in{k}_{z}") for z in range(2)] for k in range(2)]
        ys_out = [[sem(f"ys_out{k}_{z}") for z in range(2)] for k in range(2)]
        xt_ps, xt_sb, up_ps, up_act, up_sb, ht_ps, ht_sb, dn_ps, dn_sb, added = (
            [sem(f"{n}{k}") for k in range(2)] for n in ("xt_ps", "xt_sb", "up_ps", "up_act", "up_sb", "ht_ps", "ht_sb",
                                                         "dn_ps", "dn_sb", "added"))
        back = [[sem(f"back{k}_{t}") for t in range(NT)] for k in range(2)]
        q1_ps, q1_act, q1_dve, v1_ps, v1_out = (sem(n) for n in ("q1_ps", "q1_act", "q1_dve", "v1_ps", "v1_out"))
        own_set, s_ps, s_sub, s_exp, t_ps, t_act, o1_ps, att1, y1_ps, h3 = (
            sem(n) for n in ("own_set", "s_ps", "s_sub", "s_exp", "t_ps", "t_act", "o1_ps", "att1", "y1_ps", "h3"))
        dve_step, pool_step = sem("dve_step"), sem("pool_step")

        xT = at(TOK["x"])[0:KP].rearrange("p (j n) -> p j n", j=NJ)
        x2 = at(TOK["x2"])[0:KP].rearrange("p (j n) -> p j n", j=NJ)
        wt = at(TOK["w"])[0:KP].rearrange("p (g j n) -> p g j n", g=NG, j=NJ)
        weff = at(TOK["weff"])[0:KP].rearrange("p (j n) -> p j n", j=NJ)
        seg = at(TOK["seg"]).rearrange("p (b n) -> p b n", b=TT)
        pos = at(TOK["pos"]).rearrange("p (b n) -> p b n", b=TT)
        betaw = at(TOK["beta"])[0:KP].rearrange("p (u j n) -> p u j n", u=3, j=NJ)
        qkaug = [at(A0[n])[0:HC + 6].rearrange("p (h n) -> p h n", h=2) for n in ("qaug", "kaug")]
        att0b = at(A0["att"]).rearrange("p (t n) -> p t n", t=NB)
        attT0 = at(A0["attT"])[0:HC].rearrange("p (h n) -> p h n", h=2)
        qp = at(A0["qp"]).rearrange("p (r n) -> p r n", r=6)
        sq = at((A0["kp"][0], 1024))[0:HC].rearrange("p (u n) -> p u n", u=2)
        kp = at(A0["kp"]).rearrange("p (t n) -> p t n", t=NB)
        v0 = at(A0["v"]).rearrange("p (t h e) -> p t h e", t=NB, h=NH)
        kv_flat = at(A0["kv"])
        kv = kv_flat[:, 0:B * 6 * PAIR].rearrange("p (b r e) -> p b r e", b=B, r=6)
        qT1 = at(A1["qT"])[0:HC].rearrange("p (h n) -> p h n", h=2)
        kT1 = at(A1["kT"])[0:HC].rearrange("p (h n) -> p h n", h=2)
        kown = at(A1["ko"])[0:HC].rearrange("p (u x n) -> p u x n", u=3, x=4)
        v1 = at(A1["v"]).rearrange("p (b h e) -> p b h e", b=B, h=NH)
        vi = at(A1["vi"]).rearrange("p (b r e) -> p b r e", b=B, r=NH // 2)
        sx = at(A1["sx"]).rearrange("p (u n) -> p u n", u=3)
        pT = at(A1["pT"]).rearrange("p (u n) -> p u n", u=2)
        att1b = at(A1["att"]).rearrange("p (t n) -> p t n", t=NB)
        attT1 = at(A1["attT"])[0:HC].rearrange("p (h n) -> p h n", h=2)

        tri = routec[:, NE * NT + NE + NE * MAXT + NSLOT + NT:]
        token = routec[:, NE * NT + NE + NE * MAXT + NSLOT:NE * NT + NE + NE * MAXT + NSLOT + NT]
        xs = at(MB["xs"]).rearrange("p (z n) -> p z n", z=2)
        xsT = at(MB["xsT"])[0:HC].rearrange("p (z c n) -> p z c n", z=2, c=2)
        hact = at(MB["act"]).rearrange("p (z n) -> p z n", z=2)
        hT = at(MB["hT"]).rearrange("p (z i n) -> p z i n", z=2, i=HT)
        ys = at(MB["ys"]).rearrange("p (z n) -> p z n", z=2)
        yback = at(MB["back"]).rearrange("p (k t n) -> p k t n", k=2, t=NT)
        shT = at(MB["sh"]).rearrange("p (s i n) -> p s i n", s=3, i=HT)
        sa = at(MB["sa"]).rearrange("p (s n) -> p s n", s=2)
        wsh1 = [wsh[0:HC, q * 2 * HID:(q + 1) * 2 * HID].rearrange("p (c n) -> p c n", c=2) for q in range(2)]
        wsh2 = wsh[:, 4 * HID:].rearrange("p (i n) -> p i n", i=HT)
        Xs, Ys = (d["Xs0"], d["Xs1"]), d["Ys"]
        LAST = NSLOT - 1
        PIPE0, PAIRS = 2, (NSLOT - 5) // 2

        NEED = [sum(BOFF[b] < OFF[t] + ROWS[t] for b in range(NB)) for t in range(NT)]
        UNITS = [(t, None, v) for t in range(IT) for v in range(3)] + [(None, b, v) for b in range(B) for v in range(3)]
        IMG_UNITS = 3 * IT
        AFTER_UNITS = len(UNITS)

        def parts_by(u):
            return min(u + 1, IMG_UNITS) + 2 * max(0, u + 1 - IMG_UNITS)

        PROJECT_AT = {3 * NEED[t] + 4: t for t in range(NT)}
        STEPS = max(PROJECT_AT) + 1
        STATS_AT = {20: 0, 21: 1, 22: 2, 23: 3, 25: 4, 30: 5}
        POWER_AT = {23: [0, 1, 2, 3], 30: [4, 5]}
        SCALE_AT = {26: 0, 27: 1, 28: 2, 29: 3, 33: 4, 34: 5}
        NORMED = 6
        TURN_AT = {**{3 * b + 6: ("att", b) for b in range(NB)}, 28: ("xn", 0), 29: ("xn", 1), 31: ("xn", 2), 32: ("xn", 3),
                   35: ("xn", 4), 37: ("xn", 5)}
        LATE = [[6, 7], [8]]
        TURNS = [TURN_AT[u] for u in sorted(TURN_AT)]

        BTILES = list(range(IT, NB)) + list(range(IT))
        PHI = [("k", t) for t in BTILES] + [("qt", r) for r in range(6)] + [("qi", r) for r in range(3)]
        QK = [(c, s, h) for c in TEXT_FIRST for s in range(2) for h in range(2)]
        TP_XN0, TP_ATT0, TP_XN1, TP_XN2, TP_ATT1, TP_XN3 = 0, NT, NT + NB, 2 * NT + NB, 3 * NT + NB, 3 * NT + 2 * NB + NORMED
        TILES_TF = [t for _, _, ts in TEXT_FIRST for t in ts]
        TILES = list(range(NT))

        block = ctx.enter_context(nc.Block())

        @block.sync
        def _(sp):
            def load_expert(k, e, dst=None):
                w = arena[:, WBASE[k] + e * ES[k]:WBASE[k] + (e + 1) * ES[k]] if dst is None else dst[:]
                done = ld_e[k] if dst is None else ld_sh
                n = 2 * HID * (1 + k)
                sp.dma_start(w[0:HC, 0:n], d[f"m{k}_w1"][e]).then_inc(done, 16)
                sp.dma_start(w[:, n:], d[f"m{k}_w2"][e]).then_inc(done, 16)

            def load_slots(k, j, z):
                if not isinstance(j, int) or j >= 2:
                    sp.wait_ge(xt_ps[k], j - 1)
                    sp.wait_ge(dest_set[k], j - 1)
                sp.dma_start(xs[:, z, :], Xs[k][bass.ds(j * CAP, CAP), :]).then_inc(xs_in[k][z], 16)

            def slots(k):
                sp.wait_ge(sent_a[k], 16 * SENT_A)
                sp.wait_ge(sent_b[k], 16 * (NT - SENT_A))
                sp.wait_ge(sent[k], 16 * NT)
                for j in range(PIPE0 + 4):
                    load_slots(k, j, j % 2)
                with sp.Fori(0, PAIRS - 1) as i:
                    for z in range(2):
                        load_slots(k, PIPE0 + 4 + 2 * i + z, z)
                for j in range(PIPE0 + 4 + 2 * (PAIRS - 1), NSLOT):
                    load_slots(k, j, j % 2)
                for z in range(2):
                    sp.wait_ge(ys_out[k][z], 16 * ((NSLOT + 1 - z) // 2))
                rows = Ys[128:NY, :].rearrange("(c t p) n -> t p c n", c=2, p=128)
                for t in TILES:
                    P = ROWS[t]
                    sp.dma_start(yback[0:P, :, t, :], rows[t, 0:P]).then_inc(back[k][t], 16)

            sp.dma_start(ids[:], d["ids"]).then_inc(ld_ids, 16)
            sp.dma_start(gb[:], d["gb"]).then_inc(ld_tokc, 16)
            sp.dma_start(mult[:], d["mult"]).then_inc(ld_tokc, 16)
            sp.dma_start(tokb[:], d["tokb"]).then_inc(ld_tokc, 16)
            sp.dma_start(xT, d["xT"]).then_inc(ld_x, 16)
            sp.dma_start(wt[:, 0], d["wt"][:, 0]).then_inc(ld_w[0], 16)
            for g in range(1, NG):
                sp.dma_start(wt[:, g], d["wt"][:, g]).then_inc(ld_w[g], 16)
            for buf, name in ((ident[:], "ident"), (pos, "pos")):
                sp.dma_start(buf, d[name]).then_inc(ld_const, 16)
            for buf, name in ((wqkv, "wqkv"), (bd, "bd"), (nb6, "nb6"), (wproj0, "wproj0"), (rows3, "rows3")):
                sp.dma_start(buf[:], d[name]).then_inc(ld_a0, 16)
            for buf, name in ((rw, "rw"), (rank, "rank")):
                sp.dma_start(buf[:], d[name]).then_inc(ld_moe, 16)
            sp.dma_start(routec[:], d["routec"]).then_inc(ld_moe, 16)
            sp.dma_start(blank[:], d["blank"]).then_inc(ld_blank, 16)
            load_expert(1, NE, wsh)
            sp.wait_ge(ld_blank, 16)
            for k in range(2):
                sp.dma_start(Xs[k].rearrange("(j p) c -> p j c", p=CAP),
                             blank[:].unsqueeze(1).broadcast_to([128, NSLOT, C + 1])).then_inc(slots_zero, 16)
            for buf, name in ((wat, "wat"), (wproj1, "wproj1"), (kmask, "kmask"), (cmaskf, "cmask")):
                sp.dma_start(buf[:], d[name]).then_inc(ld_a1, 16)
            sp.wait_ge(tok_ps, 3)
            for e in range(2, NE):
                load_expert(0, e)
            sp.wait_ge(kv_ps, 2 * B)
            load_expert(0, 0)
            sp.wait_ge(o0_ps, NB)
            load_expert(0, 1)
            slots(0)
            for e in range(2, NE):
                load_expert(1, e)
            sp.wait_ge(y1_ps, NT)
            for e in range(2):
                load_expert(1, e)
            slots(1)
            for t in TILES:
                sp.wait_ge(added[1], 2 * (t - t % 3) + 3 + t % 3 + 1)
                sp.dma_start(out[OFF[t]:OFF[t] + ROWS[t], :], H[0:ROWS[t], t, :]).then_inc(stored, 16)
            sp.wait_ge(stored, 16 * NT)

        @block.gpsimd
        def _(pool):
            steps = [0]

            def step(ins):
                steps[0] += 1
                ins.then_inc(pool_step, 1)
                pool.wait_ge(pool_step, steps[0])

            turns = [0]

            def rsqrt(rows, cols):
                turns[0] += 1
                pool.wait_ge(var_in, turns[0])
                pool.tensor_tensor(out=rstd[0:rows, 1, cols], in0=rstd[0:rows, 0, cols], in1=mhalf[0:rows, cols],
                                   op=ALU.pow).then_inc(rs_out, 1)

            def rsqrt_tiles(tiles):
                rsqrt(ROWS[tiles[0]], slice(tiles[0], tiles[0] + len(tiles)))

            pool.memset(ones[:], 1.0).then_inc(ones_set, 1)
            pool.memset(mhalf[:], -0.5).then_inc(mhalf_set, 1)
            pool.wait_ge(idx_set, 2)
            for b in range(TT):
                P = ROWS[IT + b]
                pool.indirect_dma_start(out=H[0:P, IT + b, :], out_offset=None, in_=d["table"],
                                        in_offset=bass.IndirectOffsetOnAxis(ap=idx[0:P, 2, b:b + 1], axis=0)).then_inc(gathered, 16)
                pool.indirect_dma_start(out=seg[0:P, b, :], out_offset=None, in_=d["segt"],
                                        in_offset=bass.IndirectOffsetOnAxis(ap=idx[0:P, 2, TT + b:TT + b + 1], axis=0)).then_inc(gathered, 16)
            pool.memset(lg[:], 0.0).then_inc(lg_set, 1)
            for g in range(1, NG):
                pool.wait_ge(beta_prod, g + 1)
                if g >= 2:
                    pool.wait_ge(beta_sum, g - 1)
                pool.tensor_tensor(out=betaw[:, 0], in0=betaw[:, 0], in1=betaw[:, 2 - g % 2], op=ALU.add).then_inc(beta_sum, 1)
            pool.wait_ge(mhalf_set, 1)
            rsqrt_tiles(CHUNK[1][2])
            rsqrt_tiles(CHUNK[2][2])
            rsqrt(128, slice(0, IT))
            rsqrt_tiles(CHUNK[0][2])
            pool.wait_ge(tok_h, IT)
            pool.wait_ge(text_h, 2)
            pool.memset(v0[:, :, :, DH:DH + 1], 1.0).then_inc(v_ones0, 1)
            pool.memset(at(A0["kv"]), 0.0).then_inc(kv_zero, 1)
            pool.wait_ge(ld_a0, 80)
            for n, t in enumerate(TILES_TF):
                P = ROWS[t]
                pool.wait_ge(tp_ps, TP_XN0 + n + 1)
                pool.tensor_tensor(out=xn[0:P, t, :], in0=xn[0:P, t, :], in1=rows3[0:P, 0, :], op=ALU.add).then_inc(xnb, 1)
                pool.tensor_tensor(out=H[0:P, t, :], in0=H[0:P, t, :], in1=rows3[0:P, 2, :], op=ALU.add).then_inc(hb, 1)
            for tiles in [CHUNK[0][2]] * 2 + [(4, 5)] * 2 + LATE:
                rsqrt_tiles(tiles)

            def dispatch(k):
                pool.wait_ge(slots_zero, 32)
                for c, tiles, done in ((0, TILES[:SENT_A], sent_a), (0, TILES[SENT_A:], sent_b), (1, TILES[:SENT_A], sent),
                                       (1, TILES[SENT_A:], sent)):
                    pool.wait_ge(placed[k], c + 1)
                    pool.wait_ge(rows_set[k], 1 if c == 0 else 2 if tiles[0] == 0 else 3)
                    for t in tiles:
                        pool.indirect_dma_start(out=Xs[k], out_offset=bass.IndirectOffsetOnAxis(ap=place[0:ROWS[t], c, t:t + 1], axis=0),
                                                in_=xnd[0:ROWS[t], t, :], in_offset=None).then_inc(done[k], 16)

            def keep_rows(k, j):
                if j >= 4:
                    pool.wait_ge(ys_out[k][j % 2], 16 * (j // 2 - 1))
                pool.wait_ge(xs_in[k][j % 2], 16 * (j // 2 + 1))
                pool.tensor_copy(dest[:, j % 4:j % 4 + 1], xs[:, j % 2, C:C + 1]).then_inc(dest_set[k], 1)

            def scatter(k, j):
                pool.wait_ge(dest_set[k], j + 1)
                if j >= 1:
                    pool.wait_ge(ys_out[k][(j - 1) % 2], 16 * ((j - 1) // 2 + 1))
                pool.wait_ge(dn_sb[k], j + 1)
                pool.indirect_dma_start(out=Ys, out_offset=bass.IndirectOffsetOnAxis(ap=dest[:, j % 4:j % 4 + 1], axis=0),
                                        in_=ys[:, j % 2, :], in_offset=None).then_inc(ys_out[k][j % 2], 16)

            def slots(k):
                for j in range(3):
                    keep_rows(k, j)
                for s in range(1, NSLOT + 1):
                    if s + 2 <= LAST:
                        keep_rows(k, s + 2)
                    scatter(k, s - 1)

            for tiles in LATE:
                rsqrt_tiles(tiles)
            dispatch(0)
            slots(0)
            for _, _, tiles in CHUNK:
                rsqrt_tiles(tiles)
            pool.wait_ge(added[0], 2 * NT)
            for buf, value in ((vi[0:64, :, :, DH:DH + 1], 1.0), (vi[64:128, :, :, PAIR - 1:PAIR], 1.0), (vi[0:64, :, :, DH + 1:], 0.0),
                               (vi[64:128, :, :, 0:DH + 1], 0.0)):
                step(pool.memset(buf, value))
            pool.memset(v1[:, :, :, DH:DH + 1], 1.0).then_inc(v_ones1, 1)
            pool.wait_ge(ld_a1, 64)
            pool.tensor_copy(identb[:], ident[:]).then_inc(masks_set, 1)
            pool.tensor_copy(cmask[:], cmaskf[:]).then_inc(masks_set, 1)
            pool.wait_ge(q1_dve, 6)
            for u, (t, b, v) in enumerate(UNITS):
                if u - 3 in POWER_AT:
                    rsqrt_tiles(POWER_AT[u - 3])
                if u >= 3:
                    pool.wait_ge(s_ps, u - 2)
                for a in range(2):
                    half, h = (2 * v + a) // 3, 2 * ((2 * v + a) % 3)
                    if t is not None:
                        dst = kown[:, u % 3, 2 * a:2 * a + 2, 0:2 * NP_].rearrange("p z (k n) -> p z k n", k=2)
                        src = kT1[:, half, :].rearrange("p (b n) -> p b n", b=B)[:, 2 * t:2 * t + 2, 0:NP_]
                        src = src.unsqueeze(1).broadcast_to([HC, 2, 2, NP_])
                        own = kmask[:, h:h + 2].unsqueeze(2).unsqueeze(3).broadcast_to([HC, 2, 2, NP_])
                    else:
                        dst = kown[:, u % 3, 2 * a:2 * a + 2, :]
                        src = kT1[:, half, NK * b:NK * (b + 1)].unsqueeze(1).broadcast_to([HC, 2, NK])
                        own = kmask[:, h:h + 2].unsqueeze(2).broadcast_to([HC, 2, NK])
                    pool.tensor_tensor(out=dst, in0=src, in1=own, op=ALU.mult).then_inc(own_set, 1)
            for tiles in LATE:
                rsqrt_tiles(tiles)
            dispatch(1)
            slots(1)

        @block.scalar
        def _(act):
            A = nc.scalar.activation

            def tp_evac(n, t, dst, bank=None):
                off, P = t if isinstance(t, tuple) else (OFF[t], ROWS[t])
                act.wait_ge(tp_ps, n + 1)
                A(dst[:, :, off:off + P], PS[0:HC, 6 + n % 2 if bank is None else bank, 0:256].rearrange("p (h n) -> p h n", h=2)[:, :, 0:P],
                  ACT.Copy).then_inc(tp_out, 1)

            act.wait_ge(ld_tokc, 48)
            A(weff[:, :, C:C + 1], mult[:].unsqueeze(2), ACT.Copy).then_inc(mult_set, 1)
            act.wait_ge(ld_x, 16)
            for t in range(IT):
                cols = slice(128 * t, 128 * t + 128)
                A(x2[:, :, cols], xT[:, :, cols], ACT.Square).then_inc(x2_done, 1)
            act.wait_ge(ld_w[0], 16)
            for j in range(NJ):
                A(weff[:, j, 0:C], wt[:, 0, j, :], ACT.Copy, scale=gb[:, 0, 0, j:j + 1]).then_inc(fold0, 1)
            for g in range(NG):
                act.wait_ge(ld_w[g], 16)
                if g >= 3:
                    act.wait_ge(beta_sum, g - 2)
                for j in range(NJ):
                    last = A(betaw[:, 0 if g == 0 else 2 - g % 2, j, :], wt[:, g, j, :], ACT.Copy, scale=gb[:, 1, g, j:j + 1])
                last.then_inc(beta_prod, 1)
            act.wait_ge(tok_ps, 3)
            A(sgbw[:], PS[:, 4, 0:2 * C], ACT.Copy).then_inc(sg_sb, 1)

            for n, t in enumerate(TILES_TF[:TT]):
                tp_evac(TP_XN0 + n, t, xnT)
            for n, ((off, N, _), s, h) in enumerate(QK):
                if n == 8:
                    for m, t in enumerate(TILES_TF[TT:]):
                        tp_evac(TP_XN0 + TT + m, t, xnT)
                act.wait_ge(qk_aug, n + 1)
                if n >= 2:
                    act.wait_ge(nm_ps, n - 1)
                A(sq[:, n % 2, 0:N], qkaug[s][0:HC, h, off:off + N], ACT.Square).then_inc(qk_sq, 1)
            act.wait_ge(v_ones0, 1)
            for n, t in enumerate(BTILES):
                act.wait_ge(v_ps, n + 1)
                A(v0[0:BROWS[t], t, :, 0:DH], PS[0:BROWS[t], 4 + n % 2, 0:C].rearrange("p (h e) -> p h e", h=NH),
                  ACT.Copy).then_inc(v_out, 1)
            for n, (kind, r) in enumerate(PHI):
                act.wait_ge(ph_ps, n + 1)
                b0 = 2 * (n % 2)
                if kind == "k":
                    A(kp[0:BROWS[r], r, :].rearrange("p (u n) -> p u n", u=2), PS[0:BROWS[r], b0:b0 + 2, 0:384],
                      ACT.Exp).then_inc(ph_out, 1)
                elif kind == "qt":
                    A(qp[:, r, 512:NTOK].rearrange("p (u n) -> p u n", u=2), PS[:, b0:b0 + 2, 0:4 * NS],
                      ACT.Exp).then_inc(ph_out, 1)
                else:
                    A(qp[:, 2 * r:2 * r + 2, 0:512], PS[:, b0:b0 + 2, :], ACT.Exp).then_inc(ph_out, 1)
            for t in range(NB):
                tp_evac(TP_ATT0 + t, (BOFF[t], BROWS[t]), attT0)

            def turned_rows(k, j, z):
                act.wait_ge(xt_ps[k], j + 1)
                if not isinstance(j, int) or j >= 2:
                    act.wait_ge(up_ps[k], j - 1)
                A(xsT[:, z, :, :], PS[0:HC, 6, 0:256].rearrange("p (c n) -> p c n", c=2), ACT.Copy).then_inc(xt_sb[k], 1)

            def activate(k, j, z):
                act.wait_ge(up_ps[k], j + 1)
                if not isinstance(j, int) or j >= 2:
                    act.wait_ge(ht_ps[k], j - 1)
                bank = z if k == 0 else 2 * z
                A(hact[:, z, :], PS[:, bank, :], ACT.Silu).then_inc(up_act[k], 1)

            def result(k, j, z, round_):
                act.wait_ge(dn_ps[k], j + 1)
                if round_ is not None:
                    act.wait_ge(ys_out[k][z], 16 * round_)
                A(ys[:, z, :], PS[:, 7, 0:C], ACT.Copy).then_inc(dn_sb[k], 1)

            def slots(k):
                turned_rows(k, 0, 0)
                activate(k, 0, 0)
                turned_rows(k, 1, 1)
                activate(k, 1, 1)
                turned_rows(k, 2, 0)
                activate(k, 2, 0)
                turned_rows(k, 3, 1)
                result(k, 0, 0, None)
                with act.Fori(0, PAIRS) as i:
                    for z in range(2):
                        s = PIPE0 + 2 * i + z
                        activate(k, s + 1, 1 - z)
                        turned_rows(k, s + 2, z)
                        if z == 0:
                            act.wait_ge(ys_out[k][0], 16 * i + 16)
                            result(k, s - 1, 1, None)
                        else:
                            act.wait_ge(ys_out[k][1], 16 * i + 16)
                            result(k, s - 1, 0, i + 1)
                for s in range(PIPE0 + 2 * PAIRS, NSLOT + 1):
                    if s + 1 <= LAST:
                        activate(k, s + 1, (s + 1) % 2)
                    if s + 2 <= LAST:
                        turned_rows(k, s + 2, s % 2)
                    result(k, s - 1, (s - 1) % 2, (s - 1) // 2)

            def route_exp(k):
                act.wait_ge(rt_in[k], 1)
                A(rt[:, 0], rt[:, 0], ACT.Exp).then_inc(rt_exp[k], 1)

            for t in TILES:
                tp_evac(TP_XN1 + t, t, xnT)
            route_exp(0)
            slots(0)
            done = 0
            for c, (off, N, need) in enumerate(CHUNK1):
                for t in TILES[done:need]:
                    tp_evac(TP_XN2 + t, t, xnT)
                done = need
                for h in range(2):
                    act.wait_ge(q1_ps, 4 * c + h + 1)
                    A(qT1[:, h, off:off + N], PS[0:HC, h, 0:N], ACT.Copy).then_inc(q1_act, 1)
            act.wait_ge(v_ones1, 1)
            for n in range(2 * B):
                act.wait_ge(v1_ps, n + 1)
                b, src = n % B, PS[:, 4 + n % 2, 0:C]
                if n < B:
                    for z in range(2):
                        rows = slice(64 * z, 64 * z + 64)
                        A(vi[rows, b, :, 17 * z:17 * z + DH], src[rows, 0:HC].rearrange("p (r e) -> p r e", e=DH),
                          ACT.Copy).then_inc(v1_out, 1)
                else:
                    A(v1[0:NS, b, :, 0:DH].rearrange("p (r z) e -> p z r e", z=2),
                      src[0:NS].rearrange("p (z r e) -> p z r e", z=2, e=DH), ACT.Copy).then_inc(v1_out, 1)

            def probs(u):
                P, w = (128, 256) if u < IMG_UNITS else (NS, 4 * NK)
                act.wait_ge(s_sub, parts_by(u))
                A(sx[0:P, u % 3, 0:w], sx[0:P, u % 3, 0:w], ACT.Exp).then_inc(s_exp, 1)

            def turned(u):
                act.wait_ge(t_ps, u + 1)
                if u >= 2:
                    act.wait_ge(o1_ps, u - 1)
                if u < IMG_UNITS:
                    A(pT[:, u % 2, 0:256], PS[:, 4 + u % 2, 0:256], ACT.Copy).then_inc(t_act, 1)
                else:
                    A(pT[:, u % 2, 0:2 * NS], PS[:, 4 + u % 2, 0:2 * NS], ACT.Copy).then_inc(t_act, 1)
                    A(pT[0:NS, u % 2, 2 * NS:6 * NS], PS[0:NS, 4 + u % 2, 2 * NS:6 * NS], ACT.Copy).then_inc(t_act, 1)

            for u in range(STEPS):
                if u < AFTER_UNITS:
                    probs(u)
                if 2 <= u < AFTER_UNITS + 2:
                    turned(u - 2)
                if u in TURN_AT:
                    kind, b = TURN_AT[u]
                    where, dst = ((BOFF[b], BROWS[b]), attT1) if kind == "att" else (b, xnT)
                    tp_evac(TP_ATT1 + TURNS.index((kind, b)), where, dst, 4 + (u + 1) % 2)
            def shared(n):
                N = CHUNK[n // HT][1]
                act.wait_ge(u_ps, n + 1)
                if n >= 2:
                    act.wait_ge(g_out, n - 1)
                A(sa[:, n % 2, 0:N], PS[:, 2 * (n % 2), 0:N], ACT.Silu).then_inc(u_act, 1)

            shared(0)
            for t in TILES[NORMED:]:
                tp_evac(TP_XN3 + t - NORMED, t, xnT)
            route_exp(1)
            for n in range(1, 3 * HT):
                shared(n)
            slots(1)

        @block.vector
        def _(dve):
            V = nc.vector
            steps, norms = [0], [0]

            def step(ins):
                steps[0] += 1
                ins.then_inc(dve_step, 1)
                dve.wait_ge(dve_step, steps[0])

            def tile_stats(tiles, src, ready):
                P = ROWS[tiles[0]]
                for t in tiles:
                    ready(t)
                    steps[0] += 1
                    V.bn_stats(bnst[0:P, t, :], src[0:P, t, :]).then_inc(dve_step, 1)
                dve.wait_ge(dve_step, steps[0])
                for t in tiles:
                    steps[0] += 1
                    V.bn_aggr(mv[0:P, t, :], bnst[0:P, t, :]).then_inc(dve_step, 1)

            def ln_power(tiles):
                P, t0, n = ROWS[tiles[0]], tiles[0], len(tiles)
                dve.wait_ge(dve_step, steps[0])
                V.tensor_scalar(rstd[0:P, 0, t0:t0 + n], mv[0:P, t0:t0 + n, 1], EPS, None, ALU.add).then_inc(var_in, 1)

            def ln_stats(tiles, src, ready):
                tile_stats(tiles, src, ready)
                ln_power(tiles)

            def tile_scale(tiles, src, done):
                P = ROWS[tiles[0]]
                for t in tiles:
                    V.tensor_scalar(xn[0:P, t, :], src[0:P, t, :], mv[0:P, t, 0:1], rstd[0:P, 1, t:t + 1],
                                    ALU.subtract, ALU.mult).then_inc(done, 1)

            def ln_scale(tiles, src, done):
                norms[0] += 1
                dve.wait_ge(rs_out, norms[0])
                tile_scale(tiles, src, done)

            def layernorm(chunks, src, ready, done, scaled=lambda tiles: None):
                tiles = [c[2] for c in chunks]
                ln_stats(tiles[0], src, ready)
                for n in range(len(tiles)):
                    if n + 1 < len(tiles):
                        ln_stats(tiles[n + 1], src, ready)
                    ln_scale(tiles[n], src, done)
                    scaled(tiles[n])

            dve.wait_ge(ld_ids, 16)
            for k, size in enumerate((VOCAB, NSEG)):
                own = slice(TT * k, TT * k + TT)
                step(V.tensor_scalar(idx[:, 0, own], ids[:, own], 0.0, float(size), ALU.is_lt, ALU.mult))
                step(V.tensor_tensor(out=idx[:, 1, own], in0=idx[:, 0, own], in1=ids[:, own], op=ALU.add))
                V.tensor_scalar(idx[:, 2, own], idx[:, 1, own], 0.0, float(size - 1), ALU.max, ALU.min).then_inc(idx_set, 1)
            dve.wait_ge(ld_tokc, 48)
            for g in range(1, NG):
                dve.wait_ge(ld_w[g], 16)
                for j in range(NJ):
                    if g == 1:
                        dve.wait_ge(fold0, j + 1)
                    else:
                        dve.wait_ge(folded, NJ * (g - 2) + j + 1)
                    V.scalar_tensor_tensor(out=weff[:, j, 0:C], in0=wt[:, g, j, :], scalar=gb[:, 0, g, j:j + 1],
                                           in1=weff[:, j, 0:C], op0=ALU.mult, op1=ALU.add).then_inc(folded, 1)
            dve.wait_ge(ld_const, 32)
            dve.wait_ge(gathered, 32 * TT)
            for P, b in ((128, slice(0, TT - 1)), (ROWS[-1], slice(TT - 1, TT))):
                step(V.tensor_tensor(out=seg[0:P, b], in0=seg[0:P, b], in1=pos[0:P, b], op=ALU.add))
                t = slice(IT + b.start, IT + b.stop)
                V.tensor_tensor(out=H[0:P, t, :], in0=H[0:P, t, :], in1=seg[0:P, b], op=ALU.add).then_inc(text_h, 1)
            layernorm(CHUNK[1:], H, lambda t: dve.wait_ge(text_h, 2), xn_ready[0])
            dve.wait_ge(tok_ps, 2)
            step(V.tensor_scalar(tst[:, 0, :], PS[:, 0:IT, C], 1.0 / PDIM, None, ALU.mult))
            step(V.tensor_tensor(out=tst[:, 1, :], in0=tst[:, 0, :], in1=tst[:, 0, :], op=ALU.mult))
            step(V.scalar_tensor_tensor(out=tst[:, 2, :], in0=PS[:, 5, C:C + IT], scalar=1.0 / PDIM, in1=tst[:, 1, :],
                                        op0=ALU.mult, op1=ALU.subtract))
            V.tensor_scalar(rstd[:, 0, 0:IT], tst[:, 2, :], EPS, None, ALU.add).then_inc(var_in, 1)
            norms[0] += 1
            dve.wait_ge(rs_out, norms[0])
            step(V.scalar_tensor_tensor(out=tst[:, 4, :], in0=tst[:, 0, :], scalar=-1.0, in1=rstd[:, 1, 0:IT],
                                        op0=ALU.mult, op1=ALU.mult))
            dve.wait_ge(sg_sb, 1)
            for t in range(IT):
                step(V.scalar_tensor_tensor(out=H[:, t, :], in0=PS[:, t, 0:C], scalar=rstd[:, 1, t:t + 1],
                                            in1=sgbw[:, C:2 * C], op0=ALU.mult, op1=ALU.add))
                V.scalar_tensor_tensor(out=H[:, t, :], in0=sgbw[:, 0:C], scalar=tst[:, 4, t:t + 1],
                                       in1=H[:, t, :], op0=ALU.mult, op1=ALU.add).then_inc(tok_h, 1)

            layernorm(CHUNK[:1], H, lambda t: dve.wait_ge(tok_h, t + 1), xn_ready[0])

            def norm_rows(n):
                (off, N, _), s, h = QK[n]
                dve.wait_ge(nm_ps, n + 1)
                V.tensor_copy(qkaug[s][HC:HC + 6, h, off:off + N], PS[HC:HC + 6, 2 + n % 2, 0:N]).then_inc(nm_out, 1)
            for n, ((off, N, _), s, h) in enumerate(QK):
                dve.wait_ge(qk_ps, n + 1)
                V.tensor_copy(qkaug[s][0:HC, h, off:off + N], PS[0:HC, n % 2, 0:N]).then_inc(qk_aug, 1)
                if n >= 1:
                    norm_rows(n - 1)
            norm_rows(len(QK) - 1)

            dve.wait_ge(kv_zero, 1)
            for n in range(2 * B):
                b, y = n // 2, n % 2
                dve.wait_ge(kv_ps, n + 1)
                src = PS[:, 4 + y, 0:3 * 4 * PAIR].rearrange("p (r e) -> p r e", r=3)
                for rows, c0 in ((slice(0, 64), 0), (slice(64, 128), 17)):
                    V.tensor_copy(kv[rows, b, 3 * y:3 * y + 3, c0:c0 + 17], src[rows, :, c0:c0 + 17]).then_inc(kv_out, 1)

            def divide0(n):
                P = BROWS[n]
                dve.wait_ge(o0_ps, n + 1)
                o = PS[0:P, n % 2, 0:12 * PAIR].rearrange("p (r e) -> p r e", r=6)[:, :, 0:PAIR].rearrange("p r (z e) -> p r z e", z=2)
                norm, inverse = (rec[0:P, k, :].rearrange("p (r z) -> p r z", z=2) for k in range(2))
                step(V.tensor_scalar(norm, o[:, :, :, DH], float(M) * 1e-6, None, ALU.add))
                step(V.reciprocal(inverse, norm))
                V.tensor_tensor(out=att0b[0:P, n, :].rearrange("p (r z e) -> p r z e", r=6, z=2), in0=o[:, :, :, 0:DH],
                                in1=inverse.unsqueeze(3).broadcast_to([P, 6, 2, DH]), op=ALU.mult).then_inc(att0, 1)

            def projected0(t):
                P = ROWS[t]
                dve.wait_ge(y0_ps, t + 1)
                V.tensor_tensor(out=xn[0:P, t, :], in0=PS[0:P, 2 + t % 2, 0:C], in1=xn[0:P, t, :], op=ALU.add).then_inc(y0_out, 1)

            def affine(tiles):
                P, ts = ROWS[tiles[0]], slice(tiles[0], tiles[0] + len(tiles))
                dve.wait_ge(yn, tiles[-1] + 1)
                step(V.tensor_tensor(out=xn[0:P, ts, :], in0=xn[0:P, ts, :],
                                     in1=rows3[0:P, 1, :].unsqueeze(1).broadcast_to([P, len(tiles), C]), op=ALU.mult))
                for t in tiles:
                    V.tensor_tensor(out=H[0:P, t, :], in0=H[0:P, t, :], in1=xn[0:P, t, :], op=ALU.add).then_inc(h1, 1)

            def y_in(t):
                dve.wait_ge(y0_out, t + 1)

            def h_in(t):
                dve.wait_ge(h1, t + 1)

            dve.wait_ge(xnb, NT)
            dve.wait_ge(hb, NT)
            t, image_at = 0, None
            for n in range(NB):
                divide0(n)
                while t < NT and NEED[t] + 3 <= n:
                    projected0(t)
                    t += 1
                    image_at = n if t == IT else image_at
                if t >= IT:
                    tiles = CHUNK[0][2]
                    if n == image_at:
                        ln_stats(tiles, xn, y_in)
                    elif n == image_at + 1:
                        ln_scale(tiles, xn, yn)
                        affine(tiles)
                    elif n == image_at + 2:
                        ln_stats(tiles, H, h_in)
                    elif n == image_at + 3:
                        ln_scale(tiles, H, xn_ready[1])
            early = [4, 5]
            for last, part in ((5, lambda: ln_stats(early, xn, y_in)), (6, lambda: (ln_scale(early, xn, yn), affine(early))),
                               (7, lambda: ln_stats(early, H, h_in)), (8, lambda: ln_scale(early, H, xn_ready[1]))):
                while t <= last:
                    projected0(t)
                    t += 1
                part()
            late = [(0, 0, tiles) for tiles in LATE]
            layernorm(late, xn, y_in, yn, affine)

            def bc(ap):
                return ap.unsqueeze(2).broadcast_to([128, NT, NE])

            def route_softmax(k):
                dve.wait_ge(lg_ps[k], 1)
                dve.wait_ge(lg_set, 1)
                dve.wait_ge(ld_moe, 48)
                step(V.tensor_copy(lg[:, 0:NT - 1, :], PS[:, 4, 0:(NT - 1) * NE].rearrange("p (t e) -> p t e", t=NT - 1)))
                step(V.tensor_copy(lg[0:ROWS[-1], NT - 1, :], PS[0:ROWS[-1], 4, (NT - 1) * NE:NT * NE]))
                step(V.tensor_reduce(out=rs[:, 0, :], in_=lg[:], axis=AX, op=ALU.max))
                V.tensor_tensor(out=rt[:, 0], in0=lg[:], in1=bc(rs[:, 0, :]), op=ALU.subtract).then_inc(rt_in[k], 1)
                dve.wait_ge(rt_exp[k], 1)
                step(V.tensor_reduce(out=rs[:, 1, :], in_=rt[:, 0], axis=AX, op=ALU.add))
                step(V.reciprocal(rs[:, 2, :], rs[:, 1, :]))
                if k == 0:
                    V.tensor_tensor(out=rt[:, 1], in0=rt[:, 0], in1=bc(rs[:, 2, :]), op=ALU.mult).then_inc(imp_in, 1)
                    dve.wait_ge(imp_in, 1)
                else:
                    step(V.tensor_tensor(out=rt[:, 1], in0=rt[:, 0], in1=bc(rs[:, 2, :]), op=ALU.mult))

            def route_pick(k):
                rk = rank[:].unsqueeze(1).broadcast_to([128, NT, NE])
                for pick, src in ((2, 1), (3, 0)):
                    step(V.tensor_reduce(out=rs[:, 3, :], in_=rt[:, src], axis=AX, op=ALU.max))
                    step(V.tensor_tensor(out=rt[:, 4], in0=rt[:, src], in1=bc(rs[:, 3, :]), op=ALU.is_equal))
                    step(V.tensor_tensor(out=rt[:, 5], in0=rt[:, 4], in1=rk, op=ALU.mult))
                    step(V.tensor_reduce(out=rs[:, 4, :], in_=rt[:, 5], axis=AX, op=ALU.max))
                    step(V.tensor_tensor(out=rt[:, pick], in0=rk, in1=bc(rs[:, 4, :]), op=ALU.is_equal))
                    if pick == 2:
                        step(V.scalar_tensor_tensor(out=rt[:, 0], in0=rt[:, 2], scalar=-2.0, in1=rt[:, 1],
                                                    op0=ALU.mult, op1=ALU.add))
                V.tensor_tensor(out=rt[:, 4], in0=rt[:, 2], in1=rt[:, 3], op=ALU.add).then_inc(sel_in[k], 1)
                dve.wait_ge(sel_in[k], 1)

            def by_expert(ap):
                return ap.rearrange("p (e t) -> p e t", e=NE)

            def route_place(k):
                dve.wait_ge(rank_ps[k], 1)
                step(V.tensor_copy(by_expert(cnt[:, 0, :]), PS[:, 7, NE * NT:2 * NE * NT].rearrange("p (t e) -> p e t", t=NT)))
                step(V.tensor_tensor_scan(cnt[:, 1, :], routec[:, 0:NE * NT], cnt[:, 0, :], 0.0, ALU.mult, ALU.add))
                total = by_expert(cnt[:, 1, :])[:, :, NT - 1]
                c0 = NE * NT + NE
                steps_m = rt[:, 5].rearrange("p t e -> p (t e)")[:, 0:NE * MAXT].rearrange("p (e m) -> p e m", e=NE)
                step(V.tensor_tensor(out=steps_m, in0=total.unsqueeze(2).broadcast_to([128, NE, MAXT]),
                                     in1=routec[:, c0:c0 + NE * MAXT].rearrange("p (e m) -> p e m", e=NE), op=ALU.is_gt))
                step(V.tensor_reduce(out=tiles_of[:, 0, :], in_=steps_m, axis=AX, op=ALU.add))
                step(V.tensor_tensor_scan(tiles_of[:, 1, :], routec[:, NE * NT:c0], tiles_of[:, 0, :], 0.0, ALU.mult, ALU.add))
                step(V.tensor_tensor(out=tiles_of[:, 2, :], in0=tiles_of[:, 1, :], in1=tiles_of[:, 0, :], op=ALU.subtract))
                step(V.tensor_tensor(out=cnt[:, 2, :], in0=cnt[:, 1, :], in1=cnt[:, 0, :], op=ALU.subtract))
                step(V.scalar_tensor_tensor(out=by_expert(cnt[:, 3, :]), in0=tiles_of[:, 2, :].unsqueeze(2).broadcast_to([128, NE, NT]),
                                            scalar=float(CAP), in1=by_expert(cnt[:, 2, :]), op0=ALU.mult, op1=ALU.add))
                step(V.tensor_tensor(out=rt[:, 0], in0=PS[:, 7, 0:NE * NT].rearrange("p (t e) -> p t e", t=NT),
                                     in1=cnt[:, 3, :].rearrange("p (e t) -> p t e", e=NE), op=ALU.add))
                for c in range(2):
                    step(V.tensor_tensor(out=rt[:, 5], in0=rt[:, 0], in1=rt[:, 2 + c], op=ALU.mult))
                    step(V.tensor_reduce(out=rs[:, 3 + c, :], in_=rt[:, 5], axis=AX, op=ALU.add))
                    V.tensor_copy(place[:, c, :], rs[:, 3 + c, :]).then_inc(placed[k], 1)
                step(V.tensor_tensor(out=eidf[:], in0=routec[0:1, c0 + NE * MAXT:c0 + NE * MAXT + NSLOT].unsqueeze(2).broadcast_to([1, NSLOT, NE]),
                                     in1=tiles_of[0:1, 1, :].unsqueeze(1).broadcast_to([1, NSLOT, NE]), op=ALU.is_ge))
                step(V.tensor_reduce(out=eids[:], in_=eidf[:], axis=AX, op=ALU.add))
                V.tensor_scalar(eid[:], eids[:], float(NE - 1), float(ES[k]), ALU.min, ALU.mult).then_inc(placed[k], 1)

            def number_rows(k):
                V.tensor_copy(xnd[:, :, C], token).then_inc(rows_set[k], 1)

            def second_rows(k, half):
                ts = (slice(0, SENT_A), slice(SENT_A, NT))[half]
                dve.wait_ge((sent_a, sent_b)[half][k], 16 * (ts.stop - ts.start))
                V.tensor_scalar(xnd[:, ts, C], token[:, ts], float(CHOICE), None, ALU.add).then_inc(rows_set[k], 1)

            def route_weights(k):
                if k == 0:
                    dve.wait_ge(imp_ps, 1)
                    V.tensor_reduce(out=run[:, 0, :], in_=PS[:, 5, 0:NT * NE].rearrange("p (t e) -> p e t", t=NT),
                                    axis=AX, op=ALU.add).then_inc(imp_read, 1)
                    dve.wait_ge(imp_read, 1)
                    step(V.tensor_scalar(run[:, 1, :], run[:, 0, :], 1.0, 0.1, ALU.subtract, ALU.mult))
                    step(V.tensor_scalar(run[:, 2, :], run[:, 1, :], 1.0, 0.01, ALU.add, ALU.add))
                    step(V.reciprocal(run[:, 0, :], run[:, 2, :]))
                    step(V.tensor_tensor(out=rt[:, 1], in0=rt[:, 1], in1=run[:, 0, :].unsqueeze(1).broadcast_to([128, NT, NE]),
                                         op=ALU.mult))
                for c in range(2):
                    step(V.tensor_tensor(out=rt[:, 5], in0=rt[:, 1], in1=rt[:, 2 + c], op=ALU.mult))
                    step(V.tensor_reduce(out=cw[:, c, :], in_=rt[:, 5], axis=AX, op=ALU.add))
                step(V.tensor_tensor(out=cw[:, 2, :], in0=cw[:, 0, :], in1=cw[:, 1, :], op=ALU.add))
                if k == 1:
                    step(V.tensor_scalar(cw[:, 2, :], cw[:, 2, :], 1e-20, None, ALU.add))
                step(V.reciprocal(rs[:, 5, :], cw[:, 2, :]))
                for c in range(2):
                    step(V.tensor_tensor(out=cw[:, c, :], in0=cw[:, c, :], in1=rs[:, 5, :], op=ALU.mult))

            def gate(k, j, z):
                dve.wait_ge(up_act[k], j + 1)
                V.tensor_tensor(out=hact[:, z, :], in0=hact[:, z, :], in1=PS[:, 2 * z + 1, :], op=ALU.mult).then_inc(up_sb[k], 1)

            def turned_hidden(k, j, z):
                dve.wait_ge(ht_ps[k], j + 1)
                if not isinstance(j, int) or j >= 2:
                    dve.wait_ge(dn_ps[k], j - 1)
                V.tensor_copy(hT[:, z].rearrange("p i n -> p (i n)"), PS[:, 4 + z, :]).then_inc(ht_sb[k], 1)

            def slots(k):
                for s in range(-1, 2):
                    if k == 1:
                        gate(k, s + 1, (s + 1) % 2)
                    if s >= 0:
                        turned_hidden(k, s, s % 2)
                with dve.Fori(0, PAIRS) as i:
                    for z in range(2):
                        s = PIPE0 + 2 * i + z
                        if k == 1:
                            gate(k, s + 1, 1 - z)
                        turned_hidden(k, s, z)
                for s in range(PIPE0 + 2 * PAIRS, NSLOT):
                    if k == 1 and s + 1 <= LAST:
                        gate(k, s + 1, (s + 1) % 2)
                    turned_hidden(k, s, s % 2)

            def combine(k, tiles):
                for c in range(2):
                    for n, t in enumerate(tiles):
                        P = ROWS[t]
                        if c == 0:
                            dve.wait_ge(back[k][t], 16)
                        else:
                            dve.wait_ge(added[k], 2 * tiles[0] + n + 1)
                        V.scalar_tensor_tensor(out=H[0:P, t, :], in0=yback[0:P, c, t, :], scalar=cw[0:P, c, t:t + 1],
                                               in1=H[0:P, t, :], op0=ALU.mult, op1=ALU.add).then_inc(added[k], 1)

            def combine_and_wait(t):
                for _, _, tiles in CHUNK:
                    if t == tiles[0]:
                        combine(0, tiles)
                    if t in tiles:
                        dve.wait_ge(added[0], 2 * tiles[0] + len(tiles) + t - tiles[0] + 1)

            layernorm(late, H, h_in, xn_ready[1])
            dve.wait_ge(ld_moe, 48)
            number_rows(0)
            route_softmax(0)
            route_pick(0)
            route_place(0)
            route_weights(0)
            second_rows(0, 0)
            second_rows(0, 1)
            slots(0)

            layernorm(CHUNK, H, combine_and_wait, xn_ready[2])
            dve.wait_ge(ld_a1, 64)
            for c, (off, N, _) in enumerate(CHUNK1):
                for h in range(2):
                    dve.wait_ge(q1_ps, 4 * c + 2 + h + 1)
                    bs, ks = (slice(0, B), slice(0, NP_)) if c == 0 else (slice(4 * c - 4, 4 * c), slice(NP_, NK))
                    dst = kT1[:, h, :].rearrange("p (b n) -> p b n", b=B)[:, bs, ks]
                    V.tensor_copy(dst, PS[0:HC, 2 + h, 0:N].rearrange("p (b n) -> p b n", n=ks.stop - ks.start)).then_inc(q1_dve, 1)

            def scores_out(u):
                P, parts, w = (128, 1, NP_) if u < IMG_UNITS else (NS, 2, NK)
                dve.wait_ge(s_ps, u + 1)
                b0 = 2 * (u % 2)
                src = PS[0:P, b0:b0 + 2, 0:2 * w].rearrange("p a (h e) -> p a h e", e=w)
                if u >= 2:
                    dve.wait_ge(s_sub, parts_by(u - 2))
                m = mx[0:P, u % 2].rearrange("p (a h) -> p a h", a=2)
                step(V.tensor_reduce(out=m, in_=src, axis=AX, op=ALU.max))
                if u >= 3:
                    dve.wait_ge(t_ps, u - 2)
                for c0, k0, n in ((0, 0, NP_), (4 * NP_, NP_, NS))[0:parts]:
                    V.tensor_tensor(out=sx[0:P, u % 3, c0:c0 + 4 * n].rearrange("p (a h e) -> p a h e", a=2, e=n),
                                    in0=src[:, :, :, k0:k0 + n], in1=m.unsqueeze(3).broadcast_to([P, 2, 2, n]),
                                    op=ALU.subtract).then_inc(s_sub, 1)

            def divide(u):
                t, b, v = UNITS[u]
                dve.wait_ge(o1_ps, u + 1)
                P, tile = (128, t) if t is not None else (NS, IT + b)
                o = PS[0:P, 6 + u % 2, 0:4 * 17].rearrange("p (y z e) -> p y z e", y=2, z=2)
                r = rec[0:P, u % 2, 0:4].rearrange("p (y z) -> p y z", y=2)
                if u >= 2:
                    dve.wait_ge(att1, u - 1)
                step(V.reciprocal(r, o[:, :, :, DH]))
                dst = att1b[0:P, tile, 64 * v:64 * v + 64].rearrange("p (y z e) -> p y z e", y=2, z=2)
                V.tensor_tensor(out=dst, in0=o[:, :, :, 0:DH], in1=r.unsqueeze(3).broadcast_to([P, 2, 2, DH]),
                                op=ALU.mult).then_inc(att1, 1)

            def h3_in(t):
                dve.wait_ge(h3, t + 1)

            for u in range(STEPS):
                if u < AFTER_UNITS:
                    scores_out(u)
                if 3 <= u < AFTER_UNITS + 3:
                    divide(u - 3)
                if u in STATS_AT:
                    tile_stats([STATS_AT[u]], H, h3_in)
                if u in POWER_AT:
                    ln_power(POWER_AT[u])
                if u in SCALE_AT:
                    if SCALE_AT[u] in [tiles[0] for tiles in POWER_AT.values()]:
                        norms[0] += 1
                        dve.wait_ge(rs_out, norms[0])
                    tile_scale([SCALE_AT[u]], H, xn_ready[3])
                if u in PROJECT_AT:
                    t = PROJECT_AT[u]
                    P = ROWS[t]
                    dve.wait_ge(y1_ps, t + 1)
                    V.tensor_tensor(out=H[0:P, t, :], in0=PS[0:P, 6 + u % 2, 0:C], in1=H[0:P, t, :], op=ALU.add).then_inc(h3, 1)
            layernorm([(0, 0, tiles) for tiles in LATE], H, h3_in, xn_ready[3])

            def gate_shared(s, first=0, count=HT):
                N = CHUNK[s][1]
                for n in range(HT * s + first, HT * s + first + count):
                    dve.wait_ge(u_act, n + 1)
                    V.tensor_tensor(out=shT[:, s, n % HT, 0:N], in0=sa[:, n % 2, 0:N], in1=PS[:, 2 * (n % 2) + 1, 0:N],
                                    op=ALU.mult).then_inc(g_out, 1)

            def add_shared(s):
                for t in CHUNK[s][2]:
                    P = ROWS[t]
                    dve.wait_ge(ysh_ps, t + 1)
                    V.tensor_tensor(out=H[0:P, t, :], in0=PS[0:P, 4 + t % 2, 0:C], in1=H[0:P, t, :], op=ALU.add).then_inc(ysh_acc, 1)

            number_rows(1)
            route_softmax(1)
            route_pick(1)
            gate_shared(0, 0, 1)
            route_place(1)
            gate_shared(0, 1, HT - 1)
            second_rows(1, 0)
            gate_shared(1, 0, 1)
            second_rows(1, 1)
            gate_shared(1, 1, HT - 1)
            route_weights(1)
            add_shared(0)
            gate_shared(2)
            add_shared(1)
            add_shared(2)
            slots(1)
            for t in range(0, NT, 3):
                combine(1, TILES[t:t + 3])

        @block.tensor
        def _(pe):
            mm = nc.tensor.matmul

            def turn(n, t, src, rows=None, bank=None):
                if bank is not None:
                    pass
                elif n >= 2:
                    pe.wait_ge(tp_out, n - 1)
                P = rows or ROWS[t]
                for h in range(2):
                    last = nc.tensor.transpose(PS[0:HC, 6 + n % 2 if bank is None else bank, 128 * h:128 * h + P], src[0:P, t, h * HC:(h + 1) * HC],
                                               ident[0:P, 0:P])
                last.then_inc(tp_ps, 1)

            pe.wait_ge(ld_tokc, 48)
            for t in range(IT):
                pe.wait_ge(x2_done, t + 1)
                for j in range(NJ):
                    last = mm(PS[:, 5, C + t:C + t + 1], x2[:, j, 128 * t:128 * t + 128], mult[:, j:j + 1],
                              start=(j == 0), stop=(j == NJ - 1))
            last.then_inc(tok_ps, 1)
            pe.wait_ge(ones_set, 1)
            pe.wait_ge(folded, NJ * (NG - 1))
            for j in range(NJ):
                mm(PS[:, 4, 0:C], ones[0:KP, :], weff[:, j, 0:C], start=(j == 0), stop=(j == NJ - 1))
            pe.wait_ge(ld_x, 16)
            pe.wait_ge(mult_set, 1)
            for j in range(NJ):
                for t in range(IT):
                    last = mm(PS[:, t, 0:C + 1], xT[:, j, 128 * t:128 * t + 128], weff[:, j, :], start=(j == 0), stop=(j == NJ - 1))
            last.then_inc(tok_ps, 1)
            pe.wait_ge(beta_sum, NG - 1)
            for j in range(NJ):
                mm(PS[:, 4, C:2 * C], ones[0:KP, :], betaw[:, 0, j, :], start=(j == 0), stop=False)
            mm(PS[:, 4, C:2 * C], ones[0:1, :], tokb[:], start=False, stop=True).then_inc(tok_ps, 1)

            def turn_first(ns):
                for n in ns:
                    pe.wait_ge(xn_ready[0], n + 1)
                    turn(TP_XN0 + n, TILES_TF[n], xn)

            pe.wait_ge(ld_const, 32)
            turn_first(range(TT))

            pe.wait_ge(ld_a0, 80)
            pe.wait_ge(tok_h, IT)

            def norms(n):
                (off, N, _), s, h = QK[n]
                pe.wait_ge(qk_sq, n + 1)
                if n >= 2:
                    pe.wait_ge(nm_out, n - 1)
                mm(PS[HC:HC + 6, 2 + n % 2, 0:N], nb6[:], sq[:, n % 2, 0:N], start=True, stop=True).then_inc(nm_ps, 1)
            for n, ((off, N, _), s, h) in enumerate(QK):
                if n == 8:
                    turn_first(range(TT, NT))
                pe.wait_ge(tp_out, TP_XN0 + (4, 5, 9)[n // 4])
                if n >= 2:
                    pe.wait_ge(qk_aug, n - 1)
                for c in range(2):
                    last = mm(PS[0:HC, n % 2, 0:N], wqkv[:, c, s * C + h * HC:s * C + (h + 1) * HC], xnT[:, c, off:off + N],
                              start=(c == 0), stop=(c == 1))
                last.then_inc(qk_ps, 1)
                if n >= 1:
                    norms(n - 1)
            norms(len(QK) - 1)
            for n, t in enumerate(BTILES):
                if n >= 2:
                    pe.wait_ge(v_out, n - 1)
                for c in range(2):
                    last = mm(PS[0:BROWS[t], 4 + n % 2, 0:C], xnT[:, c, BOFF[t]:BOFF[t] + BROWS[t]], wqkv[:, c, 2 * C:3 * C],
                              start=(c == 0), stop=(c == 1))
                last.then_inc(v_ps, 1)
            pe.wait_ge(nm_out, len(QK))
            for n, (kind, r) in enumerate(PHI):
                b0 = 2 * (n % 2)
                if n >= 2:
                    pe.wait_ge(ph_out, n - 1)
                for u in range(2):
                    if kind == "k":
                        last = mm(PS[0:BROWS[r], b0 + u, 0:384], qkaug[1][:, u, BOFF[r]:BOFF[r] + BROWS[r]], bd[:], start=True, stop=True)
                    elif kind == "qt":
                        off, N = IT * 128 + 4 * NS * u, 4 * NS
                        last = mm(PS[:, b0 + u, 0:N], bd[:, (r % 3) * 128:(r % 3) * 128 + 128], qkaug[0][:, r // 3, off:off + N],
                                  start=True, stop=True)
                    else:
                        r2 = 2 * r + u
                        last = mm(PS[:, b0 + u, :], bd[:, (r2 % 3) * 128:(r2 % 3) * 128 + 128], qkaug[0][:, r2 // 3, 0:512],
                                  start=True, stop=True)
                last.then_inc(ph_ps, 1)
            pe.wait_ge(v_out, NB)
            pe.wait_ge(ph_out, NB)
            for n in range(2 * B):
                b, y = n // 2, n % 2
                if n >= 2:
                    pe.wait_ge(kv_out, 2 * (n - 1))
                p0 = 64 * (b % 2)
                for r in range(3):
                    o, f, h = PS[:, 4 + y, 3 * PAIR * r:3 * PAIR * (r + 1)], (3 * y + r) * 128, 6 * y
                    mm(o, kp[p0:p0 + 64, b // 2, f:f + 128], v0[p0:p0 + 64, b // 2, h:h + 6, :], start=True, stop=False)
                    last = mm(o, kp[0:NS, IT + b, f:f + 128], v0[0:NS, IT + b, h:h + 6, :], start=False, stop=True)
                last.then_inc(kv_ps, 1)
            pe.wait_ge(ph_out, len(PHI))
            pe.wait_ge(kv_out, 4 * B)

            def products(n):
                t = n
                if n >= 2:
                    pe.wait_ge(att0, n - 1)
                parts = [(0, 64, 2 * t, BOFF[t]), (64, 64, 2 * t + 1, BOFF[t] + 64)] if t < IT else [(0, NS, t - IT, BOFF[t])]
                for p0, P, b, off in parts:
                    for r in range(6):
                        k0 = (6 * b + r) * PAIR
                        last = mm(PS[p0:p0 + P, n % 2, 2 * r * PAIR:2 * (r + 1) * PAIR], qp[:, r, off:off + P],
                                  kv_flat[:, k0:k0 + 2 * PAIR], start=True, stop=True)
                last.then_inc(o0_ps, 1)

            def project0(t):
                P = ROWS[t]
                pe.wait_ge(tp_out, TP_ATT0 + NEED[t])
                if t >= 2:
                    pe.wait_ge(y0_out, t - 1)
                for c in range(2):
                    last = mm(PS[0:P, 2 + t % 2, 0:C], attT0[:, c, OFF[t]:OFF[t] + P], wproj0[:, c, :], start=(c == 0), stop=(c == 1))
                last.then_inc(y0_ps, 1)

            t = 0
            for n in range(NB + 2):
                if n < NB:
                    products(n)
                if n >= 2:
                    pe.wait_ge(att0, n - 1)
                    turn(TP_ATT0 + n - 2, n - 2, att0b, BROWS[n - 2])
                    while t < NT and NEED[t] + 2 <= n:
                        project0(t)
                        t += 1
            while t < NT:
                project0(t)
                t += 1

            def logits(k, base, turned):
                def route(t):
                    pe.wait_ge(tp_out, base + t - turned + 1)
                    for c in range(2):
                        last = mm(PS[0:ROWS[t], 4, t * NE:(t + 1) * NE], xnT[:, c, OFF[t]:OFF[t] + ROWS[t]], rw[:, k, c, :],
                                  start=(c == 0), stop=(c == 1))
                    if t == NT - 1:
                        last.then_inc(lg_ps[k], 1)
                pe.wait_ge(ld_moe, 48)
                for t in range(turned - 1):
                    route(t)
                for t in TILES[turned:]:
                    pe.wait_ge(xn_ready[1 + 2 * k], t + 1)
                    turn(base + t - turned, t, xn)
                    if t >= 1:
                        route(t - 1)
                route(NT - 1)

            def summed(bank, col, rows, src, last_sem):
                P, m = ROWS[-1], (NT - 1) * NE
                mm(PS[:, bank, col:col + m], rows, src[:, 0:NT - 1, :], start=True, stop=True)
                last = mm(PS[:, bank, col + m:col + NT * NE], rows[0:P, :], src[0:P, NT - 1, :], start=True, stop=True)
                if last_sem is not None:
                    last.then_inc(last_sem, 1)

            def ranks(k):
                pe.wait_ge(sel_in[k], 1)
                summed(7, 0, tri, rt[:, 4], None)
                summed(7, NE * NT, ones[:], rt[:, 4], rank_ps[k])

            def expert(k, j):
                return pe.value_load(eid[0:1, bass.ds(j, 1)], min_val=0, max_val=(NE - 1) * ES[k])

            def turn_rows(k, j, z, round_):
                pe.wait_ge(xs_in[k][z], 16 * round_ + 16)
                if not isinstance(j, int) or j >= 1:
                    pe.wait_ge(xt_sb[k], j)
                for c in range(2):
                    last = nc.tensor.transpose(PS[0:HC, 6, 128 * c:128 * c + 128], xs[:, z, c * HC:(c + 1) * HC], ident[:])
                last.then_inc(xt_ps[k], 1)

            def up(k, j, z, e=None):
                pe.wait_ge(xt_sb[k], j + 1)
                if not isinstance(j, int) or j >= 2:
                    pe.wait_ge((up_act, up_sb)[k][k], j - 1)
                e = expert(k, j) if e is None else e
                for q in range(1 + k):
                    bank = 2 * z + q if k else z
                    for c in range(2):
                        w = arena[0:HC, bass.ds(e + (WBASE[k] + (2 * q + c) * HID), HID)]
                        last = mm(PS[:, bank, :], xsT[:, z, c, :], w, start=(c == 0), stop=(c == 1))
                last.then_inc(up_ps[k], 1)

            def turn_hidden(k, j, z):
                pe.wait_ge((up_act, up_sb)[k][k], j + 1)
                if not isinstance(j, int) or j >= 2:
                    pe.wait_ge(ht_sb[k], j - 1)
                for it in range(HT):
                    last = nc.tensor.transpose(PS[:, 4 + z, 128 * it:128 * it + 128], hact[:, z, 128 * it:128 * it + 128], ident[:])
                last.then_inc(ht_ps[k], 1)

            def down(k, j, z, e=None):
                pe.wait_ge(ht_sb[k], j + 1)
                if not isinstance(j, int) or j >= 1:
                    pe.wait_ge(dn_sb[k], j)
                e = expert(k, j) if e is None else e
                for it in range(HT):
                    w = arena[:, bass.ds(e + (WBASE[k] + 2 * HID * (1 + k) + it * C), C)]
                    last = mm(PS[:, 7, 0:C], hT[:, z, it, :], w, start=(it == 0), stop=(it == HT - 1))
                last.then_inc(dn_ps[k], 1)

            def first_experts(k):
                pe.wait_ge(placed[k], 3)
                return [expert(k, j) for j in range(3)]

            def slots(k, first):
                turn_rows(k, 0, 0, 0)
                pe.wait_ge(ld_e[k], 32 * NE)
                up(k, 0, 0, first[0])
                turn_rows(k, 1, 1, 0)
                up(k, 1, 1, first[1])
                turn_rows(k, 2, 0, 1)
                turn_hidden(k, 0, 0)
                up(k, 2, 0, first[2])
                turn_rows(k, 3, 1, 1)
                down(k, 0, 0, first[0])
                turn_hidden(k, 1, 1)
                with pe.Fori(0, PAIRS) as i:
                    for z in range(2):
                        s = PIPE0 + 2 * i + z
                        up(k, s + 1, 1 - z)
                        turn_rows(k, s + 2, z, i + 2)
                        down(k, s - 1, 1 - z)
                        turn_hidden(k, s, z)
                for s in range(PIPE0 + 2 * PAIRS, NSLOT + 1):
                    if s + 1 <= LAST:
                        up(k, s + 1, (s + 1) % 2)
                    if s + 2 <= LAST:
                        turn_rows(k, s + 2, s % 2, (s + 2) // 2)
                    down(k, s - 1, (s - 1) % 2)
                    if s <= LAST:
                        turn_hidden(k, s, s % 2)

            logits(0, TP_XN1, 0)
            pe.wait_ge(imp_in, 1)
            summed(5, 0, ones[:], rt[:, 1], imp_ps)
            ranks(0)
            pe.wait_ge(imp_read, 1)
            slots(0, first_experts(0))

            pe.wait_ge(ld_a1, 64)
            n, done = 0, 0
            for ci, (off, N, need) in enumerate(CHUNK1):
                for t in TILES[done:need]:
                    pe.wait_ge(xn_ready[2], t + 1)
                    turn(TP_XN2 + t, t, xn)
                done = need
                pe.wait_ge(tp_out, TP_XN2 + need)
                for s in range(2):
                    for h in range(2):
                        if ci >= 1:
                            if s == 0:
                                pe.wait_ge(q1_act, 2 * (ci - 1) + h + 1)
                            else:
                                pe.wait_ge(q1_dve, 2 * (ci - 1) + h + 1)
                        for c in range(2):
                            last = mm(PS[0:HC, n % 4, 0:N], wat[:, c, s * C + h * HC:s * C + (h + 1) * HC], xnT[:, c, off:off + N],
                                      start=(c == 0), stop=(c == 1))
                        last.then_inc(q1_ps, 1)
                        n += 1
            for n in range(2 * B):
                if n >= 2:
                    pe.wait_ge(v1_out, 2 * (n - 1) if n - 2 < B else B + n - 1)
                else:
                    pe.wait_ge(ht_sb[0], NSLOT)
                b, bank = n % B, PS[:, 4 + n % 2, :]
                parts = [(0, 64 * b, 64, 0, HC), (64, 64 * b, 64, HC, HC)] if n < B else [(0, BOFF[IT + b], NS, 0, C)]
                for p0, off, w, c0, N in parts:
                    for c in range(2):
                        last = mm(bank[p0:p0 + w, 0:N], xnT[:, c, off:off + w], wat[:, c, 2 * C + c0:2 * C + c0 + N],
                                  start=(c == 0), stop=(c == 1))
                last.then_inc(v1_ps, 1)

            def score(u, p0, P, x, qoff, k0, w):
                return mm(PS[p0:p0 + P, 2 * (u % 2) + x // 2, (x % 2) * w:(x % 2) * w + w], qT1[:, (2 * UNITS[u][2] + x // 2) // 3, qoff:qoff + P],
                          kown[:, u % 3, x, k0:k0 + w], start=False, stop=True, skip_group_check=True)

            def scores(u):
                t, b, v = UNITS[u]
                b0 = 2 * (u % 2)
                if u >= 2:
                    pe.wait_ge(s_sub, parts_by(u - 2))
                P, c0, w, m0, n = (128, 0, NP_, 0, NP_) if t is not None else (NS, NP_, NK, NP_, NS)
                for a in range(2):
                    mm(PS[0:P, b0 + a, 0:2 * w].rearrange("p (h e) -> p h e", h=2)[:, :, c0:], identb[0:P, 0:P],
                       cmask[0:P, m0:m0 + n].unsqueeze(1).broadcast_to([P, 2, n]), start=True, stop=False, skip_group_check=True)
                pe.wait_ge(own_set, 2 * u + 2)
                for x in range(4):
                    if t is not None:
                        for k in range(2):
                            last = score(u, 64 * k, 64, x, BOFF[t] + 64 * k, NP_ * k, NP_)
                    else:
                        last = score(u, 0, NS, x, BOFF[IT + b], 0, NK)
                last.then_inc(s_ps, 1)

            def turn_probs(u):
                pe.wait_ge(s_exp, u + 1)
                if u >= 2:
                    pe.wait_ge(t_act, parts_by(u - 2))
                if u + 1 in TURN_AT:
                    pe.wait_ge(tp_out, TP_ATT1 + TURNS.index(TURN_AT[u + 1]) + 1)
                bank = PS[:, 4 + u % 2, :]
                if u < IMG_UNITS:
                    for y in range(2):
                        last = nc.tensor.transpose(bank[:, 128 * y:128 * y + 128], sx[:, u % 3, 128 * y:128 * y + 128], ident[:])
                else:
                    for y in range(2):
                        nc.tensor.transpose(bank[:, NS * y:NS * y + NS], sx[0:NS, u % 3, 2 * NP_ * y:2 * NP_ * (y + 1)], ident[0:NS, 0:NS])
                    for x in range(4):
                        c0, k0 = NS * (2 + x), 4 * NP_ + NS * x
                        last = nc.tensor.transpose(bank[0:NS, c0:c0 + NS], sx[0:NS, u % 3, k0:k0 + NS], ident[0:NS, 0:NS])
                last.then_inc(t_ps, 1)

            def weigh(u):
                t, b, v = UNITS[u]
                pe.wait_ge(t_act, parts_by(u))
                if u == 0:
                    pe.wait_ge(tp_out, TP_XN2 + NT)
                elif u >= 2:
                    pe.wait_ge(att1, u - 1)
                if u + 2 in PROJECT_AT:
                    pe.wait_ge(h3, PROJECT_AT[u + 2] + 1)
                for y in range(2):
                    o = PS[:, 6 + u % 2, PAIR * y:PAIR * (y + 1)]
                    if t is not None:
                        for k in range(2):
                            c0 = 128 * y + 64 * k
                            last = mm(o[64 * k:64 * k + 64], pT[:, u % 2, c0:c0 + 64], vi[:, 2 * t + k, 2 * v + y, :], start=True, stop=True)
                    else:
                        mm(o[0:NS], pT[:, u % 2, NS * y:NS * y + NS], vi[:, b, 2 * v + y, :], start=True, stop=False,
                           skip_group_check=True)
                        for z in range(2):
                            c0 = NS * (2 + 2 * y + z)
                            last = mm(o[0:NS, 17 * z:17 * z + 17], pT[0:NS, u % 2, c0:c0 + NS], v1[0:NS, b, 4 * v + 2 * y + z, :],
                                      start=False, stop=True, skip_group_check=True)
                last.then_inc(o1_ps, 1)

            pe.wait_ge(masks_set, 2)
            pe.wait_ge(q1_act, 6)
            pe.wait_ge(v1_out, 3 * B)
            for u in range(STEPS):
                if u < AFTER_UNITS:
                    scores(u)
                if 2 <= u < AFTER_UNITS + 2:
                    turn_probs(u - 2)
                if 3 <= u < AFTER_UNITS + 3:
                    weigh(u - 3)
                if u in TURN_AT:
                    kind, b = TURN_AT[u]
                    if kind == "att":
                        pe.wait_ge(att1, 3 * b + 3)
                    else:
                        pe.wait_ge(xn_ready[3], b + 1)
                    n = TP_ATT1 + TURNS.index((kind, b))
                    pe.wait_ge(tp_out, n)
                    turn(n, b, att1b if kind == "att" else xn, BROWS[b] if kind == "att" else ROWS[b],
                         4 + (u + 1) % 2)
                if u in PROJECT_AT:
                    t = PROJECT_AT[u]
                    P = ROWS[t]
                    pe.wait_ge(tp_out, TP_ATT1 + TURNS.index(("att", NEED[t] - 1)) + 1)
                    pe.wait_ge(att1, min(u - 3, AFTER_UNITS))
                    for c in range(2):
                        last = mm(PS[0:P, 6 + u % 2, 0:C], attT1[:, c, OFF[t]:OFF[t] + P], wproj1[:, c, :], start=(c == 0), stop=(c == 1))
                    last.then_inc(y1_ps, 1)

            def hidden_shared(s, first=0, count=HT):
                off, N, _ = CHUNK[s]
                for n in range(HT * s + first, HT * s + first + count):
                    if n >= 2:
                        pe.wait_ge(g_out, n - 1)
                    for q in range(2):
                        for c in range(2):
                            last = mm(PS[:, 2 * (n % 2) + q, 0:N], wsh1[q][:, c, (n % HT) * 128:(n % HT) * 128 + 128],
                                      xnT[:, c, off:off + N], start=(c == 0), stop=(c == 1))
                    last.then_inc(u_ps, 1)

            def out_shared(s):
                pe.wait_ge(g_out, HT * s + HT)
                for t in CHUNK[s][2]:
                    P, o = ROWS[t], OFF[t] - CHUNK[s][0]
                    if t >= 2:
                        pe.wait_ge(ysh_acc, t - 1)
                    for it in range(HT):
                        last = mm(PS[0:P, 4 + t % 2, 0:C], shT[:, s, it, o:o + P], wsh2[:, it, :], start=(it == 0), stop=(it == HT - 1))
                    last.then_inc(ysh_ps, 1)

            pe.wait_ge(ld_sh, 32)
            pe.wait_ge(tp_out, TP_XN3)
            hidden_shared(0, 0, 1)
            pe.wait_ge(h3, NT)
            logits(1, TP_XN3, NORMED)
            hidden_shared(0, 1, 1)
            ranks(1)
            hidden_shared(0, 2, HT - 2)
            hidden_shared(1)
            out_shared(0)
            hidden_shared(2)
            out_shared(1)
            first = first_experts(1)
            out_shared(2)
            pe.wait_ge(ysh_acc, NT)
            slots(1, first)


def arrange(x, x_txt, mask_BS_i2_0, L0_tok_gamma, L0_tok_beta, L0_tok_W, L0_tok_b, L0_txt_token_table, L0_txt_segm_table,
            L0_attn_W_qkv, L0_attn_W_proj, L0_attn_b_proj, L0_attn_gamma, L0_attn_beta, L0_attn_random_features,
            L0_ffn_router_w, L0_ffn_w1, L0_ffn_w2, L1_attn_W_attn, L1_attn_W_proj, L1_ffn_gate_w, L1_ffn_w1, L1_ffn_w2,
            L1_ffn_w3, L1_ffn_ws1, L1_ffn_ws2, L1_ffn_ws3):
    f = np.float32
    a = {}
    n = SIDE // PATCH
    xp = np.zeros((B, CH, SIDE + 2, SIDE + 2), f)
    xp[:, :, 1:-1, 1:-1] = x
    win = np.zeros((HALO, CH, HALO, B, n, n), f)
    for r in range(HALO):
        for q in range(HALO):
            win[r, :, q] = xp[:, :, r:r + PATCH * (n - 1) + 1:PATCH, q:q + PATCH * (n - 1) + 1:PATCH].transpose(1, 0, 2, 3)
    a["xT"] = win.reshape(HALO, CH, 2, NJ, B * n * n).transpose(2, 0, 1, 3, 4).reshape(KP, NJ, B * n * n)

    def by_pixel(w):
        w = np.asarray(w).reshape(PATCH, PATCH, NG, CH, -1)
        o = np.zeros((NG, HALO, CH, HALO, w.shape[-1]), w.dtype)
        for g, (dr, dq) in enumerate(((1, 1), (1, 0), (1, 2), (0, 1), (2, 1))):
            o[g, dr:dr + PATCH, :, dq:dq + PATCH] = w[:, :, g].transpose(0, 2, 1, 3)
        o = o.reshape(NG, HALO, CH, 2, NJ, -1).transpose(3, 1, 2, 0, 4, 5)
        return o.reshape(KP, NG, NJ, -1)
    a["wt"] = by_pixel(L0_tok_W)
    a["gb"] = np.stack([by_pixel(L0_tok_gamma)[..., 0], by_pixel(L0_tok_beta)[..., 0]], 1)
    a["mult"] = by_pixel(np.ones(PDIM, f))[..., 0].sum(1)
    a["tokb"] = L0_tok_b[None, :]
    a["ident"] = np.eye(128, dtype=f)
    p_, i_ = np.arange(NS, dtype=np.float64)[:, None], np.arange(C, dtype=np.float64)[None, :]
    ang = p_ / np.power(10000.0, np.floor(i_ / 2) * 2 / C)
    pos = np.where(np.arange(C) % 2 == 0, np.sin(ang), np.cos(ang)).astype(f)

    def in_tiles(v):
        o = np.zeros((TT * 128,) + v.shape[1:], v.dtype)
        o[:B * NS] = v
        return o.reshape((TT, 128) + v.shape[1:]).swapaxes(0, 1)
    a["pos"] = in_tiles(np.tile(pos, (B, 1)))
    a["ids"] = np.concatenate([in_tiles(v.reshape(-1)) for v in (x_txt, mask_BS_i2_0)], 1)
    a["table"] = L0_txt_token_table
    a["segt"] = L0_txt_segm_table

    def halves(w):
        return np.asarray(w).reshape(2, HC, -1).transpose(1, 0, 2)
    a["wqkv"] = halves(L0_attn_W_qkv)
    bd = np.zeros((HC + 6, 6 * M), f)
    nb = np.zeros((HC, 6), f)
    for h in range(6):
        bd[h * DH:(h + 1) * DH, h * M:(h + 1) * M] = L0_attn_random_features.T
        bd[HC + h, h * M:(h + 1) * M] = 1.0
        nb[h * DH:(h + 1) * DH, h] = -0.5
    a["bd"], a["nb6"] = bd, nb
    a["wproj0"] = halves(L0_attn_W_proj)
    a["rows3"] = np.stack([np.broadcast_to(v, (128, C)) for v in (L0_attn_b_proj, L0_attn_gamma, L0_attn_beta)], 1)
    a["rw"] = np.stack([halves(L0_ffn_router_w.T), halves(L1_ffn_gate_w.T)], 1)
    a["rank"] = np.broadcast_to(np.arange(NE, 0, -1).astype(f), (128, NE))
    wv = np.asarray(L1_attn_W_attn)[:, 2 * C:].reshape(C, NH // 2, 2, DH).transpose(0, 2, 1, 3).reshape(C, C)
    a["wat"] = halves(np.concatenate([np.asarray(L1_attn_W_attn)[:, :2 * C], wv], 1))
    a["wproj1"] = halves(L1_attn_W_proj)
    a["kmask"] = (0.25 * (np.arange(HC)[:, None] // DH == np.arange(6)[None, :])).astype(f)
    ci = np.where(np.arange(64)[None, :] <= (np.arange(128) % 64)[:, None], 0.0, -1e9)
    ct = np.where(np.arange(NS)[None, :] <= np.arange(128)[:, None], 0.0, -1e9)
    a["cmask"] = np.concatenate([ci, ct], 1).astype(f)

    def up(w):
        return halves(w.T).reshape(HC, 2 * HID)

    def down(w):
        return np.asarray(w).T.reshape(HT, 128, C).transpose(1, 0, 2).reshape(128, HT * C)
    a["m0_w1"] = np.stack([up(L0_ffn_w1[e]) for e in range(NE)])
    a["m0_w2"] = np.stack([down(L0_ffn_w2[e]) for e in range(NE)])
    g1 = list(L1_ffn_w1) + [L1_ffn_ws1]
    g3 = list(L1_ffn_w3) + [L1_ffn_ws3]
    g2 = list(L1_ffn_w2) + [L1_ffn_ws2]
    a["m1_w1"] = np.stack([np.concatenate([up(g1[e]), up(g3[e])], 1) for e in range(NE + 1)])
    a["m1_w2"] = np.stack([down(w) for w in g2])
    row = [(np.arange(NE * NT) % NT != 0), np.ones(NE), np.tile(CAP * np.arange(MAXT), NE), np.arange(NSLOT)]
    row = np.broadcast_to(np.concatenate(row).astype(f), (128, NE * NT + NE + NE * MAXT + NSLOT))
    token = 128 + np.arange(128, dtype=f)[:, None] + 128 * np.arange(NT, dtype=f)[None, :]
    a["blank"] = np.concatenate([np.zeros((128, C), f), np.arange(128, dtype=f)[:, None]], 1)
    a["routec"] = np.concatenate([row, token, np.triu(np.ones((128, 128), f), 1)], 1)
    return a


def kernel(**inputs):
    import concourse.bacc as _bacc
    from concourse.bass_utils import run_bass_kernel_spmd as _run

    nc = _bacc.Bacc("TRN2", target_bir_lowering=False, num_devices=1)
    arrays, aps = {}, {}
    for name, v in arrange(**{k: np.asarray(v) for k, v in inputs.items()}).items():
        v = np.ascontiguousarray(v)
        arrays[f"in_{name}"] = v
        aps[name] = nc.dram_tensor(f"in_{name}", v.shape, mybir.dt.from_np(v.dtype), kind="ExternalInput").ap()
    out = nc.dram_tensor("out_h", (NTOK, C), F32, kind="ExternalOutput").ap()
    for name, shape in (("Xs0", (NSLOT * CAP, C + 1)), ("Xs1", (NSLOT * CAP, C + 1)), ("Ys", (NY, C))):
        aps[name] = nc.dram_tensor(name, shape, F32).ap()
    build(nc, aps, out)
    r = _run(nc, [arrays], core_ids=[0])
    got = np.asarray(r.results[0]["out_h"])
    return np.concatenate([got[:B * NP_].reshape(B, NP_, C), got[B * NP_:].reshape(B, NS, C)], 1)
```
